# Optimizing a Trainium2 kernel written in Bass

```python
import numpy as np
import jax
import jax.numpy as jnp

def _softmax(x, axis=-1):
    return jax.nn.softmax(x, axis=axis)

def _gelu(x):
    return jax.nn.gelu(x, approximate=True)

def _silu(x):
    return jax.nn.silu(x)

def _sigmoid(x):
    return jax.nn.sigmoid(x)

def _layernorm(x, axis=-1, eps=1e-05):
    m = jnp.mean(x, axis=axis, keepdims=True)
    v = jnp.var(x, axis=axis, keepdims=True)
    return (x - m) / jnp.sqrt(v + eps)

def _scatter_add(tgt, idx, src, axis=0):
    return tgt.at[idx].add(src)

def _segment_sum(src, seg, n):
    return jax.ops.segment_sum(src, seg, n)
kernel_name = 'mk_sandwich_d1_jaxref_r4_f955a5'

def setup_inputs(seed: int=0):
    np.random.seed(seed)
    _w = jnp.asarray

    def _L0_attn_setup():
        import jax, jax.numpy as jnp
        import numpy as np
        HIDDEN, HEADS, HDIM = (256, 8, 64)
        B, S = (4, 2048)
        LN_EPS = 1e-06
        key = jax.random.key(seed)
        ks = jax.random.split(key, 12)
        inner = HEADS * HDIM
        sd = HIDDEN ** (-0.5)
        return {'x': jax.random.normal(ks[0], (B, S, HIDDEN), jnp.float32), 'Wq': jax.random.normal(ks[1], (HIDDEN, inner), jnp.float32) * sd, 'bq': jnp.zeros((inner,), jnp.float32), 'Wk': jax.random.normal(ks[2], (HIDDEN, inner), jnp.float32) * sd, 'bk': jnp.zeros((inner,), jnp.float32), 'Wv': jax.random.normal(ks[3], (HIDDEN, inner), jnp.float32) * sd, 'bv': jnp.zeros((inner,), jnp.float32), 'Wo': jax.random.normal(ks[4], (inner, HIDDEN), jnp.float32) * inner ** (-0.5), 'bo': jnp.zeros((HIDDEN,), jnp.float32), 'alpha': jnp.ones((HEADS, HDIM), jnp.float32), 'aug_param': jax.random.normal(ks[5], (1, HEADS, HDIM), jnp.float32), 'ln_scale': jnp.ones((HIDDEN,), jnp.float32), 'ln_bias': jnp.zeros((HIDDEN,), jnp.float32)}
    _L0_attn_in = _L0_attn_setup()

    def _L0_ffn_setup():
        import jax, jax.numpy as jnp
        import numpy as np
        B, L, D = (4, 512, 256)
        H = 16
        E = 16
        NS = 16
        S = NS // E
        F = 1024
        EPS = 1e-05

        def _layernorm(x, g, b):
            mu = jnp.mean(x, axis=-1, keepdims=True)
            var = jnp.mean(jnp.square(x - mu), axis=-1, keepdims=True)
            return (x - mu) * jax.lax.rsqrt(var + EPS) * g + b

        def _mha(q, k, v, Wq, bq, Wk, bk, Wv, bv, Wo, bo):
            Bq, Lq, Dm = q.shape
            dh = Dm // H
            qh = (q @ Wq + bq).reshape(Bq, Lq, H, dh)
            kh = (k @ Wk + bk).reshape(Bq, -1, H, dh)
            vh = (v @ Wv + bv).reshape(Bq, -1, H, dh)
            scores = jnp.einsum('bqhd,bkhd->bhqk', qh, kh) / jnp.asarray(np.sqrt(dh), q.dtype)
            attn = jax.nn.softmax(scores, axis=-1)
            out = jnp.einsum('bhqk,bkhd->bqhd', attn, vh).reshape(Bq, Lq, Dm)
            return out @ Wo + bo
        key = jax.random.key(seed)
        ks = jax.random.split(key, 32)
        s = 0.02
        d = {}
        d['x'] = jax.random.normal(ks[0], (B, L, D), jnp.float32)
        d['slot_query'] = jax.random.normal(ks[1], (1, NS, D), jnp.float32) * 0.01
        for i, nm in enumerate(['d_Wq', 'd_Wk', 'd_Wv', 'd_Wo']):
            d[nm] = jax.random.normal(ks[2 + i], (D, D), jnp.float32) * s
        for nm in ['d_bq', 'd_bk', 'd_bv', 'd_bo']:
            d[nm] = jnp.zeros((D,), jnp.float32)
        for i, nm in enumerate(['c_Wq', 'c_Wk', 'c_Wv', 'c_Wo']):
            d[nm] = jax.random.normal(ks[6 + i], (D, D), jnp.float32) * s
        for nm in ['c_bq', 'c_bk', 'c_bv', 'c_bo']:
            d[nm] = jnp.zeros((D,), jnp.float32)
        d['e_ln_g'] = jnp.ones((E, D), jnp.float32)
        d['e_ln_b'] = jnp.zeros((E, D), jnp.float32)
        d['e_W1'] = jax.random.normal(ks[10], (E, D, F), jnp.float32) * s
        d['e_b1'] = jnp.zeros((E, F), jnp.float32)
        d['e_Wg'] = jax.random.normal(ks[11], (E, D, F), jnp.float32) * s
        d['e_bg'] = jnp.zeros((E, F), jnp.float32)
        d['e_W2'] = jax.random.normal(ks[12], (E, F, D), jnp.float32) * s
        d['e_b2'] = jnp.zeros((E, D), jnp.float32)
        return d
    _L0_ffn_in = _L0_ffn_setup()
    _d = {'L0_attn_x': _L0_attn_in['x'], 'L0_attn_Wq': _L0_attn_in['Wq'], 'L0_attn_bq': _L0_attn_in['bq'], 'L0_attn_Wk': _L0_attn_in['Wk'], 'L0_attn_bk': _L0_attn_in['bk'], 'L0_attn_Wv': _L0_attn_in['Wv'], 'L0_attn_bv': _L0_attn_in['bv'], 'L0_attn_Wo': _L0_attn_in['Wo'], 'L0_attn_bo': _L0_attn_in['bo'], 'L0_attn_alpha': _L0_attn_in['alpha'], 'L0_attn_aug_param': _L0_attn_in['aug_param'], 'L0_attn_ln_scale': _L0_attn_in['ln_scale'], 'L0_attn_ln_bias': _L0_attn_in['ln_bias'], 'L0_ffn_slot_query': _L0_ffn_in['slot_query'], 'L0_ffn_d_Wq': _L0_ffn_in['d_Wq'], 'L0_ffn_d_Wk': _L0_ffn_in['d_Wk'], 'L0_ffn_d_Wv': _L0_ffn_in['d_Wv'], 'L0_ffn_d_Wo': _L0_ffn_in['d_Wo'], 'L0_ffn_d_bq': _L0_ffn_in['d_bq'], 'L0_ffn_d_bk': _L0_ffn_in['d_bk'], 'L0_ffn_d_bv': _L0_ffn_in['d_bv'], 'L0_ffn_d_bo': _L0_ffn_in['d_bo'], 'L0_ffn_c_Wq': _L0_ffn_in['c_Wq'], 'L0_ffn_c_Wk': _L0_ffn_in['c_Wk'], 'L0_ffn_c_Wv': _L0_ffn_in['c_Wv'], 'L0_ffn_c_Wo': _L0_ffn_in['c_Wo'], 'L0_ffn_c_bq': _L0_ffn_in['c_bq'], 'L0_ffn_c_bk': _L0_ffn_in['c_bk'], 'L0_ffn_c_bv': _L0_ffn_in['c_bv'], 'L0_ffn_c_bo': _L0_ffn_in['c_bo'], 'L0_ffn_e_ln_g': _L0_ffn_in['e_ln_g'], 'L0_ffn_e_ln_b': _L0_ffn_in['e_ln_b'], 'L0_ffn_e_W1': _L0_ffn_in['e_W1'], 'L0_ffn_e_b1': _L0_ffn_in['e_b1'], 'L0_ffn_e_Wg': _L0_ffn_in['e_Wg'], 'L0_ffn_e_bg': _L0_ffn_in['e_bg'], 'L0_ffn_e_W2': _L0_ffn_in['e_W2'], 'L0_ffn_e_b2': _L0_ffn_in['e_b2']}
    _x0 = _d['L0_attn_x']
    _d['L0_attn_x'] = jax.random.normal(jax.random.fold_in(jax.random.key(seed), 1), (4, 1024, 256), dtype=_x0.dtype)
    del _x0
    return _d

def reference(L0_attn_x, L0_attn_Wq, L0_attn_bq, L0_attn_Wk, L0_attn_bk, L0_attn_Wv, L0_attn_bv, L0_attn_Wo, L0_attn_bo, L0_attn_alpha, L0_attn_aug_param, L0_attn_ln_scale, L0_attn_ln_bias, L0_ffn_slot_query, L0_ffn_d_Wq, L0_ffn_d_Wk, L0_ffn_d_Wv, L0_ffn_d_Wo, L0_ffn_d_bq, L0_ffn_d_bk, L0_ffn_d_bv, L0_ffn_d_bo, L0_ffn_c_Wq, L0_ffn_c_Wk, L0_ffn_c_Wv, L0_ffn_c_Wo, L0_ffn_c_bq, L0_ffn_c_bk, L0_ffn_c_bv, L0_ffn_c_bo, L0_ffn_e_ln_g, L0_ffn_e_ln_b, L0_ffn_e_W1, L0_ffn_e_b1, L0_ffn_e_Wg, L0_ffn_e_bg, L0_ffn_e_W2, L0_ffn_e_b2):

    def _L0_attn_ref(x, Wq, bq, Wk, bk, Wv, bv, Wo, bo, alpha, aug_param, ln_scale, ln_bias):
        import jax, jax.numpy as jnp
        import numpy as np
        HIDDEN, HEADS, HDIM = (256, 8, 64)
        B, S = (4, 2048)
        LN_EPS = 1e-06
        b, s, _ = x.shape
        h, d = alpha.shape
        scale = d ** (-0.5)
        q = (x @ Wq + bq).reshape(b, s, h, d)
        k = (x @ Wk + bk).reshape(b, s, h, d)
        v = (x @ Wv + bv).reshape(b, s, h, d)
        decay = jax.nn.sigmoid(alpha)

        def step(state, qkv):
            q_t, k_t, v_t = qkv
            attn = jax.nn.softmax(jnp.einsum('bhd,bhd->bh', q_t, k_t) * scale, axis=-1)
            new_state = decay * state + (1.0 - decay) * attn[..., None] * v_t
            return (new_state, new_state)
        qs = jnp.moveaxis(q, 1, 0)
        ks_ = jnp.moveaxis(k, 1, 0)
        vs = jnp.moveaxis(v, 1, 0)
        init = jnp.zeros((b, h, d), x.dtype)
        _, states = jax.lax.scan(step, init, (qs, ks_, vs))
        states = jnp.moveaxis(states, 0, 1)
        aug = jax.nn.sigmoid(q * aug_param)
        out = (q * states + aug).reshape(b, s, h * d)
        out = out @ Wo + bo
        mean = jnp.mean(out, axis=-1, keepdims=True)
        var = jnp.var(out, axis=-1, keepdims=True)
        return (out - mean) * jax.lax.rsqrt(var + LN_EPS) * ln_scale + ln_bias

    def _L0_ffn_ref(x, slot_query, d_Wq, d_Wk, d_Wv, d_Wo, d_bq, d_bk, d_bv, d_bo, c_Wq, c_Wk, c_Wv, c_Wo, c_bq, c_bk, c_bv, c_bo, e_ln_g, e_ln_b, e_W1, e_b1, e_Wg, e_bg, e_W2, e_b2):
        import jax, jax.numpy as jnp
        import numpy as np
        B, L, D = (4, 512, 256)
        H = 16
        E = 16
        NS = 16
        S = NS // E
        F = 1024
        EPS = 1e-05

        def _layernorm(x, g, b):
            mu = jnp.mean(x, axis=-1, keepdims=True)
            var = jnp.mean(jnp.square(x - mu), axis=-1, keepdims=True)
            return (x - mu) * jax.lax.rsqrt(var + EPS) * g + b

        def _mha(q, k, v, Wq, bq, Wk, bk, Wv, bv, Wo, bo):
            Bq, Lq, Dm = q.shape
            dh = Dm // H
            qh = (q @ Wq + bq).reshape(Bq, Lq, H, dh)
            kh = (k @ Wk + bk).reshape(Bq, -1, H, dh)
            vh = (v @ Wv + bv).reshape(Bq, -1, H, dh)
            scores = jnp.einsum('bqhd,bkhd->bhqk', qh, kh) / jnp.asarray(np.sqrt(dh), q.dtype)
            attn = jax.nn.softmax(scores, axis=-1)
            out = jnp.einsum('bhqk,bkhd->bqhd', attn, vh).reshape(Bq, Lq, Dm)
            return out @ Wo + bo
        Bx = x.shape[0]
        q = jnp.broadcast_to(slot_query, (Bx, NS, D))
        o = q + _mha(q, x, x, d_Wq, d_bq, d_Wk, d_bk, d_Wv, d_bv, d_Wo, d_bo)
        os = o.reshape(Bx, E, S, D)
        h = _layernorm(os, e_ln_g[None, :, None, :], e_ln_b[None, :, None, :])
        u = jax.nn.silu(jnp.einsum('besd,edf->besf', h, e_W1) + e_b1[None, :, None, :])
        g = jax.nn.silu(jnp.einsum('besd,edf->besf', h, e_Wg) + e_bg[None, :, None, :])
        y = jnp.einsum('besf,efd->besd', u * g, e_W2) + e_b2[None, :, None, :]
        o = o + y.reshape(Bx, NS, D)
        out = _mha(x, o, o, c_Wq, c_bq, c_Wk, c_bk, c_Wv, c_bv, c_Wo, c_bo)
        return out
    x = L0_attn_x
    x = x + _layernorm(_L0_attn_ref(_layernorm(x, axis=-1), L0_attn_Wq, L0_attn_bq, L0_attn_Wk, L0_attn_bk, L0_attn_Wv, L0_attn_bv, L0_attn_Wo, L0_attn_bo, L0_attn_alpha, L0_attn_aug_param, L0_attn_ln_scale, L0_attn_ln_bias), axis=-1)
    x = x + _layernorm(_L0_ffn_ref(_layernorm(x, axis=-1), L0_ffn_slot_query, L0_ffn_d_Wq, L0_ffn_d_Wk, L0_ffn_d_Wv, L0_ffn_d_Wo, L0_ffn_d_bq, L0_ffn_d_bk, L0_ffn_d_bv, L0_ffn_d_bo, L0_ffn_c_Wq, L0_ffn_c_Wk, L0_ffn_c_Wv, L0_ffn_c_Wo, L0_ffn_c_bq, L0_ffn_c_bk, L0_ffn_c_bv, L0_ffn_c_bo, L0_ffn_e_ln_g, L0_ffn_e_ln_b, L0_ffn_e_W1, L0_ffn_e_b1, L0_ffn_e_Wg, L0_ffn_e_bg, L0_ffn_e_W2, L0_ffn_e_b2), axis=-1)
    return x

_drawn_inputs = setup_inputs


def setup_inputs(seed=0):
    import zlib

    import numpy as np

    out = dict(_drawn_inputs(seed))
    spreads = {'L0_attn_bq': (0.0, 0.386),
     'L0_attn_bk': (0.0, 0.8),
     'L0_attn_bv': (0.0, 0.647),
     'L0_attn_bo': (0.0, 0.1),
     'L0_attn_alpha': (1.0, 0.6),
     'L0_attn_ln_scale': (1.0, 0.2),
     'L0_attn_ln_bias': (0.0, 0.1),
     'L0_ffn_d_bq': (0.0, 0.8),
     'L0_ffn_d_bk': (0.0, 2.0),
     'L0_ffn_d_bv': (0.0, 0.371),
     'L0_ffn_d_bo': (0.0, 0.1),
     'L0_ffn_c_bq': (0.0, 0.8),
     'L0_ffn_c_bk': (0.0, 2.0),
     'L0_ffn_c_bv': (0.0, 2.0),
     'L0_ffn_c_bo': (0.0, 0.7),
     'L0_ffn_e_ln_g': (1.0, 0.6),
     'L0_ffn_e_ln_b': (0.0, 0.8),
     'L0_ffn_e_b1': (0.0, 0.8),
     'L0_ffn_e_bg': (0.0, 0.8),
     'L0_ffn_e_b2': (0.0, 0.626)}
    factors = {'L0_ffn_slot_query': 8.0,
     'L0_ffn_d_Wq': 8.0,
     'L0_ffn_d_Wk': 8.0,
     'L0_ffn_c_Wq': 8.0,
     'L0_ffn_c_Wk': 8.0,
     'L0_ffn_e_W1': 8.0,
     'L0_ffn_e_Wg': 8.0,
     'L0_ffn_e_W2': 8.0}
    for name, (base, spread) in spreads.items():
        noise = np.random.default_rng([zlib.crc32(name.encode()), seed]).standard_normal(out[name].shape)
        drawn = base * np.exp(spread * noise) if base else spread * noise
        out[name] = jnp.asarray(drawn.astype(out[name].dtype))
    for name, factor in factors.items():
        out[name] = (out[name] * factor).astype(out[name].dtype)
    return out
```

```python
import concourse.bass as bass
from concourse import mybir
from contextlib import ExitStack

F32 = mybir.dt.float32
F32R = mybir.dt.float32r
ALU = mybir.AluOpType
ACT = mybir.ActivationFunctionType
X = mybir.AxisListType.X

P = 128
B, S, D = 4, 1024, 256
KC = D // P
INNER, HEADS = 512, 8
CH = INNER // P
T = 512
TJ = T // P
HALVES = S // T
NS, MH = 16, 16
HQ = MH * NS
HM = HQ // P
F = 1024
FC = F // P
GROUP = 4
PIECES = 6
RING = 3
DVE_OWN = 38
POOL_OWN = 34
EPS, EPS_OUT = 1e-5, 1e-6
RECUR_SCALE = (INNER // HEADS) ** -0.5
SCORE_SCALE = (D // MH) ** -0.5


def part(k):
    return (0, 1, 1, 0, 0, 1)[k]


class Count:

    def __init__(self, sem):
        self.sem, self.base, self.step, self.turn, self.per = sem, 0, 0, None, 0

    def enter(self, turn, per):
        self.base, self.step, self.turn, self.per = self.base + self.step, 0, turn, per

    def leave(self, turns):
        assert self.step == self.per, (self.sem, self.step, self.per)
        self.base, self.step, self.turn = self.base + self.per * turns, 0, None

    def now(self):
        return self.base + self.step + (0 if self.turn is None else self.turn * self.per)


class Unit:

    def __init__(self, b, h):
        self.b, self.h, self.n = b, h, b * HALVES + h

    def next(self):
        return Unit(self.b, 1) if self.h == 0 else Unit(self.b + 1, 0)

    def prev(self):
        return Unit(self.b, 0) if self.h == 1 else Unit(self.b - 1, 1)


def build(nc, a, out):
    ctx = ExitStack()
    with ctx:
        def sb(name, shape, dt=F32):
            return ctx.enter_context(nc.sbuf_tensor(name, shape, dt))

        def sem(name):
            return ctx.enter_context(nc.semaphore(name))

        x1_dram = nc.dram_tensor("x1_scratch", (B, HALVES, P, TJ, D), F32).ap()
        qh_dram = nc.dram_tensor("qh_scratch", (B, P, HM, S), F32).ap()

        ident = sb("ident", [P, P])
        mask8 = sb("mask8", [P, 8])
        pair = sb("pair", [P, 2])
        sel = sb("sel", [40, CH, P], F32R)
        minus_half = sb("minus_half", [P, 8])
        per_d = sb("per_d", [P, 8])
        minus_one = sb("minus_one", [P, 8])
        eps_c = sb("eps_c", [P, 2, 8])
        VECTORS = (("bq_c", "L0_attn_bq", CH), ("bk_c", "L0_attn_bk", CH), ("bv_c", "L0_attn_bv", CH),
                   ("alpha_c", "L0_attn_alpha", CH), ("aug_c", "L0_attn_aug_param", CH),
                   ("dbq_c", "L0_ffn_d_bq", HM), ("dbk_c", "L0_ffn_d_bk", HM), ("cbq_c", "L0_ffn_c_bq", HM),
                   ("cbk_c", "L0_ffn_c_bk", HM), ("cbv_c", "L0_ffn_c_bv", HM), ("b2_c", "L0_ffn_e_b2", NS * KC))
        VROWS = sum(n for _, _, n in VECTORS)
        vec = sb("vec", [P, VROWS])
        col, at_row = {}, {}
        for short, name, n in VECTORS:
            at_row[name] = sum(at_row[m][1] for m in at_row), n
            col[short] = vec[:, at_row[name][0]:at_row[name][0] + n]
        bq_c, bk_c, bv_c, alpha_c, aug_c = (col[n] for n in ("bq_c", "bk_c", "bv_c", "alpha_c", "aug_c"))
        dbq_c, dbk_c, cbq_c, cbk_c, cbv_c = (col[n] for n in ("dbq_c", "dbk_c", "cbq_c", "cbk_c", "cbv_c"))
        b2t = col["b2_c"].rearrange("p (e k) -> p k e", k=KC)
        decay = sb("decay", [P, CH])
        keep2 = sb("keep2", [P, CH])
        bv2 = sb("bv2", [P, CH])
        aug_half = sb("aug_half", [P, CH])
        bo_r = sb("bo_r", [P, D])
        lns_r = sb("lns_r", [P, D])
        lnb_r = sb("lnb_r", [P, D])
        cbo_r = sb("cbo_r", [P, D])
        w_hi = sb("w_hi", [P, KC, 3, INNER], F32R)
        w_lo = sb("w_lo", [P, KC, 3, INNER], F32R)
        wo = sb("wo", [P, CH, D])
        m_hi = sb("m_hi", [P, KC, HQ], F32R)
        m_lo = sb("m_lo", [P, KC, HQ], F32R)
        m_bias = sb("m_bias", [P, HM])
        cq_hi = sb("cq_hi", [P, KC, D], F32R)
        cq_lo = sb("cq_lo", [P, KC, D], F32R)
        x = sb("x", [P, 2, TJ, D])
        xn = sb("xn", [P, TJ, D])
        x_hi = sb("x_hi", [P, KC, T], F32R)
        x_lo = sb("x_lo", [P, KC, T], F32R)
        q = sb("q", [P, 2, CH, T])
        v = sb("v", [P, 2, CH, T])
        qk = sb("qk", [P, 2, T])
        th = sb("th", [P, 2, T])
        st = sb("st", [P, 2, T])
        carry = sb("carry", [P, CH])
        o = sb("o", [P, TJ, D])
        x1 = sb("x1", [P, TJ, D])
        xn2 = sb("xn2", [P, HALVES * TJ, D])
        x2_hi = sb("x2_hi", [P, KC, T], F32R)
        x2_lo = sb("x2_lo", [P, KC, T], F32R)
        sc = sb("sc", [P, HM, S])
        pt = sb("pt", [P, 2, 2, HQ])
        qh = sb("qh", [P, HM, T])
        zt = sb("zt", [P, KC, MH, B, NS])
        stats = sb("stats", [P, TJ, 6])
        both = sb("both", [P, TJ, 2])
        apart = sb("apart", [P, TJ])
        mv1 = sb("mv1", [P, TJ, 2])
        mv2 = sb("mv2", [P, TJ, 2])
        mv3 = sb("mv3", [P, TJ, 2])
        mv4 = sb("mv4", [P, TJ, 2])
        r1 = sb("r1", [P, 3, TJ])
        r2 = sb("r2", [P, 3, TJ])
        r3 = sb("r3", [P, 3, TJ])
        r4 = sb("r4", [P, 3, TJ])
        smx = sb("smx", [P, TJ])
        sums = sb("sums", [P, TJ])
        rsum = sb("rsum", [P, TJ])
        att = sb("att", [P, TJ, HEADS])
        att_parts = sb("att_parts", [40, T], F32R)
        cmx = sb("cmx", [P, HM])
        cneg = sb("cneg", [P, HM])
        csum = sb("csum", [P, HM])
        crec = sb("crec", [P, HM])
        ring = sb("ring", [P, RING, GROUP, 1024])
        w_raw = ring[:, 0, :, :].rearrange("p j n -> p (j n)")[:, 0:KC * 3 * INNER].rearrange("p (k w n) -> p k w n", k=KC, w=3)
        stage1 = ring[:, 1, :, :].rearrange("p j n -> p (j n)")
        dwq = stage1[:, 0:512].rearrange("p (k n) -> p k n", k=KC)
        dwk = stage1[:, 512:1024].rearrange("p (k n) -> p k n", k=KC)
        cwq = stage1[:, 1024:1536].rearrange("p (k n) -> p k n", k=KC)
        wkt = stage1[:, 1536:2048].rearrange("p (m n) -> p m n", m=HM)
        qbd = stage1[:, 2048:2304].rearrange("p (m n) -> p m n", m=HM)
        slot_in = stage1[0:NS, 2304:2560]
        vec_rows = stage1[0:VROWS, 3584:3584 + P]
        sel_raw = stage1[0:40, 3072:3584].rearrange("r (c a n) -> r c a n", c=CH, a=2)
        sqt = stage1[:, 2560:2592].rearrange("p (k n) -> p k n", k=KC)
        qht = stage1[:, 2592:2624].rearrange("p (m n) -> p m n", m=HM)

        late = q[:].rearrange("p a c t -> p (a c t)")
        d_wv = late[:, 0:512].rearrange("p (k n) -> p k n", k=KC)
        d_wo = late[:, 512:1024].rearrange("p (k n) -> p k n", k=KC)
        c_wk = late[:, 1024:1536].rearrange("p (k n) -> p k n", k=KC)
        c_wv = late[:, 1536:2048].rearrange("p (k n) -> p k n", k=KC)
        c_wo = late[:, 2048:2560].rearrange("p (k n) -> p k n", k=KC)
        dbv_r = late[0:64, 2560:2816]
        dbo_r = late[0:64, 2816:3072]
        slot_r = late[0:64, 3072:3328]
        eg_r = late[0:64, 3328:3584]
        eb_r = late[0:64, 3584:3840]
        late2 = v[:].rearrange("p a c t -> p (a c t)")
        b1t = late2[:, 0:256].rearrange("p (w e c) -> p w e c", w=2, e=NS)
        vo = late2[0:64, 256:512]
        vot = late2[:, 512:640].rearrange("p (k n) -> p k n", k=KC)
        os_ = late2[0:64, 640:896]
        hs = late2[0:64, 896:1152]
        ht = late2[:, 1152:1280].rearrange("p (k b e) -> p k b e", k=KC, b=B)
        o2t = late2[:, 1280:1408].rearrange("p (k b e) -> p k b e", k=KC, b=B)
        hcur = late2[:, 1408:1664].rearrange("p (k j n) -> p k j n", k=KC, j=GROUP)
        at = late2[:, 1664:2688].rearrange("p (c j n) -> p c j n", c=FC, j=GROUP)
        ug = late2[:, 2688:2944].rearrange("p (w c j b) -> p w c j b", w=2, c=FC, j=GROUP)
        eug = late2[:, 2944:3200].rearrange("p (w c j b) -> p w c j b", w=2, c=FC, j=GROUP)
        ysb = late2[:, 3200:3456]
        kv_t = late2[:, 3456:3712].rearrange("p (w m b s) -> p w m b s", w=2, m=HM, b=B)
        u_sb = sc[:].rearrange("p m s -> p (m s)")[:, 0:F]
        g_sb = sc[:].rearrange("p m s -> p (m s)")[:, F:2 * F]
        xn2_flat = xn2[:].rearrange("p j d -> p (j d)")
        kb = xn2_flat[:, 0:1024].rearrange("p (m b n) -> p m b n", m=HM, b=B)
        vb = xn2_flat[:, 1024:2048].rearrange("p (m b n) -> p m b n", m=HM, b=B)
        vp = x[:].rearrange("p a j d -> p (a j d)").rearrange("p (m b n) -> p m b n", m=HM, b=B)
        qh_in = late.rearrange("p (a m s) -> p a m s", a=2, m=HM)
        x1_in = late2.rearrange("p (a j d) -> p a j d", a=2, d=D)
        prob = [sc[:].rearrange("p m s -> p (m s)")[:, i * 512:(i + 1) * 512] for i in range(4)]
        ptl = [pt[:].rearrange("p a t n -> p (a t n)")[:, i * 512:(i + 1) * 512] for i in range(2)]
        y = [o[:].rearrange("p j d -> p (j d)")[:, i * 512:(i + 1) * 512] for i in range(2)]
        res = [x1[:].rearrange("p j d -> p (j d)")[:, i * 512:(i + 1) * 512] for i in range(2)]
        tmx = sb("tmx", [P, 2, 32])
        tsum = sb("tsum", [P, 2, 32])
        trec = sb("trec", [P, 2, 32])
        mv5 = sb("mv5", [P, 2, 2, 2])
        st5 = sb("st5", [P, 2, 2, 6])
        r5 = sb("r5", [P, 2, 3, 2])

        bank = [ctx.enter_context(nc.psum_tensor(f"bank{i}", [P, 512], F32)) for i in range(8)]

        x_in = [sem("x_in0"), sem("x_in1")]
        vec_in, vec_turned, vec_made = sem("vec_in"), sem("vec_turned"), sem("vec_made")
        w_in, small_in, fold_in, late_in = sem("w_in"), sem("small_in"), sem("fold_in"), sem("late_in")
        x1_out, qh_out, res_out = sem("x1_out"), sem("qh_out"), [sem("res_out0"), sem("res_out1")]
        piece_in = [sem(f"piece_in{i}") for i in range(RING)]
        qh_back = [sem("qh_back0"), sem("qh_back1")]
        x1_back = [sem("x1_back0"), sem("x1_back1")]
        consts_made, sel_split, tanh_alpha, rates_made = sem("consts_made"), sem("sel_split"), sem("tanh_alpha"), sem("rates_made")
        w_hi_made, w_lo_made = sem("w_hi_made"), sem("w_lo_made")
        fold_pe, fold_dve, m_hi_made, m_lo_made = sem("fold_pe"), sem("fold_dve"), sem("m_hi_made"), sem("m_lo_made")
        ln1_stats, ln1_rate, xn_made = sem("ln1_stats"), sem("ln1_rate"), sem("xn_made")
        t1_done, x_hi_made, x_lo_made = sem("t1_done"), sem("x_hi_made"), sem("x_lo_made")
        q_done, k_done, v_done = sem("q_done"), sem("k_done"), sem("v_done")
        q_made, qk_made, v_made = sem("q_made"), sem("qk_made"), sem("v_made")
        sum_done, cen_made, exp_made, att_made = sem("sum_done"), sem("cen_made"), sem("exp_made"), sem("att_made")
        att_t_done, att_hi_made, att_lo_made, spread_done = sem("att_t_done"), sem("att_hi_made"), sem("att_lo_made"), sem("spread_done")
        th_made, scan_made, qst_made, inner_made = sem("th_made"), sem("scan_made"), sem("qst_made"), sem("inner_made")
        wo_done, ln2_stats, ln2_rate, ln2_made = sem("wo_done"), sem("ln2_stats"), sem("ln2_rate"), sem("ln2_made")
        gain_made, ln3_stats, ln3_rate, ln3_made = sem("gain_made"), sem("ln3_stats"), sem("ln3_rate"), sem("ln3_made")
        x1_made, ln4_stats, ln4_rate, xn2_made = sem("x1_made"), sem("ln4_stats"), sem("ln4_rate"), sem("xn2_made")
        t2_done, x2_hi_made, x2_lo_made = sem("t2_done"), sem("x2_hi_made"), sem("x2_lo_made")
        s_done, qp_done, s_made, qh_made = sem("s_done"), sem("qp_done"), sem("s_made"), sem("qh_made")
        smax_made, p_made, pn_made = sem("smax_made"), sem("p_made"), sem("pn_made")
        pt_done, pt_made, z_pair, zt_made = sem("pt_done"), sem("pt_made"), sem("z_pair"), sem("zt_made")
        o_made, val_made = sem("o_made"), sem("val_made")
        c_pe, c_dve, c_pool = sem("c_pe"), sem("c_dve"), sem("c_pool")
        pads_made, hcur_made, piece_used = sem("pads_made"), sem("hcur_made"), sem("piece_used")
        u_out, g_out = sem("u_out"), sem("g_out")
        ut_done, ug_made, eug_made, at_made = sem("ut_done"), sem("ug_made"), sem("eug_made"), sem("at_made")
        y_out, yt_done, slots_made = sem("y_out"), sem("yt_done"), sem("slots_made")
        kv_done, kv_made, vp_done, vp_made = sem("kv_done"), sem("kv_made"), sem("vp_done"), sem("vp_made")
        f_s_done, f_cen, f_exp, f_rec, f_norm = sem("f_s_done"), sem("f_cen"), sem("f_exp"), sem("f_rec"), sem("f_norm")
        f_t_done, f_pt, f_y_done, f_y_made, f_stats, f_rate, f_res = (
            sem("f_t_done"), sem("f_pt"), sem("f_y_done"), sem("f_y_made"), sem("f_stats"), sem("f_rate"), sem("f_res"))
        dve_own, pool_own = sem("dve_own"), sem("pool_own")

        x_dram = a["L0_attn_x"].rearrange("b (h j p) d -> b h p j d", h=HALVES, j=TJ)
        out_dram = out.rearrange("b (n j p) d -> b n p j d", j=2, p=P)

        def chunks(w):
            return w.rearrange("(k p) n -> p k n", p=P)

        def row(vec, n=P):
            return vec.rearrange("(o n) -> o n", o=1).to_broadcast([n, D])

        SMALL_LOADS = 4
        FOLD_LOADS = 5
        LATE_LOADS = 5 + 2 + B * 3 + 2

        block = ctx.enter_context(nc.Block())

        @block.sync
        def _(sp):
            for _, name, n in VECTORS:
                vector = a[name]
                if len(vector.shape) == 2:
                    vector = vector.rearrange("h d -> (h d)")
                elif len(vector.shape) == 3:
                    vector = vector.rearrange("o h d -> (o h d)")
                first = at_row[name][0]
                sp.dma_start(vec_rows[first:first + n, :], vector.rearrange("(c p) -> c p", p=P)).then_inc(vec_in, 16)
            sp.dma_start(w_raw[:, :, 0, :], chunks(a["L0_attn_Wq"])).then_inc(w_in, 16)
            sp.dma_start(w_raw[:, :, 1, :], chunks(a["L0_attn_Wk"])).then_inc(w_in, 16)
            sp.dma_start(w_raw[:, :, 2, :], chunks(a["L0_attn_Wv"])).then_inc(w_in, 16)
            for h in range(HALVES):
                sp.dma_start(x[:, h], x_dram[0, h]).then_inc(x_in[h], 16)
            sp.dma_start(dwq, chunks(a["L0_ffn_d_Wq"])).then_inc(fold_in, 16)
            sp.dma_start(dwk, chunks(a["L0_ffn_d_Wk"])).then_inc(fold_in, 16)
            sp.dma_start(cwq, chunks(a["L0_ffn_c_Wq"])).then_inc(fold_in, 16)
            sp.dma_start(slot_in, a["L0_ffn_slot_query"].rearrange("o s d -> (o s) d")).then_inc(fold_in, 16)
            sp.dma_start(wo[:], chunks(a["L0_attn_Wo"])).then_inc(fold_in, 16)
            sp.dma_start(bo_r[:], row(a["L0_attn_bo"])).then_inc(small_in, 16)
            sp.dma_start(lns_r[:], row(a["L0_attn_ln_scale"])).then_inc(small_in, 16)
            sp.dma_start(lnb_r[:], row(a["L0_attn_ln_bias"])).then_inc(small_in, 16)
            sp.dma_start(cbo_r[:], row(a["L0_ffn_c_bo"])).then_inc(small_in, 16)

            def piece(g, k):
                w = a[("L0_ffn_e_W1", "L0_ffn_e_Wg", "L0_ffn_e_W2")[k // 2]]
                src = w.rearrange("(g j) (p r) n -> g p j (r n)", j=GROUP, p=P)[g]
                sp.dma_start(ring[:, k % RING], src[:, :, part(k) * 1024:(part(k) + 1) * 1024]) \
                    .then_inc(piece_in[k % RING], 16)

            sp.wait_ge(w_lo_made, KC + 1)
            sp.wait_ge(m_lo_made, 1)
            sp.wait_ge(sel_split, 1)
            for k in range(RING):
                piece(0, k)

            def stage(b, last):
                for h in range(HALVES):
                    u = Unit(b, h)
                    if not (isinstance(b, int) and u.n == 0):
                        p = u.prev()
                        sp.wait_ge(qh_made, HM * (p.n + 1))
                        sp.dma_start(qh_dram[p.b, :, :, p.h * T:(p.h + 1) * T], qh[:]).then_inc(qh_out, 16)
                    sp.wait_ge(x1_made, u.n + 1)
                    sp.dma_start(x1_dram[b, h], x1[:]).then_inc(x1_out, 16)
                    if not last:
                        sp.dma_start(x[:, h], x_dram[b + 1, h]).then_inc(x_in[h], 16)

            stage(0, False)
            with sp.Fori(1, B - 1) as b:
                stage(b, False)
            stage(B - 1, True)
            sp.wait_ge(qh_made, HM * HALVES * B)
            sp.dma_start(qh_dram[B - 1, :, :, T:], qh[:]).then_inc(qh_out, 16)

            sp.wait_ge(inner_made, CH * HALVES * B)
            for dst, name in ((d_wv, "d_Wv"), (d_wo, "d_Wo"), (c_wk, "c_Wk"), (c_wv, "c_Wv"), (c_wo, "c_Wo")):
                sp.dma_start(dst, chunks(a["L0_ffn_" + name])).then_inc(late_in, 16)
            sp.dma_start(dbv_r, row(a["L0_ffn_d_bv"], 64)).then_inc(late_in, 16)
            sp.dma_start(dbo_r, row(a["L0_ffn_d_bo"], 64)).then_inc(late_in, 16)
            for b in range(B):
                rows = slice(b * NS, (b + 1) * NS)
                sp.dma_start(slot_r[rows, :], a["L0_ffn_slot_query"].rearrange("o s d -> (o s) d")).then_inc(late_in, 16)
                sp.dma_start(eg_r[rows, :], a["L0_ffn_e_ln_g"]).then_inc(late_in, 16)
                sp.dma_start(eb_r[rows, :], a["L0_ffn_e_ln_b"]).then_inc(late_in, 16)
            sp.wait_ge(wo_done, 2 * HALVES * B)
            sp.dma_start(b1t[:, 0], a["L0_ffn_e_b1"].rearrange("e (p c) -> p e c", p=P)).then_inc(late_in, 16)
            sp.dma_start(b1t[:, 1], a["L0_ffn_e_bg"].rearrange("e (p c) -> p e c", p=P)).then_inc(late_in, 16)

            def refill(g, k):
                sp.wait_ge(piece_used, PIECES * g + k + 1)
                piece(g if k < RING else g + 1, (k + RING) % PIECES)

            with sp.Fori(1, NS // GROUP) as after:
                for k in range(PIECES):
                    refill(after - 1, k)
            for k in range(RING):
                refill(NS // GROUP - 1, k)

            sp.wait_ge(qh_out, 16 * HALVES * B)
            sp.wait_ge(x1_out, 16 * HALVES * B)
            sp.wait_ge(vp_done, 1)

            def back(b, par):
                sp.dma_start(qh_in[:, par], qh_dram[b]).then_inc(qh_back[par], 16)
                for h in range(HALVES):
                    sp.dma_start(x1_in[:, par, h * TJ:(h + 1) * TJ], x1_dram[b, h]).then_inc(x1_back[par], 16)

            back(0, 0)
            back(1, 1)
            for t in range(B // 2):
                for i in range(8):
                    sp.wait_ge(f_res, 8 * t + i + 1)
                    sp.dma_start(out_dram[2 * t + i // 4, i % 4], res[i % 2].rearrange("p (j d) -> p j d", j=2)) \
                        .then_inc(res_out[i % 2], 16)
                    if i % 4 == 3 and t + 1 < B // 2:
                        back(2 * (t + 1) + i // 4, i // 4)
            for s in range(2):
                sp.wait_ge(res_out[s], 16 * 8)

        @block.gpsimd
        def _(pool):
            own = Count(pool_own)

            def link(ins):
                own.step += 1
                ins.then_inc(pool_own, 1)
                pool.wait_ge(pool_own, own.now())

            nc.gpsimd.memset(minus_half[:], -0.5)
            nc.gpsimd.memset(minus_one[:], -1.0)
            nc.gpsimd.memset(per_d[:], 1.0 / D)
            nc.gpsimd.memset(eps_c[:, 0], EPS * D)
            nc.gpsimd.memset(eps_c[:, 1], EPS_OUT * D)
            nc.gpsimd.memset(mask8[:], 1.0)
            nc.gpsimd.memset(pair[:], 1.0)
            nc.gpsimd.memset(sel_raw, 0.0)
            link(nc.gpsimd.memset(ident[:], 0.0))
            nc.gpsimd.affine_select(out=ident[:], in_=ident[:], compare_op=ALU.not_equal, fill=1.0, base=0,
                                    pattern=[[-1, P]], channel_multiplier=1)
            for t, width, n in ((mask8, NS, 8), (pair, 64, 2)):
                link(nc.gpsimd.affine_select(out=t[:], in_=t[:], compare_op=ALU.is_ge, fill=0.0, base=0,
                                             pattern=[[-width, n]], channel_multiplier=1))
                link(nc.gpsimd.affine_select(out=t[:], in_=t[:], compare_op=ALU.is_ge, fill=0.0, base=width - 1,
                                             pattern=[[width, n]], channel_multiplier=-1))
            link(nc.gpsimd.affine_select(out=sel_raw, in_=sel_raw, compare_op=ALU.not_equal, fill=1.0, base=0,
                                         pattern=[[-2, CH], [-1, 2], [0, 64]], channel_multiplier=1))
            nc.gpsimd.affine_select(out=sel_raw, in_=sel_raw, compare_op=ALU.not_equal, fill=1.0, base=-32,
                                    pattern=[[-2, CH], [-1, 2], [0, 64]], channel_multiplier=1).then_inc(consts_made, 1)

            def rate(mv, r, eps, n, ready, at, done):
                pool.wait_ge(ready, at)
                link(nc.gpsimd.tensor_tensor(r[:, 0, 0:n], mv[:, :, 1], eps_c[:, eps, 0:n], ALU.add))
                link(nc.gpsimd.tensor_tensor(r[:, 0, 0:n], r[:, 0, 0:n], per_d[:, 0:n], ALU.mult))
                link(nc.gpsimd.tensor_tensor(r[:, 1, 0:n], r[:, 0, 0:n], minus_half[:, 0:n], ALU.pow))
                link(nc.gpsimd.tensor_tensor(r[:, 2, 0:n], mv[:, :, 0], r[:, 1, 0:n], ALU.mult))
                nc.gpsimd.tensor_tensor(r[:, 2, 0:n], r[:, 2, 0:n], minus_one[:, 0:n], ALU.mult).then_inc(done, 1)

            def norm_rates(u, last):
                rate(mv2, r2, 1, TJ, ln2_stats, u.n + 1, ln2_rate)
                pool.wait_ge(ln2_made, u.n + 1)
                gain = lns_r[:].unsqueeze(1).to_broadcast([P, TJ, D])
                shift = lnb_r[:].unsqueeze(1).to_broadcast([P, TJ, D])
                link(nc.gpsimd.tensor_tensor(o[:], o[:], gain, ALU.mult))
                nc.gpsimd.tensor_tensor(o[:], o[:], shift, ALU.add).then_inc(gain_made, 1)
                rate(mv3, r3, 0, TJ, ln3_stats, u.n + 1, ln3_rate)
                rate(mv4, r4, 0, TJ, ln4_stats, u.n + 1, ln4_rate)

            pool.wait_ge(small_in, 16 * SMALL_LOADS)

            def stage(b, first, last):
                for h in range(HALVES):
                    u = Unit(b, h)
                    for c in range(CH):
                        pool.wait_ge(scan_made, CH * u.n + c + 1)
                        nc.gpsimd.tensor_tensor(v[:, h, c], q[:, h, c], st[:, c % 2], ALU.mult).then_inc(qst_made, 1)
                    norm_rates(u, last)
                    if not last:
                        w = Unit(b + 1, h)
                        pool.wait_ge(xn_made, w.n)
                        rate(mv1, r1, 0, TJ, ln1_stats, w.n + 1, ln1_rate)

            rate(mv1, r1, 0, TJ, ln1_stats, 1, ln1_rate)
            pool.wait_ge(xn_made, 1)
            rate(mv1, r1, 0, TJ, ln1_stats, 2, ln1_rate)
            stage(0, True, False)
            with pool.Fori(1, B - 1) as b:
                own.enter(b - 1, POOL_OWN)
                stage(b, False, False)
                own.leave(B - 2)
            stage(B - 1, False, True)

            pool.wait_ge(wo_done, 2 * HALVES * B)
            nc.gpsimd.memset(hcur, 0.0)
            nc.gpsimd.memset(at, 0.0).then_inc(pads_made, 1)
            pool.wait_ge(c_dve, 3)
            link(nc.gpsimd.tensor_scalar(r5[0:64, 0, 0, 0:1], mv5[0:64, 0, 0, 1:2], EPS, None, ALU.add))
            nc.gpsimd.tensor_tensor(r5[0:64, 0, 1, 0:1], r5[0:64, 0, 0, 0:1], minus_half[0:64, 0:1], ALU.pow).then_inc(c_pool, 1)

            def f_normalise(n, i):
                pool.wait_ge(f_rec, n + 1)
                pv = prob[i % 4].rearrange("p (th s) -> p th s", s=NS)
                nc.gpsimd.tensor_tensor(pv, pv, trec[:, i % 2].unsqueeze(2).to_broadcast([P, 32, NS]), ALU.mult) \
                    .then_inc(f_norm, 1)

            def f_rates(n, i):
                rate(mv5[:, i % 2], r5[:, i % 2], 0, 2, f_stats, n + 1, f_rate)

            with pool.Fori(0, B // 2) as t:
                own.enter(t, 4 * 8)
                for i in range(8 + 1):
                    if i < 8:
                        f_normalise(t * 8 + i, i)
                    if i >= 1:
                        f_rates(t * 8 + (i - 1), i - 1)
                own.leave(B // 2)

        @block.scalar
        def _(act):
            act.wait_ge(vec_made, 1)
            nc.scalar.activation(alpha_c, alpha_c, ACT.Tanh, scale=0.5).then_inc(tanh_alpha, 1)
            act.wait_ge(consts_made, 1)
            nc.scalar.copy(sel[:], sel_raw.rearrange("r c a n -> r c (a n)")).then_inc(sel_split, 1)
            act.wait_ge(w_in, 48)
            for k in range(KC):
                nc.scalar.copy(w_hi[:, k], w_raw[:, k]).then_inc(w_hi_made, 1)
            act.wait_ge(fold_in, 16 * FOLD_LOADS)
            nc.scalar.copy(cq_hi[:], cwq).then_inc(w_hi_made, 1)

            def ln1(u):
                act.wait_ge(ln1_rate, u.n + 1)
                if not (isinstance(u.n, int) and u.n == 0):
                    act.wait_ge(t1_done, KC * u.n)
                for j in range(TJ):
                    ins = nc.scalar.activation(xn[:, j], x[:, u.h, j], ACT.Identity,
                                               bias=r1[:, 2, j:j + 1], scale=r1[:, 1, j:j + 1])
                ins.then_inc(xn_made, 1)

            def x_high(u):
                for k in range(KC):
                    act.wait_ge(t1_done, KC * u.n + k + 1)
                    if k == 0 and not (isinstance(u.n, int) and u.n == 0):
                        act.wait_ge(v_done, CH * u.n)
                    nc.scalar.copy(x_hi[:, k], bank[3 + k][:]).then_inc(x_hi_made, 1)

            def qv(u, c):
                act.wait_ge(q_done, CH * u.n + c + 1)
                if not (isinstance(u.b, int) and u.b == 0):
                    act.wait_ge(qst_made, CH * (u.n - 2) + c + 1)
                    act.wait_ge(inner_made, CH * (u.n - 2) + c + 1)
                nc.scalar.activation(q[:, u.h, c], bank[0][:], ACT.Identity, bias=bq_c[:, c:c + 1]).then_inc(q_made, 1)
                act.wait_ge(v_done, CH * u.n + c + 1)
                if not (isinstance(u.b, int) and u.b == 0):
                    act.wait_ge(wo_done, 2 * (u.n - 1))
                nc.scalar.activation(v[:, u.h, c], bank[2][:], ACT.Identity, bias=bv2[:, c:c + 1],
                                     scale=keep2[:, c:c + 1]).then_inc(v_made, 1)

            def tanh_q(u, c):
                act.wait_ge(q_made, CH * u.n + c + 1)
                if not (isinstance(u.n, int) and u.n == 0 and c < 2):
                    act.wait_ge(inner_made, CH * u.n + c - 1)
                nc.scalar.activation(th[:, c % 2], q[:, u.h, c], ACT.Tanh, scale=aug_half[:, c:c + 1]).then_inc(th_made, 1)

            def softmax_exp(u):
                act.wait_ge(cen_made, u.n + 1)
                nc.scalar.activation(att[:], att[:], ACT.Exp, scale=RECUR_SCALE).then_inc(exp_made, 1)

            def att_high(u):
                act.wait_ge(att_t_done, u.n + 1)
                if not (isinstance(u.n, int) and u.n == 0):
                    act.wait_ge(spread_done, CH * u.n)
                nc.scalar.copy(att_parts[0:HEADS, :], bank[5][0:HEADS, :]).then_inc(att_hi_made, 1)

            def project(u):
                for k in range(KC):
                    act.wait_ge(t2_done, KC * u.n + k + 1)
                    if k == 0 and not (isinstance(u.n, int) and u.n == 0):
                        act.wait_ge(qp_done, HM * u.n)
                    nc.scalar.copy(x2_hi[:, k], bank[3 + k][:]).then_inc(x2_hi_made, 1)
                for m in range(HM):
                    act.wait_ge(s_done, HM * u.n + m + 1)
                    if m == 0 and u.h == 0 and not (isinstance(u.b, int) and u.b == 0):
                        act.wait_ge(pt_done, 4 * u.b)
                    nc.scalar.activation(sc[:, m, u.h * T:(u.h + 1) * T], bank[m][:], ACT.Identity,
                                         bias=m_bias[:, m:m + 1]).then_inc(s_made, 1)
                for m in range(HM):
                    act.wait_ge(qp_done, HM * u.n + m + 1)
                    if m == 0 and not (isinstance(u.n, int) and u.n == 0):
                        act.wait_ge(qh_out, 16 * u.n)
                    nc.scalar.activation(qh[:, m], bank[(2, 0)[m]][:], ACT.Identity,
                                         bias=cbq_c[:, m:m + 1]).then_inc(qh_made, 1)

            def slots(b):
                act.wait_ge(smax_made, b + 1)
                for m in range(HM):
                    nc.scalar.activation(sc[:, m], sc[:, m], ACT.Exp, bias=cneg[:, m:m + 1], scale=SCORE_SCALE,
                                         accum_out=csum[:, m:m + 1]).then_inc(p_made, 1)
                for t in range(4):
                    act.wait_ge(pt_done, 4 * b + t + 1)
                    if t >= 2:
                        act.wait_ge(z_pair, 4 * b + t - 1)
                    nc.scalar.copy(pt[:, t % 2], bank[3 + t % 2][:].rearrange("p (t n) -> p t n", t=2)) \
                        .then_inc(pt_made, 1)
                act.wait_ge(z_pair, 4 * b + 4)
                for k in range(KC):
                    nc.scalar.copy(zt[:, k, :, b, :], bank[1 + k][:, 0:HQ].rearrange("p (h q) -> p h q", q=NS)) \
                        .then_inc(zt_made, 1)

            def ln4(u):
                act.wait_ge(ln4_rate, u.n + 1)
                if u.h == 0 and not (isinstance(u.b, int) and u.b == 0):
                    act.wait_ge(z_pair, 4 * u.b)
                for j in range(TJ):
                    ins = nc.scalar.activation(xn2[:, u.h * TJ + j], x1[:, j], ACT.Identity,
                                               bias=r4[:, 2, j:j + 1], scale=r4[:, 1, j:j + 1])
                ins.then_inc(xn2_made, 1)

            def stage(b, first, last):
                for h in range(HALVES):
                    u = Unit(b, h)
                    ahead = not (last and h == 1)
                    softmax_exp(u)
                    if ahead:
                        x_high(u.next())
                        qv(u.next(), 0)
                    att_high(u)
                    if ahead:
                        qv(u.next(), 1)
                    tanh_q(u, 0)
                    tanh_q(u, 1)
                    if ahead:
                        qv(u.next(), 2)
                    tanh_q(u, 2)
                    if ahead:
                        qv(u.next(), 3)
                    tanh_q(u, 3)
                    if not (first and h == 0):
                        project(u.prev())
                        if h == 0:
                            slots(u.prev().b)
                    ln4(u)
                    if not last:
                        ln1(Unit(b + 1, h))

            act.wait_ge(rates_made, 1)
            ln1(Unit(0, 0))
            x_high(Unit(0, 0))
            for c in range(CH):
                qv(Unit(0, 0), c)
            ln1(Unit(0, 1))
            act.wait_ge(fold_pe, 3)
            nc.scalar.copy(m_hi[:], bank[6][:].rearrange("p (k n) -> p k n", k=KC)).then_inc(m_hi_made, 1)
            stage(0, True, False)
            with act.Fori(1, B - 1) as b:
                stage(b, False, False)
            stage(B - 1, False, True)
            project(Unit(B - 1, 1))
            slots(B - 1)

            act.wait_ge(pads_made, 1)
            act.wait_ge(c_dve, 5)
            with act.Fori(0, NS // GROUP) as g:
                for k in range(KC):
                    ins = nc.scalar.copy(hcur[:, k, :, 0:B],
                                         ht[:, k, :, bass.ds(g * GROUP, GROUP)].rearrange("p b j -> p j b"))
                ins.then_inc(hcur_made, 1)
                act.wait_ge(piece_used, PIECES * g + 2)
                nc.scalar.copy(u_sb[:, 0:512], bank[0][:])
                nc.scalar.copy(u_sb[:, 512:1024], bank[1][:]).then_inc(u_out, 1)
                act.wait_ge(ug_made, g + 1)
                nc.scalar.activation(eug.rearrange("p w c j b -> p (w c j b)"),
                                     ug.rearrange("p w c j b -> p (w c j b)"), ACT.Exp, scale=-1.0).then_inc(eug_made, 1)
                act.wait_ge(piece_used, PIECES * g + 6)
                nc.scalar.copy(ysb, bank[0][:, 0:D]).then_inc(y_out, 1)

            act.wait_ge(vp_done, 1)
            for i in range(4):
                ins = nc.scalar.copy(vp[:, i // 2, (i % 2) * 2:(i % 2) * 2 + 2, :],
                                     bank[4 + i][:].rearrange("p (b n) -> p b n", b=2))
            ins.then_inc(vp_made, 1)

            def f_exponent(n, i):
                act.wait_ge(f_cen, n + 1)
                nc.scalar.activation(prob[i % 4], prob[i % 4], ACT.Exp, scale=SCORE_SCALE).then_inc(f_exp, 1)

            def f_transposed(n, i):
                act.wait_ge(f_t_done, n + 1)
                if i >= 2:
                    act.wait_ge(f_y_done, n - 1)
                nc.scalar.copy(ptl[i % 2], bank[2 + i % 2][:]).then_inc(f_pt, 1)

            with act.Fori(0, B // 2) as t:
                for i in range(8 + 1):
                    if i < 8:
                        f_exponent(t * 8 + i, i)
                    if i >= 1:
                        f_transposed(t * 8 + (i - 1), i - 1)

        @block.vector
        def _(dve):
            own = Count(dve_own)

            def link(ins):
                own.step += 1
                ins.then_inc(dve_own, 1)
                dve.wait_ge(dve_own, own.now())

            def combine(st, both, apart, mv, done):
                nc.vector.tensor_tensor(both, st[:, :, 1:3], st[:, :, 4:6], ALU.add)
                link(nc.vector.tensor_tensor(apart, st[:, :, 1], st[:, :, 4], ALU.subtract))
                link(nc.vector.tensor_tensor(apart, apart, apart, ALU.mult))
                nc.vector.tensor_scalar(mv[:, :, 0], both[:, :, 0], 0.5, None, ALU.mult)
                nc.vector.scalar_tensor_tensor(out=mv[:, :, 1], in0=apart, scalar=D / 4.0, in1=both[:, :, 1],
                                               op0=ALU.mult, op1=ALU.add).then_inc(done, 1)

            def moments(src, mv, done):
                for j in range(TJ - 1):
                    nc.vector.bn_stats(stats[:, j], src(j))
                link(nc.vector.bn_stats(stats[:, TJ - 1], src(TJ - 1)))
                combine(stats[:], both[:], apart[:], mv, done)

            def ln1(u):
                dve.wait_ge(x_in[u.h], 16 * (u.b + 1))
                if not (isinstance(u.n, int) and u.n == 0):
                    dve.wait_ge(ln1_rate, u.n)
                moments(lambda j: x[:, u.h, j], mv1, ln1_stats)

            def x_low(u):
                for k in range(KC):
                    dve.wait_ge(x_hi_made, KC * u.n + k + 1)
                    nc.vector.tensor_tensor(x_lo[:, k], bank[3 + k][:], x_hi[:, k], ALU.subtract).then_inc(x_lo_made, 1)

            def q_times_k(u, c):
                dve.wait_ge(q_made, CH * u.n + c + 1)
                dve.wait_ge(k_done, CH * u.n + c + 1)
                if not (isinstance(u.n, int) and u.n == 0 and c < 2):
                    dve.wait_ge(sum_done, CH * u.n + c - 1)
                nc.vector.scalar_tensor_tensor(out=qk[:, c % 2], in0=bank[1][:], scalar=bk_c[:, c:c + 1],
                                               in1=q[:, u.h, c], op0=ALU.add, op1=ALU.mult).then_inc(qk_made, 1)

            def softmax(u):
                heads = bank[5][:, 0:TJ * HEADS].rearrange("p (j h) -> p j h", h=HEADS)
                dve.wait_ge(sum_done, CH * (u.n + 1))
                link(nc.vector.tensor_reduce(smx[:], heads, X, ALU.max))
                nc.vector.tensor_tensor(att[:], heads, smx[:].unsqueeze(2).to_broadcast([P, TJ, HEADS]), ALU.subtract) \
                    .then_inc(cen_made, 1)
                dve.wait_ge(exp_made, u.n + 1)
                link(nc.vector.tensor_reduce(sums[:], att[:], X, ALU.add))
                link(nc.vector.reciprocal(rsum[:], sums[:]))
                nc.vector.tensor_tensor(att[:], att[:], rsum[:].unsqueeze(2).to_broadcast([P, TJ, HEADS]), ALU.mult) \
                    .then_inc(att_made, 1)

            def att_low(u):
                dve.wait_ge(att_hi_made, u.n + 1)
                nc.vector.tensor_tensor(att_parts[32:32 + HEADS, :], bank[5][0:HEADS, :], att_parts[0:HEADS, :],
                                        ALU.subtract).then_inc(att_lo_made, 1)

            def recur(u, c):
                dve.wait_ge(spread_done, CH * u.n + c + 1)
                dve.wait_ge(v_made, CH * u.n + c + 1)
                nc.vector.tensor_tensor(v[:, u.h, c], bank[6 + c % 2][:], v[:, u.h, c], ALU.mult).then_inc(val_made, 1)
                dve.wait_ge(val_made, CH * u.n + c + 1)
                if not (isinstance(u.n, int) and u.n == 0 and c < 2):
                    dve.wait_ge(qst_made, CH * u.n + c - 1)
                initial = 0.0 if u.h == 0 else carry[:, c:c + 1]
                nc.vector.tensor_tensor_scan(st[:, c % 2], decay[:, c:c + 1].to_broadcast([P, T]), v[:, u.h, c],
                                             initial, ALU.mult, ALU.add).then_inc(scan_made, 1)
                if u.h == 0:
                    dve.wait_ge(scan_made, CH * u.n + c + 1)
                    link(nc.vector.tensor_copy(carry[:, c:c + 1], st[:, c % 2, T - 1:T]))

            def inner(u, c):
                dve.wait_ge(qst_made, CH * u.n + c + 1)
                dve.wait_ge(th_made, CH * u.n + c + 1)
                nc.vector.scalar_tensor_tensor(out=v[:, u.h, c], in0=th[:, c % 2], scalar=1.0, in1=v[:, u.h, c],
                                               op0=ALU.add, op1=ALU.add).then_inc(inner_made, 1)

            def out_rows(u):
                for p in range(2):
                    dve.wait_ge(wo_done, 2 * u.n + p + 1)
                    ins = nc.vector.scalar_tensor_tensor(
                        out=o[:, 2 * p:2 * p + 2], in0=bank[6 + p][:].rearrange("p (j d) -> p j d", j=2), scalar=0.5,
                        in1=bo_r[:].unsqueeze(1).to_broadcast([P, 2, D]), op0=ALU.mult, op1=ALU.add)
                    ins.then_inc(o_made, 1)

            def norms(u):
                dve.wait_ge(o_made, 2 * u.n + 2)
                moments(lambda j: o[:, j], mv2, ln2_stats)
                dve.wait_ge(ln2_rate, u.n + 1)
                for j in range(TJ):
                    ins = nc.vector.tensor_scalar(o[:, j], o[:, j], mv2[:, j, 0:1], r2[:, 1, j:j + 1], ALU.subtract, ALU.mult)
                ins.then_inc(ln2_made, 1)
                dve.wait_ge(gain_made, u.n + 1)
                moments(lambda j: o[:, j], mv3, ln3_stats)
                dve.wait_ge(ln3_rate, u.n + 1)
                for j in range(TJ - 1):
                    nc.vector.tensor_scalar(o[:, j], o[:, j], mv3[:, j, 0:1], r3[:, 1, j:j + 1], ALU.subtract, ALU.mult)
                j = TJ - 1
                link(nc.vector.tensor_scalar(o[:, j], o[:, j], mv3[:, j, 0:1], r3[:, 1, j:j + 1], ALU.subtract, ALU.mult))
                if not (isinstance(u.n, int) and u.n == 0):
                    dve.wait_ge(x1_out, 16 * u.n)
                    dve.wait_ge(xn2_made, u.n)
                nc.vector.tensor_tensor(x1[:], o[:], x[:, u.h], ALU.add).then_inc(x1_made, 1)
                dve.wait_ge(x1_made, u.n + 1)
                moments(lambda j: x1[:, j], mv4, ln4_stats)

            def x2_low(u):
                for k in range(KC):
                    dve.wait_ge(x2_hi_made, KC * u.n + k + 1)
                    nc.vector.tensor_tensor(x2_lo[:, k], bank[3 + k][:], x2_hi[:, k], ALU.subtract).then_inc(x2_lo_made, 1)

            def slot_max(b):
                dve.wait_ge(s_made, HM * HALVES * (b + 1))
                link(nc.vector.tensor_reduce(cmx[:], sc[:], X, ALU.max))
                nc.vector.tensor_scalar(cneg[:], cmx[:], -SCORE_SCALE, None, ALU.mult).then_inc(smax_made, 1)

            def slot_norm(b):
                dve.wait_ge(p_made, HM * (b + 1))
                link(nc.vector.reciprocal(crec[:], csum[:]))
                for m in range(HM):
                    nc.vector.tensor_scalar(sc[:, m], sc[:, m], crec[:, m:m + 1], None, ALU.mult).then_inc(pn_made, 1)

            def stage(b, first, last):
                for h in range(HALVES):
                    u = Unit(b, h)
                    ahead = not (last and h == 1)
                    softmax(u)
                    if ahead:
                        x_low(u.next())
                        q_times_k(u.next(), 0)
                    att_low(u)
                    if ahead:
                        q_times_k(u.next(), 1)
                    recur(u, 0)
                    recur(u, 1)
                    inner(u, 0)
                    if ahead:
                        q_times_k(u.next(), 2)
                    recur(u, 2)
                    inner(u, 1)
                    recur(u, 3)
                    if ahead:
                        q_times_k(u.next(), 3)
                    inner(u, 2)
                    inner(u, 3)
                    if not (first and h == 0):
                        x2_low(u.prev())
                        if h == 0:
                            slot_max(u.prev().b)
                    out_rows(u)
                    if h == 0 and not first:
                        slot_norm(u.prev().b)
                    norms(u)
                    if not last:
                        ln1(Unit(b + 1, h))

            nc.vector.memset(att_parts[:].bitcast(F32), 0.0)
            dve.wait_ge(vec_turned, 1)
            nc.vector.tensor_copy(vec[:], bank[7][:, 0:VROWS]).then_inc(vec_made, 1)
            dve.wait_ge(tanh_alpha, 1)
            nc.vector.tensor_scalar(decay[:], alpha_c, 0.5, 0.5, ALU.mult, ALU.add)
            link(nc.vector.tensor_scalar(keep2[:], alpha_c, -1.0, 1.0, ALU.mult, ALU.add))
            nc.vector.tensor_tensor(bv2[:], bv_c, keep2[:], ALU.mult)
            nc.vector.tensor_scalar(aug_half[:], aug_c, 0.5, None, ALU.mult).then_inc(rates_made, 1)
            ln1(Unit(0, 0))
            for k in range(KC):
                dve.wait_ge(w_hi_made, k + 1)
                nc.vector.tensor_tensor(w_lo[:, k], w_raw[:, k], w_hi[:, k], ALU.subtract).then_inc(w_lo_made, 1)
            ln1(Unit(0, 1))
            dve.wait_ge(w_hi_made, KC + 1)
            nc.vector.tensor_tensor(cq_lo[:], cwq, cq_hi[:], ALU.subtract).then_inc(w_lo_made, 1)
            x_low(Unit(0, 0))
            for c in range(CH):
                q_times_k(Unit(0, 0), c)
            dve.wait_ge(fold_pe, 1)
            nc.vector.tensor_copy(sqt, bank[7][:, 0:KC * NS].rearrange("p (k n) -> p k n", k=KC))
            nc.vector.tensor_copy(wkt, bank[6][:].rearrange("p (m n) -> p m n", m=HM)).then_inc(fold_dve, 1)
            dve.wait_ge(fold_pe, 2)
            for m in range(HM):
                link(nc.vector.tensor_scalar(qht[:, m], bank[7][:, m * NS:(m + 1) * NS], dbq_c[:, m:m + 1], None, ALU.add))
                ins = nc.vector.tensor_tensor(qbd[:, m].rearrange("p (h s) -> p h s", s=NS),
                                              qht[:, m].unsqueeze(1).to_broadcast([P, 8, NS]),
                                              mask8[:].unsqueeze(2).to_broadcast([P, 8, NS]), ALU.mult)
            ins.then_inc(fold_dve, 1)
            dve.wait_ge(m_hi_made, 1)
            nc.vector.tensor_copy(m_bias[:], bank[7][:, 0:HM])
            nc.vector.tensor_tensor(m_lo[:], bank[6][:].rearrange("p (k n) -> p k n", k=KC), m_hi[:], ALU.subtract) \
                .then_inc(m_lo_made, 1)

            stage(0, True, False)
            with dve.Fori(1, B - 1) as b:
                own.enter(b - 1, DVE_OWN)
                stage(b, False, False)
                own.leave(B - 2)
            stage(B - 1, False, True)
            x2_low(Unit(B - 1, 1))
            slot_max(B - 1)
            slot_norm(B - 1)

            dve.wait_ge(late_in, 16 * LATE_LOADS)
            dve.wait_ge(c_pe, 1)
            nc.vector.tensor_tensor(vo, bank[0][0:64, 0:D], dbv_r, ALU.add).then_inc(c_dve, 1)
            dve.wait_ge(c_pe, 2)
            nc.vector.tensor_copy(vot.rearrange("p k n -> p (k n)"), bank[1][:, 0:128]).then_inc(c_dve, 1)
            dve.wait_ge(c_pe, 3)
            link(nc.vector.tensor_tensor(os_, bank[2][0:64, 0:D], dbo_r, ALU.add))
            link(nc.vector.tensor_tensor(os_, os_, slot_r, ALU.add))
            link(nc.vector.bn_stats(st5[0:64, 0, 0], os_))
            nc.vector.bn_aggr(mv5[0:64, 0, 0], st5[0:64, 0, 0]).then_inc(c_dve, 1)
            dve.wait_ge(c_pool, 1)
            link(nc.vector.tensor_scalar(hs, os_, mv5[0:64, 0, 0, 0:1], r5[0:64, 0, 1, 0:1], ALU.subtract, ALU.mult))
            link(nc.vector.tensor_tensor(hs, hs, eg_r, ALU.mult))
            nc.vector.tensor_tensor(hs, hs, eb_r, ALU.add).then_inc(c_dve, 1)
            dve.wait_ge(c_pe, 4)
            nc.vector.tensor_copy(ht.rearrange("p k b e -> p (k b e)"), bank[3][:, 128:256])
            nc.vector.tensor_tensor(o2t, bank[3][:, 0:128].rearrange("p (k b e) -> p k b e", k=KC, b=B),
                                    b2t.unsqueeze(2).to_broadcast([P, KC, B, NS]), ALU.add).then_inc(c_dve, 1)

            with dve.Fori(0, NS // GROUP) as g:
                own.enter(g, 3)
                dve.wait_ge(piece_used, PIECES * g + 4)
                nc.vector.tensor_copy(g_sb[:, 0:512], bank[2][:])
                nc.vector.tensor_copy(g_sb[:, 512:1024], bank[3][:]).then_inc(g_out, 1)
                for w in range(2):
                    dve.wait_ge(ut_done, 2 * g + w + 1)
                    for i in range(2):
                        bias = b1t[:, w, bass.ds(g * GROUP, GROUP), 4 * i:4 * i + 4].rearrange("p j c -> p c j") \
                            .unsqueeze(3).to_broadcast([P, 4, GROUP, B])
                        ins = nc.vector.tensor_tensor(
                            ug[:, w, 4 * i:4 * i + 4],
                            bank[4 + 2 * w + i][:].rearrange("p (c j n) -> p c j n", c=4, j=GROUP)[:, :, :, 0:B],
                            bias, ALU.add)
                ins.then_inc(ug_made, 1)
                dve.wait_ge(eug_made, g + 1)
                flat = "p w c j b -> p (w c j b)"
                link(nc.vector.tensor_scalar(eug.rearrange(flat), eug.rearrange(flat), 1.0, None, ALU.add))
                link(nc.vector.reciprocal(eug.rearrange(flat), eug.rearrange(flat)))
                link(nc.vector.tensor_tensor(ug.rearrange(flat), ug.rearrange(flat), eug.rearrange(flat), ALU.mult))
                nc.vector.tensor_tensor(at[:, :, :, 0:B], ug[:, 0], ug[:, 1], ALU.mult).then_inc(at_made, 1)
                dve.wait_ge(yt_done, g + 1)
                for k in range(KC):
                    part = o2t[:, k, :, bass.ds(g * GROUP, GROUP)].rearrange("p b j -> p j b")
                    ins = nc.vector.tensor_tensor(
                        part, part, bank[6][:, k * P:(k + 1) * P].rearrange("p (j n) -> p j n", j=GROUP)[:, :, 0:B], ALU.add)
                ins.then_inc(slots_made, 1)
                own.leave(NS // GROUP)

            dve.wait_ge(kv_done, 1)
            for w, bias in ((0, cbk_c), (1, cbv_c)):
                for m in range(HM):
                    link(nc.vector.tensor_scalar(kv_t[:, w, m].rearrange("p b s -> p (b s)"),
                                                 bank[2 + w][:, m * 64:(m + 1) * 64], bias[:, m:m + 1], None, ALU.add))
                    dst = (kb, vb)[w]
                    for b in range(B):
                        ins = nc.vector.tensor_tensor(
                            dst[:, m, b].rearrange("p (h s) -> p h s", s=NS),
                            kv_t[:, w, m, b].unsqueeze(1).to_broadcast([P, 8, NS]),
                            mask8[:].unsqueeze(2).to_broadcast([P, 8, NS]), ALU.mult)
            ins.then_inc(kv_made, 1)

            def f_centre(n, i):
                scores = bank[i % 2][:].rearrange("p (th s) -> p th s", s=NS)
                dve.wait_ge(f_s_done, n + 1)
                if i >= 4:
                    dve.wait_ge(f_t_done, n - 3)
                link(nc.vector.tensor_reduce(tmx[:, i % 2], scores, X, ALU.max))
                nc.vector.tensor_tensor(prob[i % 4].rearrange("p (th s) -> p th s", s=NS), scores,
                                        tmx[:, i % 2].unsqueeze(2).to_broadcast([P, 32, NS]), ALU.subtract).then_inc(f_cen, 1)

            def f_sums(n, i):
                dve.wait_ge(f_exp, n + 1)
                if i >= 2:
                    dve.wait_ge(f_norm, n - 1)
                link(nc.vector.tensor_reduce(tsum[:, i % 2], prob[i % 4].rearrange("p (th s) -> p th s", s=NS), X, ALU.add))
                nc.vector.reciprocal(trec[:, i % 2], tsum[:, i % 2]).then_inc(f_rec, 1)

            def f_output(n, i):
                dve.wait_ge(f_y_done, n + 1)
                nc.vector.tensor_tensor(y[i % 2].rearrange("p (j d) -> p j d", j=2),
                                        bank[4 + i % 2][:].rearrange("p (j d) -> p j d", j=2),
                                        cbo_r[:].unsqueeze(1).to_broadcast([P, 2, D]), ALU.add).then_inc(f_y_made, 1)
                dve.wait_ge(f_y_made, n + 1)
                nc.vector.bn_stats(st5[:, i % 2, 0], y[i % 2][:, 0:D])
                link(nc.vector.bn_stats(st5[:, i % 2, 1], y[i % 2][:, D:2 * D]))
                combine(st5[:, i % 2], both[:, 0:2], apart[:, 0:2], mv5[:, i % 2], f_stats)

            def f_result(n, i, t):
                dve.wait_ge(f_rate, n + 1)
                for j in range(2):
                    ins = nc.vector.tensor_scalar(y[i % 2][:, j * D:(j + 1) * D], y[i % 2][:, j * D:(j + 1) * D],
                                                  mv5[:, i % 2, j, 0:1], r5[:, i % 2, 1, j:j + 1], ALU.subtract, ALU.mult)
                link(ins)
                if i % 4 == 0:
                    dve.wait_ge(x1_back[i // 4], 32 * (t + 1))
                if i >= 2:
                    dve.wait_ge(res_out[i % 2], (t * 4 + i // 2) * 16)
                nc.vector.tensor_tensor(res[i % 2], y[i % 2],
                                        x1_in[:, i // 4, 2 * (i % 4):2 * (i % 4) + 2].rearrange("p j d -> p (j d)"),
                                        ALU.add).then_inc(f_res, 1)

            with dve.Fori(0, B // 2) as t:
                own.enter(t, 6 * 8)
                for i in range(8 + 4):
                    if i < 8:
                        f_centre(t * 8 + i, i)
                    if 1 <= i <= 8:
                        f_sums(t * 8 + (i - 1), i - 1)
                    if i >= 4:
                        f_result(t * 8 + (i - 4), i - 4, t)
                    if 3 <= i <= 10:
                        f_output(t * 8 + (i - 3), i - 3)
                for s in range(2):
                    dve.wait_ge(res_out[s], (t * 4 + 4) * 16)
                own.leave(B // 2)

        @block.tensor
        def _(pe):
            def t1(u, prev):
                pe.wait_ge(xn_made, u.n + 1)
                for k in range(KC):
                    prev(k)
                    for j in range(TJ):
                        ins = nc.tensor.transpose(bank[3 + k][:, j * P:(j + 1) * P], xn[:, j, k * P:(k + 1) * P], ident[:])
                    ins.then_inc(t1_done, 1)

            def project(dst, w_h, w_l, x_h, x_l, cols, done):
                n = 0
                for k in range(KC):
                    for w, r in ((w_h, x_h), (w_h, x_l), (w_l, x_h)):
                        ins = nc.tensor.matmul(dst, w[:, k, cols], r[:, k], start=n == 0, stop=n == 3 * KC - 1)
                        n += 1
                ins.then_inc(done, 1)

            def qkv(u, c, free):
                if c == 0:
                    pe.wait_ge(x_hi_made, KC * (u.n + 1))
                    pe.wait_ge(x_lo_made, KC * (u.n + 1))
                cols = slice(c * P, (c + 1) * P)
                for w, done in ((0, q_done), (1, k_done), (2, v_done)):
                    if c:
                        pe.wait_ge((q_made, qk_made, v_made)[w], CH * u.n + c)
                    else:
                        free(w)
                    project(bank[w][:], w_hi[:, :, w], w_lo[:, :, w], x_hi, x_lo, cols, done)

            def head_sums(u, c):
                pe.wait_ge(qk_made, CH * u.n + c + 1)
                if c == 0 and not (isinstance(u.n, int) and u.n == 0):
                    pe.wait_ge(att_lo_made, u.n)
                for j in range(TJ):
                    at_ = j * HEADS + 2 * c
                    ins = nc.tensor.matmul(bank[5][:, at_:at_ + 2], qk[:, c % 2, j * P:(j + 1) * P], pair[:],
                                           start=True, stop=True)
                ins.then_inc(sum_done, 1)

            def att_transpose(u):
                pe.wait_ge(att_made, u.n + 1)
                for j in range(TJ):
                    ins = nc.tensor.transpose(bank[5][0:HEADS, j * P:(j + 1) * P], att[:, j], ident[:])
                ins.then_inc(att_t_done, 1)

            def spread(u, c):
                if c == 0:
                    pe.wait_ge(att_lo_made, u.n + 1)
                if c >= 2:
                    pe.wait_ge(val_made, CH * u.n + c - 1)
                elif not (isinstance(u.n, int) and u.n == 0):
                    pe.wait_ge(o_made, 2 * u.n + c - 1)
                nc.tensor.matmul(bank[6 + c % 2][:], sel[:, c], att_parts[:], start=True, stop=True) \
                    .then_inc(spread_done, 1)

            def out_project(u):
                pe.wait_ge(inner_made, CH * (u.n + 1))
                for p in range(2):
                    for j in (2 * p, 2 * p + 1):
                        for c in range(CH):
                            ins = nc.tensor.matmul(bank[6 + p][:, (j % 2) * D:(j % 2 + 1) * D],
                                                   v[:, u.h, c, j * P:(j + 1) * P], wo[:, c], start=c == 0, stop=c == CH - 1)
                    ins.then_inc(wo_done, 1)

            def slot_scores(n, ahead, first_h):
                u = n
                pe.wait_ge(xn2_made, u.n + 1)
                for k in range(KC):
                    if ahead:
                        pe.wait_ge(x_lo_made, KC * (u.n + 2) + k + 1)
                    elif u.h == 0:
                        pe.wait_ge(pt_made, 4 * u.b - 1 + k)
                    else:
                        pe.wait_ge(x2_lo_made, KC * (u.n - 1) + k + 1)
                    for j in range(TJ):
                        ins = nc.tensor.transpose(bank[3 + k][:, j * P:(j + 1) * P],
                                                  xn2[:, u.h * TJ + j, k * P:(k + 1) * P], ident[:])
                    ins.then_inc(t2_done, 1)
                pe.wait_ge(x2_hi_made, KC * (u.n + 1))
                pe.wait_ge(x2_lo_made, KC * (u.n + 1))
                for m in range(HM):
                    if ahead:
                        pe.wait_ge((q_made, qk_made)[m], CH * (u.n + 3))
                    elif m == 0:
                        pe.wait_ge(qh_made, HM * u.n)
                    elif u.h == 0:
                        pe.wait_ge(zt_made, KC * u.b)
                    else:
                        pe.wait_ge(s_made, HM * u.n)
                    project(bank[m][:], m_hi, m_lo, x2_hi, x2_lo, slice(m * P, (m + 1) * P), s_done)
                for m in range(HM):
                    if m == 1:
                        pe.wait_ge(s_made, HM * u.n + 1)
                    elif ahead:
                        pe.wait_ge(v_made, CH * (u.n + 3))
                    elif u.h == 0:
                        pe.wait_ge(zt_made, KC * u.b)
                    else:
                        pe.wait_ge(qh_made, HM * u.n)
                    project(bank[(2, 0)[m]][:], cq_hi, cq_lo, x2_hi, x2_lo, slice(m * P, (m + 1) * P), qp_done)

            def slots(b):
                pe.wait_ge(pn_made, HM * (b + 1))
                pe.wait_ge(s_made, HM * HALVES * (b + 1))
                pe.wait_ge(qh_made, HM * (HALVES * b + 1) + 1)

                def turn(t):
                    if t < 2:
                        pe.wait_ge(x2_lo_made, KC * (HALVES * b + 1) + t + 1)
                    else:
                        pe.wait_ge(pt_made, 4 * b + t - 1)
                    for i in range(2):
                        for m in range(HM):
                            ins = nc.tensor.transpose(bank[3 + t % 2][:, i * HQ + m * P:i * HQ + (m + 1) * P],
                                                      sc[:, m, (2 * t + i) * P:(2 * t + i + 1) * P], ident[:])
                    ins.then_inc(pt_done, 1)

                def add(t):
                    pe.wait_ge(pt_made, 4 * b + t + 1)
                    for i in range(2):
                        for k in range(KC):
                            ins = nc.tensor.matmul(bank[1 + k][:, 0:HQ], xn2[:, 2 * t + i, k * P:(k + 1) * P], pt[:, t % 2, i],
                                                   start=t + i == 0, stop=t == 3 and i == 1)
                    ins.then_inc(z_pair, 1)

                turn(0)
                for t in range(4):
                    if t < 3:
                        turn(t + 1)
                    add(t)

            def stage(b, first, last):
                for h in range(HALVES):
                    u = Unit(b, h)
                    ahead = not (last and h == 1)
                    w = u.next()
                    head_sums(u, 3)

                    def banks34(k):
                        if first:
                            pe.wait_ge(x_lo_made, KC * (w.n - 1) + k + 1)
                        elif h == 0:
                            pe.wait_ge(x2_lo_made, KC * (w.n - 3) + k + 1)
                        else:
                            pe.wait_ge(pt_made, 4 * b - 1 + k)

                    def banks012(i):
                        if first:
                            pe.wait_ge((q_made, qk_made, v_made)[i], CH * w.n)
                        elif i == 0:
                            pe.wait_ge(qh_made, HM * (w.n - 2))
                        elif h == 1:
                            pe.wait_ge(zt_made, KC * b)
                        elif i == 1:
                            pe.wait_ge(s_made, HM * (w.n - 2))
                        else:
                            pe.wait_ge(qh_made, HM * (w.n - 3) + 1)

                    if ahead:
                        t1(w, banks34)
                        qkv(w, 0, banks012)
                    att_transpose(u)
                    if ahead:
                        qkv(w, 1, banks012)
                        head_sums(w, 0)
                    spread(u, 0)
                    spread(u, 1)
                    if ahead:
                        qkv(w, 2, banks012)
                        head_sums(w, 1)
                    spread(u, 2)
                    spread(u, 3)
                    if ahead:
                        qkv(w, 3, banks012)
                        head_sums(w, 2)
                    if not (first and h == 0):
                        slot_scores(u.prev(), ahead, first)
                    out_project(u)
                    if h == 0 and not first:
                        slots(u.prev().b)

            pe.wait_ge(consts_made, 1)
            pe.wait_ge(vec_in, 16 * len(VECTORS))
            nc.tensor.transpose(bank[7][:, 0:VROWS], vec_rows, ident[0:VROWS, 0:VROWS]).then_inc(vec_turned, 1)
            t1(Unit(0, 0), lambda k: None)
            pe.wait_ge(w_lo_made, KC)
            for c in range(CH):
                qkv(Unit(0, 0), c, lambda i: None)
                if c:
                    head_sums(Unit(0, 0), c - 1)
            pe.wait_ge(fold_in, 16 * FOLD_LOADS)
            pe.wait_ge(small_in, 16 * SMALL_LOADS)
            for k in range(KC):
                nc.tensor.transpose(bank[7][:, k * NS:(k + 1) * NS], slot_in[:, k * P:(k + 1) * P], ident[0:NS, 0:NS])
            for m in range(HM):
                for k in range(KC):
                    ins = nc.tensor.transpose(bank[6][:, m * D + k * P:m * D + (k + 1) * P], dwk[:, k, m * P:(m + 1) * P], ident[:])
            ins.then_inc(fold_pe, 1)
            pe.wait_ge(fold_dve, 1)
            for m in range(HM):
                for k in range(KC):
                    ins = nc.tensor.matmul(bank[7][:, m * NS:(m + 1) * NS], dwq[:, k, m * P:(m + 1) * P], sqt[:, k],
                                           start=k == 0, stop=k == KC - 1)
            ins.then_inc(fold_pe, 1)
            pe.wait_ge(fold_dve, 2)
            for k in range(KC):
                for m in range(HM):
                    nc.tensor.matmul(bank[6][:, k * HQ + m * P:k * HQ + (m + 1) * P], wkt[:, m, k * P:(k + 1) * P], qbd[:, m],
                                     start=True, stop=True)
            for m in range(HM):
                ins = nc.tensor.matmul(bank[7][:, m:m + 1], qbd[:, m], dbk_c[:, m:m + 1], start=True, stop=True)
            ins.then_inc(fold_pe, 1)
            pe.wait_ge(m_lo_made, 1)
            pe.wait_ge(w_lo_made, KC + 1)
            pe.wait_ge(sel_split, 1)

            stage(0, True, False)
            with pe.Fori(1, B - 1) as b:
                stage(b, False, False)
            stage(B - 1, False, True)
            slot_scores(Unit(B - 1, 1), False, False)
            slots(B - 1)

            pe.wait_ge(late_in, 16 * LATE_LOADS)
            pe.wait_ge(zt_made, KC * B)
            pe.wait_ge(qh_made, HM * HALVES * B)
            for h in range(MH):
                for k in range(KC):
                    ins = nc.tensor.matmul(bank[0][0:64, h * 16:(h + 1) * 16], zt[:, k, h].rearrange("p b q -> p (b q)"),
                                           d_wv[:, k, h * 16:(h + 1) * 16], start=k == 0, stop=k == KC - 1)
            ins.then_inc(c_pe, 1)
            pe.wait_ge(c_dve, 1)
            for k in range(KC):
                ins = nc.tensor.transpose(bank[1][:, k * 64:(k + 1) * 64], vo[:, k * P:(k + 1) * P], ident[0:64, 0:64])
            ins.then_inc(c_pe, 1)
            pe.wait_ge(c_dve, 2)
            for k in range(KC):
                ins = nc.tensor.matmul(bank[2][0:64, 0:D], vot[:, k], d_wo[:, k], start=k == 0, stop=k == KC - 1)
            ins.then_inc(c_pe, 1)
            pe.wait_ge(c_dve, 4)
            for k in range(KC):
                nc.tensor.transpose(bank[3][:, k * 64:(k + 1) * 64], os_[:, k * P:(k + 1) * P], ident[0:64, 0:64])
            hs_v = hs.rearrange("p (n k) -> p k n", k=KC)
            for k in range(KC):
                ins = nc.tensor.transpose(bank[3][:, 128 + k * 64:128 + (k + 1) * 64], hs_v[:, k], ident[0:64, 0:64])
            ins.then_inc(c_pe, 1)

            with pe.Fori(0, NS // GROUP) as g:
                pe.wait_ge(hcur_made, g + 1)
                for k in range(PIECES):
                    if k == 4:
                        for w, out_s, src in ((0, u_out, u_sb), (1, g_out, g_sb)):
                            pe.wait_ge(out_s, g + 1)
                            view = src.rearrange("p (n c) -> p c n", c=FC)
                            for c in range(FC):
                                ins = nc.tensor.transpose(bank[4 + 2 * w + c // 4][:, (c % 4) * P:(c % 4 + 1) * P], view[:, c], ident[:])
                            ins.then_inc(ut_done, 1)
                        pe.wait_ge(at_made, g + 1)
                    pe.wait_ge(piece_in[k % RING], (g * 2 + (k // RING + 1)) * 16)
                    if k < 4:
                        for n in range(2):
                            for j in range(GROUP):
                                ins = nc.tensor.matmul(bank[2 * (k // 2) + n][32 * j:32 * j + 32, :], hcur[:, part(k), j],
                                                       ring[:, k % RING, j, n * 512:(n + 1) * 512],
                                                       start=k % 2 == 0, stop=k % 2 == 1, tile_position=(0, 32 * j))
                    else:
                        for c in range(4):
                            for j in range(GROUP):
                                cc = part(k) * 4 + c
                                ins = nc.tensor.matmul(bank[0][32 * j:32 * j + 32, 0:D], at[:, cc, j],
                                                       ring[:, k % RING, j, c * D:(c + 1) * D],
                                                       start=k == 4 and c == 0, stop=k == 5 and c == 3, tile_position=(0, 32 * j))
                    ins.then_inc(piece_used, 1)
                pe.wait_ge(y_out, g + 1)
                for k in range(KC):
                    ins = nc.tensor.transpose(bank[6][:, k * P:(k + 1) * P], ysb[:, k * P:(k + 1) * P], ident[:])
                ins.then_inc(yt_done, 1)

            pe.wait_ge(slots_made, NS // GROUP)
            for w, weight in ((0, c_wk), (1, c_wv)):
                for m in range(HM):
                    for k in range(KC):
                        ins = nc.tensor.matmul(bank[2 + w][:, m * 64:(m + 1) * 64], weight[:, k, m * P:(m + 1) * P],
                                               o2t[:, k].rearrange("p b e -> p (b e)"), start=k == 0, stop=k == KC - 1)
            ins.then_inc(kv_done, 1)
            pe.wait_ge(kv_made, 1)
            for m in range(HM):
                for b in range(B):
                    i = m * B + b
                    ins = nc.tensor.matmul(bank[4 + i // 2][:, (i % 2) * D:(i % 2 + 1) * D], vb[:, m, b], c_wo[:, m],
                                           start=True, stop=True)
            ins.then_inc(vp_done, 1)

            def f_scores(n, i, t):
                if i % 4 == 0:
                    pe.wait_ge(qh_back[i // 4], (t + 1) * 16)
                if i >= 2:
                    pe.wait_ge(f_cen, n - 1)
                for j in range(2):
                    tile = 2 * (i % 4) + j
                    for m in range(HM):
                        ins = nc.tensor.matmul(bank[i % 2][:, j * HQ + m * P:j * HQ + (m + 1) * P],
                                               qh_in[:, i // 4, m, tile * P:(tile + 1) * P],
                                               kb[:, m, t * 2 + i // 4], start=True, stop=True)
                ins.then_inc(f_s_done, 1)

            def f_turn(n, i):
                pe.wait_ge(f_norm, n + 1)
                if i >= 2:
                    pe.wait_ge(f_pt, n - 1)
                for j in range(4):
                    ins = nc.tensor.transpose(bank[2 + i % 2][:, j * P:(j + 1) * P], prob[i % 4][:, j * P:(j + 1) * P], ident[:])
                ins.then_inc(f_t_done, 1)

            def f_values(n, i, t):
                pe.wait_ge(f_pt, n + 1)
                if i >= 2:
                    pe.wait_ge(f_y_made, n - 1)
                for j in range(2):
                    for m in range(HM):
                        ins = nc.tensor.matmul(bank[4 + i % 2][:, j * D:(j + 1) * D],
                                               ptl[i % 2][:, (2 * j + m) * P:(2 * j + m + 1) * P],
                                               vp[:, m, t * 2 + i // 4], start=m == 0, stop=m == HM - 1)
                ins.then_inc(f_y_done, 1)

            pe.wait_ge(vp_made, 1)
            with pe.Fori(0, B // 2) as t:
                for i in range(8 + 2):
                    if i < 8:
                        f_scores(t * 8 + i, i, t)
                    if 1 <= i <= 8:
                        f_turn(t * 8 + (i - 1), i - 1)
                    if i >= 2:
                        f_values(t * 8 + (i - 2), i - 2, t)


def kernel(**inputs):
    import numpy as np
    import concourse.bacc as bacc
    from concourse.bass_utils import run_bass_kernel_spmd

    nc = bacc.Bacc("TRN2", target_bir_lowering=False, num_devices=1)
    arrays, aps = {}, {}
    for name, value in inputs.items():
        value = np.ascontiguousarray(value)
        arrays[name] = value
        aps[name] = nc.dram_tensor(name, value.shape, mybir.dt.from_np(value.dtype), kind="ExternalInput").ap()
    result = nc.dram_tensor("result", (B, S, D), F32, kind="ExternalOutput").ap()
    build(nc, aps, result)
    r = run_bass_kernel_spmd(nc, [arrays], core_ids=[0])
    return r.results[0]["result"]
```

```python
import concourse.bass as bass
from concourse import mybir
from contextlib import ExitStack

F32 = mybir.dt.float32
F32R = mybir.dt.float32r
ALU = mybir.AluOpType
ACT = mybir.ActivationFunctionType
X = mybir.AxisListType.X

P = 128
B, S, D = 4, 1024, 256
KC = D // P
INNER, HEADS = 512, 8
CH = INNER // P
T = 512
TJ = T // P
HALVES = S // T
PAIRS = S // (2 * P)
NS, MH = 16, 16
HQ = MH * NS
HM = HQ // P
F = 1024
FC = F // P
GROUP = 4
PIECES = 6
STAGED = 3
NW = 3
DVE_OWN = 36
POOL_OWN = 8
EPS, EPS_OUT = 1e-5, 1e-6
RECUR_SCALE = (INNER // HEADS) ** -0.5
SCORE_SCALE = (D // MH) ** -0.5


def part(k):
    return (0, 1, 1, 0, 0, 1)[k]


class Count:

    def __init__(self, sem):
        self.sem, self.base, self.step, self.turn, self.per = sem, 0, 0, None, 0

    def enter(self, turn, per):
        self.base, self.step, self.turn, self.per = self.base + self.step, 0, turn, per

    def leave(self, turns):
        assert self.step == self.per, (self.sem, self.step, self.per)
        self.base, self.step, self.turn = self.base + self.per * turns, 0, None

    def now(self):
        return self.base + self.step + (0 if self.turn is None else self.turn * self.per)


class Pair:

    def __init__(self, b, i, lag=0):
        self.b, self.i = b + (i - lag) // PAIRS, (i - lag) % PAIRS
        self.n = self.b * PAIRS + self.i
        self.half = self.i // 2
        self.there = not isinstance(self.n, int) or 0 <= self.n < B * PAIRS

    def after(self, n):
        return not isinstance(self.n, int) or self.n >= n


class Unit:

    def __init__(self, b, h):
        self.b, self.h, self.n = b, h, b * HALVES + h

    def next(self):
        return Unit(self.b, 1) if self.h == 0 else Unit(self.b + 1, 0)

    def prev(self):
        if self.h == 0 and isinstance(self.b, int) and self.b == 0:
            return None
        return Unit(self.b, 0) if self.h == 1 else Unit(self.b - 1, 1)

    def before(self):
        return None if isinstance(self.b, int) and self.b == 0 else Unit(self.b - 1, self.h)


def build(nc, a, out):
    ctx = ExitStack()
    with ctx:
        def sb(name, shape, dt=F32):
            return ctx.enter_context(nc.sbuf_tensor(name, shape, dt))

        def sem(name):
            return ctx.enter_context(nc.semaphore(name))

        x1_dram = nc.dram_tensor("x1_scratch", (B, HALVES, P, TJ, D), F32).ap()
        qh_dram = nc.dram_tensor("qh_scratch", (B, P, HM, S), F32).ap()

        ident = sb("ident", [P, P])
        mask8 = sb("mask8", [P, 8])
        pair = sb("pair", [P, 2])
        sel = sb("sel", [40, CH, P], F32R)
        minus_half = sb("minus_half", [P, 8])
        VECTORS = (("bq_c", "L0_attn_bq", CH), ("bk_c", "L0_attn_bk", CH), ("bv_c", "L0_attn_bv", CH),
                   ("alpha_c", "L0_attn_alpha", CH), ("aug_c", "L0_attn_aug_param", CH),
                   ("dbq_c", "L0_ffn_d_bq", HM), ("dbk_c", "L0_ffn_d_bk", HM), ("cbq_c", "L0_ffn_c_bq", HM),
                   ("cbk_c", "L0_ffn_c_bk", HM), ("cbv_c", "L0_ffn_c_bv", HM), ("b2_c", "L0_ffn_e_b2", NS * KC))
        VROWS = sum(n for _, _, n in VECTORS)
        vec = sb("vec", [P, VROWS])
        col, at_row = {}, {}
        for short, name, n in VECTORS:
            at_row[name] = sum(at_row[m][1] for m in at_row), n
            col[short] = vec[:, at_row[name][0]:at_row[name][0] + n]
        bq_c, bk_c, bv_c, alpha_c, aug_c = (col[n] for n in ("bq_c", "bk_c", "bv_c", "alpha_c", "aug_c"))
        dbq_c, dbk_c, cbq_c, cbk_c, cbv_c = (col[n] for n in ("dbq_c", "dbk_c", "cbq_c", "cbk_c", "cbv_c"))
        b2t = col["b2_c"].rearrange("p (e k) -> p k e", k=KC)
        decay = sb("decay", [P, CH])
        keep2 = sb("keep2", [P, CH])
        bv2 = sb("bv2", [P, CH])
        aug_half = sb("aug_half", [P, CH])
        lns_r = sb("lns_r", [P, D])
        lnb_r = sb("lnb_r", [P, D])
        ones_parts = sb("ones_parts", [33, P], F32R)
        bo_parts = sb("bo_parts", [33, D], F32R)
        cbo_parts = sb("cbo_parts", [33, D], F32R)
        W_WORDS = KC * NW * INNER
        wx_at = nc.sbuf_base
        wx = sb("wx", [P, 2 * W_WORDS + 2 * KC * T], F32R)
        w_hi, w_lo = (wx[:, i * W_WORDS:(i + 1) * W_WORDS].rearrange("p (k w n) -> p k w n", k=KC, w=NW) for i in range(2))
        x_hi, x_lo = (wx[:, 2 * W_WORDS + i * KC * T:2 * W_WORDS + (i + 1) * KC * T].rearrange("p (k t) -> p k t", k=KC)
                      for i in range(2))
        wo = sb("wo", [P, CH, D])
        m_hi = sb("m_hi", [P, KC, HQ], F32R)
        m_lo = sb("m_lo", [P, KC, HQ], F32R)
        m_bias = sb("m_bias", [P, HM])
        cq_hi = sb("cq_hi", [P, KC, D], F32R)
        cq_lo = sb("cq_lo", [P, KC, D], F32R)
        x_pair = sb("x_pair", [P, 2, TJ, D])
        x, x_res = x_pair[:, 0], x_pair[:, 1]
        work = sb("work", [P, 4, 1024])
        xn = work[:, 0].rearrange("p (j d) -> p j d", j=TJ)
        qk, th, st = (work[:, 1 + i].rearrange("p (a t) -> p a t", a=2) for i in range(3))
        q = sb("q", [P, 2, CH, T])
        v = sb("v", [P, 2, CH, T])
        carry = sb("carry", [P, CH])
        o = sb("o", [P, TJ, D])
        x1 = sb("x1", [P, TJ, D])
        xn2 = sb("xn2", [P, HALVES * TJ, D])
        x2_hi = sb("x2_hi", [P, KC, T], F32R)
        x2_lo = sb("x2_lo", [P, KC, T], F32R)
        sc = sb("sc", [P, HM, S])
        pt = sb("pt", [P, 2, 2, HQ])
        qh = sb("qh", [P, HM, T])
        zt = sb("zt", [P, KC, MH, B, NS])
        stats = sb("stats", [P, TJ, 6])
        spread_var = sb("spread_var", [P, TJ])
        both = sb("both", [P, TJ, 2])
        apart = sb("apart", [P, TJ])
        mv1 = sb("mv1", [P, TJ, 2])
        mv2 = sb("mv2", [P, TJ, 2])
        mv3 = sb("mv3", [P, TJ, 2])
        mv4 = sb("mv4", [P, TJ, 2])
        r1 = sb("r1", [P, 2, TJ])
        r2 = sb("r2", [P, 2, TJ])
        r3 = sb("r3", [P, 2, TJ])
        r4 = sb("r4", [P, 2, TJ])
        smx = sb("smx", [P, TJ])
        sums = sb("sums", [P, TJ])
        rsum = sb("rsum", [P, TJ])
        att = sb("att", [P, TJ, HEADS])
        att_parts = sb("att_parts", [40, T], F32R)
        cmx = sb("cmx", [P, HM])
        cneg = sb("cneg", [P, HM])
        csum = sb("csum", [P, HM])
        crec = sb("crec", [P, HM])
        ring = sb("ring", [P, STAGED, GROUP, 1024])
        place = [ring[:, k] for k in range(STAGED)]
        over_wx = nc.alloc_sbuf_tensor_at("over_wx", [P, 2, GROUP, 1024], F32, offset=wx_at)
        place += [over_wx[:, i] for i in range(2)]
        place += [work[:]]
        w_raw = ring[:, 0, :, :].rearrange("p j n -> p (j n)")[:, 0:W_WORDS].rearrange("p (k w n) -> p k w n", k=KC, w=NW)
        bias_rows = ring[0:1, 0, 3, 0:2 * D].rearrange("p (a n) -> p a n", a=2)
        stage1 = ring[:, 1, :, :].rearrange("p j n -> p (j n)")
        dwq = stage1[:, 0:512].rearrange("p (k n) -> p k n", k=KC)
        dwk = stage1[:, 512:1024].rearrange("p (k n) -> p k n", k=KC)
        cwq = stage1[:, 1024:1536].rearrange("p (k n) -> p k n", k=KC)
        wkt = stage1[:, 1536:2048].rearrange("p (m n) -> p m n", m=HM)
        qbd = stage1[:, 2048:2304].rearrange("p (m n) -> p m n", m=HM)
        slot_in = stage1[0:NS, 2304:2560]
        vec_rows = stage1[0:VROWS, 3584:3584 + P]
        sel_raw = stage1[0:40, 3072:3584].rearrange("r (c a n) -> r c a n", c=CH, a=2)
        sqt = stage1[:, 2560:2592].rearrange("p (k n) -> p k n", k=KC)
        qht = stage1[:, 2592:2624].rearrange("p (m n) -> p m n", m=HM)

        late = q[:].rearrange("p a c t -> p (a c t)")
        d_wv = late[:, 0:512].rearrange("p (k n) -> p k n", k=KC)
        d_wo = late[:, 512:1024].rearrange("p (k n) -> p k n", k=KC)
        c_wk = late[:, 1024:1536].rearrange("p (k n) -> p k n", k=KC)
        c_wv = late[:, 1536:2048].rearrange("p (k n) -> p k n", k=KC)
        c_wo = late[:, 2048:2560].rearrange("p (k n) -> p k n", k=KC)
        dbv_r = late[0:64, 2560:2816]
        dbo_r = late[0:64, 2816:3072]
        slot_r = late[0:64, 3072:3328]
        eg_r = late[0:64, 3328:3584]
        eb_r = late[0:64, 3584:3840]
        late2 = v[:].rearrange("p a c t -> p (a c t)")
        b1t = late2[:, 0:256].rearrange("p (w e c) -> p w e c", w=2, e=NS)
        vo = late2[0:64, 256:512]
        vot = late2[:, 512:640].rearrange("p (k n) -> p k n", k=KC)
        os_ = late2[0:64, 640:896]
        hs = late2[0:64, 896:1152]
        ht = late2[:, 1152:1280].rearrange("p (k b e) -> p k b e", k=KC, b=B)
        o2t = late2[:, 1280:1408].rearrange("p (k b e) -> p k b e", k=KC, b=B)
        hcur = late2[:, 1408:1664].rearrange("p (k j n) -> p k j n", k=KC, j=GROUP)
        at = late2[:, 1664:2688].rearrange("p (c j n) -> p c j n", c=FC, j=GROUP)
        ug = late2[:, 2688:2944].rearrange("p (w c j b) -> p w c j b", w=2, c=FC, j=GROUP)
        eug = late2[:, 2944:3200].rearrange("p (w c j b) -> p w c j b", w=2, c=FC, j=GROUP)
        ysb = late2[:, 3200:3456]
        kv_t = late2[:, 3456:3712].rearrange("p (w m b s) -> p w m b s", w=2, m=HM, b=B)
        u_sb = sc[:].rearrange("p m s -> p (m s)")[:, 0:F]
        g_sb = sc[:].rearrange("p m s -> p (m s)")[:, F:2 * F]
        xn2_flat = xn2[:].rearrange("p j d -> p (j d)")
        kb = xn2_flat[:, 0:1024].rearrange("p (m b n) -> p m b n", m=HM, b=B)
        vb = xn2_flat[:, 1024:2048].rearrange("p (m b n) -> p m b n", m=HM, b=B)
        vp = x_pair[:].rearrange("p a j d -> p (a j d)").rearrange("p (m b n) -> p m b n", m=HM, b=B)
        qh_in = late.rearrange("p (h m s) -> p h m s", h=2 * HALVES, m=HM)[:, 0:HALVES]
        x1_in = late2.rearrange("p (h j d) -> p h j d", h=2 * HALVES, d=D)[:, 0:HALVES]
        prob = [sc[:].rearrange("p m s -> p (m s)")[:, i * 512:(i + 1) * 512] for i in range(4)]
        ptl = [pt[:].rearrange("p a t n -> p (a t n)")[:, i * 512:(i + 1) * 512] for i in range(2)]
        y = [o[:].rearrange("p j d -> p (j d)")[:, i * 512:(i + 1) * 512] for i in range(2)]
        res = [x1[:].rearrange("p j d -> p (j d)")[:, i * 512:(i + 1) * 512] for i in range(2)]
        tmx = sb("tmx", [P, 2, 32])
        tsum = sb("tsum", [P, 2, 32])
        trec = sb("trec", [P, 2, 32])
        mv5 = sb("mv5", [P, 2, 2, 2])
        st5 = sb("st5", [P, 2, 2, 6])
        r5 = sb("r5", [P, 2, 2, 2])

        bank = [ctx.enter_context(nc.psum_tensor(f"bank{i}", [P, 512], F32)) for i in range(8)]

        x_in, xr_in = sem("x_in"), sem("xr_in")
        vec_in, vec_turned, vec_made = sem("vec_in"), sem("vec_turned"), sem("vec_made")
        w_in = [sem("wq_in"), sem("wk_in"), sem("wv_in")]
        small_in, fold_in, cq_in, wo_in, late_in = sem("small_in"), sem("fold_in"), sem("cq_in"), sem("wo_in"), sem("late_in")
        x1_out, qh_out, res_out = sem("x1_out"), sem("qh_out"), [sem("res_out0"), sem("res_out1")]
        piece_in = [sem(f"piece_in{i}") for i in range(PIECES)]
        qh_back = [sem("qh_back0"), sem("qh_back1")]
        x1_back = [sem("x1_back0"), sem("x1_back1")]
        consts_made, sel_split, tanh_alpha, rates_made = sem("consts_made"), sem("sel_split"), sem("tanh_alpha"), sem("rates_made")
        w_hi_made, w_lo_made, rows_hi, rows_lo, rows_zero, rows_twice = (
            sem("w_hi_made"), sem("w_lo_made"), sem("rows_hi"), sem("rows_lo"), sem("rows_zero"), sem("rows_twice"))
        fold_pe, fold_dve, m_hi_made, m_lo_made = sem("fold_pe"), sem("fold_dve"), sem("m_hi_made"), sem("m_lo_made")
        ln1_stats, ln1_rate, xn_made = sem("ln1_stats"), sem("ln1_rate"), sem("xn_made")
        t1_done, x_hi_made, x_lo_made = sem("t1_done"), sem("x_hi_made"), sem("x_lo_made")
        q_done, k_done, v_done = sem("q_done"), sem("k_done"), sem("v_done")
        q_made, qk_made, v_made = sem("q_made"), sem("qk_made"), sem("v_made")
        sum_done, cen_made, exp_made, att_made = sem("sum_done"), sem("cen_made"), sem("exp_made"), sem("att_made")
        att_t_done, att_hi_made, att_lo_made, spread_done = sem("att_t_done"), sem("att_hi_made"), sem("att_lo_made"), sem("spread_done")
        th_made, scan_made, qst_made, inner_made = sem("th_made"), sem("scan_made"), sem("qst_made"), sem("inner_made")
        wo_done, ln2_stats, ln2_rate, ln2_made = sem("wo_done"), sem("ln2_stats"), sem("ln2_rate"), sem("ln2_made")
        gain_made, ln3_stats, ln3_rate, ln3_made = sem("gain_made"), sem("ln3_stats"), sem("ln3_rate"), sem("ln3_made")
        x1_made, ln4_stats, ln4_rate, xn2_made = sem("x1_made"), sem("ln4_stats"), sem("ln4_rate"), sem("xn2_made")
        t2_done, x2_hi_made, x2_lo_made = sem("t2_done"), sem("x2_hi_made"), sem("x2_lo_made")
        s_done, qp_done, s_made, qh_made = sem("s_done"), sem("qp_done"), sem("s_made"), sem("qh_made")
        smax_made, p_made, pn_made = sem("smax_made"), sem("p_made"), sem("pn_made")
        pt_done, pt_made, z_pair, zt_made = sem("pt_done"), sem("pt_made"), sem("z_pair"), sem("zt_made")
        val_made = sem("val_made")
        c_pe, c_dve, c_pool = sem("c_pe"), sem("c_dve"), sem("c_pool")
        pads_made, hcur_made, piece_used = sem("pads_made"), sem("hcur_made"), sem("piece_used")
        u_out, g_out = sem("u_out"), sem("g_out")
        ut_done, ug_made, eug_made, at_made = sem("ut_done"), sem("ug_made"), sem("eug_made"), sem("at_made")
        y_out, yt_done, slots_made = sem("y_out"), sem("yt_done"), sem("slots_made")
        kv_done, kv_made, vp_done, vp_made = sem("kv_done"), sem("kv_made"), sem("vp_done"), sem("vp_made")
        f_s_done, f_cen, f_exp, f_rec, f_norm = sem("f_s_done"), sem("f_cen"), sem("f_exp"), sem("f_rec"), sem("f_norm")
        f_t_done, f_pt, f_y_done, f_norm2, f_stats, f_rate, f_res = (
            sem("f_t_done"), sem("f_pt"), sem("f_y_done"), sem("f_norm2"), sem("f_stats"), sem("f_rate"), sem("f_res"))
        dve_own, pool_own = sem("dve_own"), sem("pool_own")

        x_dram = a["L0_attn_x"].rearrange("b (h j p) d -> b h p j d", h=HALVES, j=TJ)
        out_dram = out.rearrange("b (n j p) d -> b n p j d", j=2, p=P)

        def chunks(w):
            return w.rearrange("(k p) n -> p k n", p=P)

        def row(vec, n=P):
            return vec.rearrange("(o n) -> o n", o=1).to_broadcast([n, D])

        SMALL_LOADS = 4
        FOLD_LOADS = 3
        LATE_LOADS = 5 + 2 + B * 3 + 2

        block = ctx.enter_context(nc.Block())

        @block.sync
        def _(sp):
            sp.dma_start(x, x_dram[0, 0]).then_inc(x_in, 16)
            sp.dma_start(w_raw[:, :, 0, :], chunks(a["L0_attn_Wq"])).then_inc(w_in[0], 16)
            sp.dma_start(w_raw[:, :, 1, :], chunks(a["L0_attn_Wk"])).then_inc(w_in[1], 16)
            sp.dma_start(w_raw[:, :, 2, :], chunks(a["L0_attn_Wv"])).then_inc(w_in[2], 16)
            for _, name, n in VECTORS:
                vector = a[name]
                if len(vector.shape) == 2:
                    vector = vector.rearrange("h d -> (h d)")
                elif len(vector.shape) == 3:
                    vector = vector.rearrange("o h d -> (o h d)")
                first = at_row[name][0]
                sp.dma_start(vec_rows[first:first + n, :], vector.rearrange("(c p) -> c p", p=P)).then_inc(vec_in, 16)
            sp.wait_ge(xn_made, 1)
            sp.dma_start(x, x_dram[0, 1]).then_inc(x_in, 16)
            sp.dma_start(dwq, chunks(a["L0_ffn_d_Wq"])).then_inc(fold_in, 16)
            sp.dma_start(dwk, chunks(a["L0_ffn_d_Wk"])).then_inc(fold_in, 16)
            sp.dma_start(slot_in, a["L0_ffn_slot_query"].rearrange("o s d -> (o s) d")).then_inc(fold_in, 16)
            sp.dma_start(cwq, chunks(a["L0_ffn_c_Wq"])).then_inc(cq_in, 16)
            for i, name in enumerate(("L0_attn_bo", "L0_ffn_c_bo")):
                sp.dma_start(bias_rows[:, i], row(a[name], 1)).then_inc(small_in, 16)
            sp.dma_start(lns_r[:], row(a["L0_attn_ln_scale"])).then_inc(small_in, 16)
            sp.dma_start(lnb_r[:], row(a["L0_attn_ln_bias"])).then_inc(small_in, 16)
            sp.dma_start(wo[:], chunks(a["L0_attn_Wo"])).then_inc(wo_in, 16)
            sp.dma_start(x_res, x_dram[0, 0]).then_inc(xr_in, 16)

            def piece(g, k):
                w = a[("L0_ffn_e_W1", "L0_ffn_e_Wg", "L0_ffn_e_W2")[k // 2]]
                src = w.rearrange("(g j) (p r) n -> g p j (r n)", j=GROUP, p=P)[g]
                sp.dma_start(place[k], src[:, :, part(k) * 1024:(part(k) + 1) * 1024]).then_inc(piece_in[k], 16)

            def stored(u):
                sp.wait_ge(x1_made, u.n + 1)
                sp.dma_start(x1_dram[u.b, u.h], x1[:]).then_inc(x1_out, 16)
                if not (isinstance(u.n, int) and u.n == HALVES * B - 1):
                    w = u.next()
                    sp.dma_start(x_res, x_dram[w.b, w.h]).then_inc(xr_in, 16)

            def queries_stored(u):
                sp.wait_ge(qh_made, HM * (u.n + 1))
                sp.dma_start(qh_dram[u.b, :, :, u.h * T:(u.h + 1) * T], qh[:]).then_inc(qh_out, 16)

            def stage(b, first, last):
                for h in range(HALVES):
                    u = Unit(b, h)
                    if not last:
                        sp.wait_ge(xn_made, u.n + 2)
                        sp.dma_start(x, x_dram[b + 1, h]).then_inc(x_in, 16)
                    if first and h == 0:
                        sp.wait_ge(w_lo_made, NW + 1)
                        sp.wait_ge(m_lo_made, 1)
                        sp.wait_ge(sel_split, 1)
                        sp.wait_ge(rows_lo, 2)
                        piece(0, 0)
                    else:
                        if u.before():
                            queries_stored(u.before())
                        stored(u.prev())
                        if first:
                            piece(0, 1)

            stage(0, True, False)
            with sp.Fori(1, B - 1) as b:
                stage(b, False, False)
            piece(0, 2)
            stage(B - 1, False, True)
            sp.wait_ge(v_done, CH * HALVES * B)
            piece(0, 3)
            piece(0, 4)
            sp.wait_ge(inner_made, CH * HALVES * B)
            for dst, name in ((d_wv, "d_Wv"), (d_wo, "d_Wo"), (c_wk, "c_Wk"), (c_wv, "c_Wv"), (c_wo, "c_Wo")):
                sp.dma_start(dst, chunks(a["L0_ffn_" + name])).then_inc(late_in, 16)
            sp.dma_start(dbv_r, row(a["L0_ffn_d_bv"], 64)).then_inc(late_in, 16)
            sp.dma_start(dbo_r, row(a["L0_ffn_d_bo"], 64)).then_inc(late_in, 16)
            for b in range(B):
                rows = slice(b * NS, (b + 1) * NS)
                sp.dma_start(slot_r[rows, :], a["L0_ffn_slot_query"].rearrange("o s d -> (o s) d")).then_inc(late_in, 16)
                sp.dma_start(eg_r[rows, :], a["L0_ffn_e_ln_g"]).then_inc(late_in, 16)
                sp.dma_start(eb_r[rows, :], a["L0_ffn_e_ln_b"]).then_inc(late_in, 16)
            queries_stored(Unit(B - 1, 0))
            sp.wait_ge(wo_done, 2 * HALVES * B)
            sp.dma_start(b1t[:, 0], a["L0_ffn_e_b1"].rearrange("e (p c) -> p e c", p=P)).then_inc(late_in, 16)
            sp.dma_start(b1t[:, 1], a["L0_ffn_e_bg"].rearrange("e (p c) -> p e c", p=P)).then_inc(late_in, 16)
            piece(0, 5)
            stored(Unit(B - 1, 1))
            queries_stored(Unit(B - 1, 1))

            with sp.Fori(1, NS // GROUP) as g:
                for k in range(PIECES):
                    sp.wait_ge(piece_used, PIECES * (g - 1) + k + 1)
                    piece(g, k)

            sp.wait_ge(qh_out, 16 * HALVES * B)
            sp.wait_ge(x1_out, 16 * HALVES * B)
            sp.wait_ge(vp_done, 1)

            def queries(b, h):
                sp.dma_start(qh_in[:, h], qh_dram[b, :, :, h * T:(h + 1) * T]).then_inc(qh_back[h], 16)

            def stream(b, h):
                sp.dma_start(x1_in[:, h], x1_dram[b, h]).then_inc(x1_back[h], 16)

            def f_turn(b):
                for i in range(PAIRS):
                    p = Pair(b, i, 6)
                    if p.there:
                        sp.wait_ge(f_res, p.n + 1)
                        sp.dma_start(out_dram[p.b, p.i], res[p.i % 2].rearrange("p (j d) -> p j d", j=2)) \
                            .then_inc(res_out[p.i % 2], 16)
                        if i % 2 == 1 and not (isinstance(p.b, int) and p.b == B - 1):
                            stream(p.b + 1, p.half)
                    if i % 2 == 1 and not (isinstance(b, int) and b >= B - 1):
                        sp.wait_ge(f_s_done, PAIRS * b + i + 1)
                        queries(b + 1, i // 2)

            for h in range(HALVES):
                queries(0, h)
                stream(0, h)
            f_turn(0)
            f_turn(1)
            with sp.Fori(2, B - 1) as b:
                f_turn(b)
            f_turn(B - 1)
            f_turn(B)
            f_turn(B + 1)
            for s in range(2):
                sp.wait_ge(res_out[s], 16 * B * PAIRS // 2)

        @block.gpsimd
        def _(pool):
            own = Count(pool_own)

            def link(ins):
                own.step += 1
                ins.then_inc(pool_own, 1)
                pool.wait_ge(pool_own, own.now())

            nc.gpsimd.memset(minus_half[:], -0.5)
            nc.gpsimd.memset(mask8[:], 1.0)
            nc.gpsimd.memset(pair[:], 1.0)
            nc.gpsimd.memset(sel_raw, 0.0)
            link(nc.gpsimd.memset(ident[:], 0.0))
            nc.gpsimd.affine_select(out=ident[:], in_=ident[:], compare_op=ALU.not_equal, fill=1.0, base=0,
                                    pattern=[[-1, P]], channel_multiplier=1)
            for t, width, n in ((mask8, NS, 8), (pair, 64, 2)):
                link(nc.gpsimd.affine_select(out=t[:], in_=t[:], compare_op=ALU.is_ge, fill=0.0, base=0,
                                             pattern=[[-width, n]], channel_multiplier=1))
                link(nc.gpsimd.affine_select(out=t[:], in_=t[:], compare_op=ALU.is_ge, fill=0.0, base=width - 1,
                                             pattern=[[width, n]], channel_multiplier=-1))
            link(nc.gpsimd.affine_select(out=sel_raw, in_=sel_raw, compare_op=ALU.not_equal, fill=1.0, base=0,
                                         pattern=[[-2, CH], [-1, 2], [0, 64]], channel_multiplier=1))
            nc.gpsimd.affine_select(out=sel_raw, in_=sel_raw, compare_op=ALU.not_equal, fill=1.0, base=-32,
                                    pattern=[[-2, CH], [-1, 2], [0, 64]], channel_multiplier=1).then_inc(consts_made, 1)

            def rate(mv, r, n, ready, at, done):
                pool.wait_ge(ready, at)
                link(nc.gpsimd.tensor_tensor(r[:, 0, 0:n], mv[:, :, 1], minus_half[:, 0:n], ALU.pow))
                nc.gpsimd.tensor_tensor(r[:, 1, 0:n], mv[:, :, 0], r[:, 0, 0:n], ALU.mult).then_inc(done, 1)

            def q_state(u, c):
                pool.wait_ge(scan_made, CH * u.n + c + 1)
                nc.gpsimd.tensor_tensor(v[:, u.h, c], q[:, u.h, c], st[:, c % 2], ALU.mult).then_inc(qst_made, 1)

            def stage(b, first, last):
                for h in range(HALVES):
                    u = Unit(b, h)
                    p = u.prev()
                    if p:
                        rate(mv2, r2, TJ, ln2_stats, p.n + 1, ln2_rate)
                        rate(mv3, r3, TJ, ln3_stats, p.n + 1, ln3_rate)
                    if not last:
                        w = Unit(b + 1, h)
                        pool.wait_ge(xn_made, w.n)
                        rate(mv1, r1, TJ, ln1_stats, w.n + 1, ln1_rate)
                    for c in range(CH):
                        q_state(u, c)
                    if p:
                        rate(mv4, r4, TJ, ln4_stats, p.n + 1, ln4_rate)

            rate(mv1, r1, TJ, ln1_stats, 1, ln1_rate)
            pool.wait_ge(xn_made, 1)
            rate(mv1, r1, TJ, ln1_stats, 2, ln1_rate)
            pool.wait_ge(small_in, 16 * SMALL_LOADS)
            stage(0, True, False)
            with pool.Fori(1, B - 1) as b:
                own.enter(b - 1, POOL_OWN)
                stage(b, False, False)
                own.leave(B - 2)
            stage(B - 1, False, True)
            u = Unit(B - 1, 1)
            rate(mv2, r2, TJ, ln2_stats, u.n + 1, ln2_rate)
            rate(mv3, r3, TJ, ln3_stats, u.n + 1, ln3_rate)
            rate(mv4, r4, TJ, ln4_stats, u.n + 1, ln4_rate)

            pool.wait_ge(wo_done, 2 * HALVES * B)
            nc.gpsimd.memset(hcur, 0.0)
            nc.gpsimd.memset(at, 0.0).then_inc(pads_made, 1)
            pool.wait_ge(c_dve, 3)
            link(nc.gpsimd.tensor_scalar(r5[0:64, 0, 1, 0:1], mv5[0:64, 0, 0, 1:2], EPS, None, ALU.add))
            nc.gpsimd.tensor_tensor(r5[0:64, 0, 0, 0:1], r5[0:64, 0, 1, 0:1], minus_half[0:64, 0:1], ALU.pow).then_inc(c_pool, 1)

            def f_normalise(p):
                pool.wait_ge(f_rec, p.n + 1)
                pv = prob[p.i].rearrange("p (th s) -> p th s", s=NS)
                nc.gpsimd.tensor_tensor(pv, pv, trec[:, p.i % 2].unsqueeze(2).to_broadcast([P, 32, NS]), ALU.mult) \
                    .then_inc(f_norm, 1)

            def f_result(p):
                pool.wait_ge(f_norm2, p.n + 1)
                if p.i % 2 == 0:
                    pool.wait_ge(x1_back[p.half], (p.b + 1) * 16)
                if p.after(2):
                    pool.wait_ge(res_out[p.i % 2], (p.b * 2 + p.i // 2) * 16)
                nc.gpsimd.tensor_tensor(res[p.i % 2], y[p.i % 2],
                                        x1_in[:, p.half, 2 * (p.i % 2):2 * (p.i % 2) + 2].rearrange("p j d -> p (j d)"),
                                        ALU.add).then_inc(f_res, 1)

            def f_turn(b):
                for i in range(PAIRS):
                    made, rated, ended = Pair(b, i, 1), Pair(b, i, 4), Pair(b, i, 6)
                    if made.there:
                        f_normalise(made)
                    if rated.there:
                        if rated.after(2):
                            pool.wait_ge(f_norm2, rated.n - 1)
                        rate(mv5[:, rated.i % 2], r5[:, rated.i % 2], 2, f_stats, rated.n + 1, f_rate)
                    if ended.there:
                        f_result(ended)

            f_turn(0)
            f_turn(1)
            with pool.Fori(2, B) as b:
                own.enter(b - 2, PAIRS)
                f_turn(b)
                own.leave(B - 2)
            f_turn(B)
            f_turn(B + 1)

        @block.scalar
        def _(act):
            def ln1(u):
                act.wait_ge(ln1_rate, u.n + 1)
                if not (isinstance(u.n, int) and u.n == 0):
                    act.wait_ge(t1_done, KC * u.n)
                for j in range(TJ):
                    ins = nc.scalar.activation(xn[:, j], x[:, j], ACT.Identity,
                                               bias=r1[:, 1, j:j + 1], scale=r1[:, 0, j:j + 1])
                ins.then_inc(xn_made, 1)

            def ln3(u):
                act.wait_ge(ln3_rate, u.n + 1)
                for j in range(TJ):
                    ins = nc.scalar.activation(o[:, j], o[:, j], ACT.Identity,
                                               bias=r3[:, 1, j:j + 1], scale=r3[:, 0, j:j + 1])
                ins.then_inc(ln3_made, 1)

            def x_high(u):
                for k in range(KC):
                    act.wait_ge(t1_done, KC * u.n + k + 1)
                    if k == 0 and not (isinstance(u.n, int) and u.n == 0):
                        act.wait_ge(v_done, CH * u.n)
                    nc.scalar.copy(x_hi[:, k], bank[3 + k][:]).then_inc(x_hi_made, 1)

            def qv(u, c):
                act.wait_ge(q_done, CH * u.n + c + 1)
                if not (isinstance(u.b, int) and u.b == 0):
                    act.wait_ge(qst_made, CH * (u.n - 2) + c + 1)
                    act.wait_ge(inner_made, CH * (u.n - 2) + c + 1)
                nc.scalar.activation(q[:, u.h, c], bank[0][:], ACT.Identity, bias=bq_c[:, c:c + 1]).then_inc(q_made, 1)
                act.wait_ge(v_done, CH * u.n + c + 1)
                if not (isinstance(u.b, int) and u.b == 0):
                    act.wait_ge(wo_done, 2 * (u.n - 1))
                nc.scalar.activation(v[:, u.h, c], bank[2][:], ACT.Identity, bias=bv2[:, c:c + 1],
                                     scale=keep2[:, c:c + 1]).then_inc(v_made, 1)

            def tanh_q(u, c):
                act.wait_ge(q_made, CH * u.n + c + 1)
                if not (isinstance(u.n, int) and u.n == 0 and c < 2):
                    act.wait_ge(inner_made, CH * u.n + c - 1)
                nc.scalar.activation(th[:, c % 2], q[:, u.h, c], ACT.Tanh, scale=aug_half[:, c:c + 1]).then_inc(th_made, 1)

            def softmax_exp(u):
                act.wait_ge(cen_made, u.n + 1)
                nc.scalar.activation(att[:], att[:], ACT.Exp, scale=RECUR_SCALE).then_inc(exp_made, 1)

            def att_high(u):
                act.wait_ge(att_t_done, u.n + 1)
                if not (isinstance(u.n, int) and u.n == 0):
                    act.wait_ge(spread_done, CH * u.n)
                nc.scalar.copy(att_parts[0:HEADS, :], bank[5][0:HEADS, :]).then_inc(att_hi_made, 1)

            def x2_high(u):
                for k in range(KC):
                    act.wait_ge(t2_done, KC * u.n + k + 1)
                    if k == 0 and not (isinstance(u.n, int) and u.n == 0):
                        act.wait_ge(qp_done, HM * u.n)
                    nc.scalar.copy(x2_hi[:, k], bank[3 + k][:]).then_inc(x2_hi_made, 1)

            def scored(u, m):
                act.wait_ge(s_done, HM * u.n + m + 1)
                if m == 0 and u.h == 0 and not (isinstance(u.b, int) and u.b == 0):
                    act.wait_ge(pt_done, 4 * u.b)
                nc.scalar.activation(sc[:, m, u.h * T:(u.h + 1) * T], bank[3 + m][:], ACT.Identity,
                                     bias=m_bias[:, m:m + 1]).then_inc(s_made, 1)

            def queried(u, m):
                act.wait_ge(qp_done, HM * u.n + m + 1)
                if m == 0 and not (isinstance(u.n, int) and u.n == 0):
                    act.wait_ge(qh_out, 16 * u.n)
                nc.scalar.activation(qh[:, m], bank[3 + m][:], ACT.Identity, bias=cbq_c[:, m:m + 1]).then_inc(qh_made, 1)

            def slot_exp(b):
                act.wait_ge(smax_made, b + 1)
                for m in range(HM):
                    nc.scalar.activation(sc[:, m], sc[:, m], ACT.Exp, bias=cneg[:, m:m + 1], scale=SCORE_SCALE,
                                         accum_out=csum[:, m:m + 1]).then_inc(p_made, 1)

            def slot_weights(b, steps):
                for t in steps:
                    act.wait_ge(pt_done, 4 * b + t + 1)
                    if t >= 2:
                        act.wait_ge(z_pair, 4 * b + t - 1)
                    nc.scalar.copy(pt[:, t % 2], bank[3 + t % 2][:].rearrange("p (t n) -> p t n", t=2)) \
                        .then_inc(pt_made, 1)

            def slot_sums(b):
                act.wait_ge(z_pair, 4 * b + 4)
                for k in range(KC):
                    nc.scalar.copy(zt[:, k, :, b, :], bank[1 + k][:, 0:HQ].rearrange("p (h q) -> p h q", q=NS)) \
                        .then_inc(zt_made, 1)

            def ln4(u):
                act.wait_ge(ln4_rate, u.n + 1)
                if u.h == 0 and not (isinstance(u.b, int) and u.b == 0):
                    act.wait_ge(z_pair, 4 * u.b)
                for j in range(TJ):
                    ins = nc.scalar.activation(xn2[:, u.h * TJ + j], x1[:, j], ACT.Identity,
                                               bias=r4[:, 1, j:j + 1], scale=r4[:, 0, j:j + 1])
                ins.then_inc(xn2_made, 1)

            def stage(b, first, last):
                for h in range(HALVES):
                    u = Unit(b, h)
                    ahead = not (last and h == 1)
                    p = u.prev()
                    with_slots = h == 1 and not first
                    p2 = u.before()
                    if p2:
                        x2_high(p2)
                    softmax_exp(u)
                    if ahead:
                        qv(u.next(), 0)
                    att_high(u)
                    if p2:
                        scored(p2, 0)
                        scored(p2, 1)
                        queried(p2, 0)
                    tanh_q(u, 0)
                    tanh_q(u, 1)
                    if ahead:
                        qv(u.next(), 1)
                    if p:
                        ln3(p)
                    if not last:
                        ln1(Unit(b + 1, h))
                    if ahead:
                        qv(u.next(), 2)
                    if with_slots:
                        slot_exp(b - 1)
                    tanh_q(u, 2)
                    if p2:
                        queried(p2, 1)
                    tanh_q(u, 3)
                    if ahead:
                        qv(u.next(), 3)
                    if with_slots:
                        slot_weights(b - 1, range(4))
                        slot_sums(b - 1)
                    if not last:
                        x_high(Unit(b + 1, h))
                    if p:
                        ln4(p)

            def w_high(w):
                act.wait_ge(w_in[w], 16)
                nc.scalar.copy(w_hi[:, :, w], w_raw[:, :, w]).then_inc(w_hi_made, 1)

            w_high(0)
            ln1(Unit(0, 0))
            w_high(1)
            w_high(2)
            x_high(Unit(0, 0))
            act.wait_ge(vec_made, 1)
            nc.scalar.activation(alpha_c, alpha_c, ACT.Tanh, scale=0.5).then_inc(tanh_alpha, 1)
            act.wait_ge(consts_made, 1)
            nc.scalar.copy(sel[:], sel_raw.rearrange("r c a n -> r c (a n)")).then_inc(sel_split, 1)
            act.wait_ge(rates_made, 1)
            qv(Unit(0, 0), 0)
            ln1(Unit(0, 1))
            qv(Unit(0, 0), 1)
            act.wait_ge(rows_zero, 1)
            act.wait_ge(rows_twice, 1)
            nc.scalar.copy(bo_parts[0:1, :], bias_rows[:, 0])
            nc.scalar.copy(cbo_parts[0:1, :], bias_rows[:, 1]).then_inc(rows_hi, 1)
            act.wait_ge(cq_in, 16)
            nc.scalar.copy(cq_hi[:], cwq).then_inc(w_hi_made, 1)
            qv(Unit(0, 0), 2)
            act.wait_ge(fold_pe, 3)
            nc.scalar.copy(m_hi[:], bank[6][:].rearrange("p (k n) -> p k n", k=KC)).then_inc(m_hi_made, 1)
            qv(Unit(0, 0), 3)
            x_high(Unit(0, 1))
            stage(0, True, False)
            with act.Fori(1, B - 1) as b:
                stage(b, False, False)
            stage(B - 1, False, True)
            u = Unit(B - 1, 1)
            x2_high(u.prev())
            for m in range(HM):
                scored(u.prev(), m)
            for m in range(HM):
                queried(u.prev(), m)
            ln3(u)
            ln4(u)
            x2_high(u)
            for m in range(HM):
                scored(u, m)
            for m in range(HM):
                queried(u, m)
            slot_exp(B - 1)
            slot_weights(B - 1, range(4))
            slot_sums(B - 1)

            act.wait_ge(pads_made, 1)
            act.wait_ge(c_dve, 5)
            with act.Fori(0, NS // GROUP) as g:
                for k in range(KC):
                    ins = nc.scalar.copy(hcur[:, k, :, 0:B],
                                         ht[:, k, :, bass.ds(g * GROUP, GROUP)].rearrange("p b j -> p j b"))
                ins.then_inc(hcur_made, 1)
                act.wait_ge(piece_used, PIECES * g + 2)
                nc.scalar.copy(u_sb[:, 0:512], bank[0][:])
                nc.scalar.copy(u_sb[:, 512:1024], bank[1][:]).then_inc(u_out, 1)
                act.wait_ge(ug_made, g + 1)
                nc.scalar.activation(eug.rearrange("p w c j b -> p (w c j b)"),
                                     ug.rearrange("p w c j b -> p (w c j b)"), ACT.Exp, scale=-1.0).then_inc(eug_made, 1)
                act.wait_ge(piece_used, PIECES * g + 6)
                nc.scalar.copy(ysb, bank[0][:, 0:D]).then_inc(y_out, 1)

            act.wait_ge(vp_done, 1)
            for i in range(4):
                ins = nc.scalar.copy(vp[:, i // 2, (i % 2) * 2:(i % 2) * 2 + 2, :],
                                     bank[4 + i][:].rearrange("p (b n) -> p b n", b=2))
            ins.then_inc(vp_made, 1)

            def f_exponent(p):
                act.wait_ge(f_cen, p.n + 1)
                nc.scalar.activation(prob[p.i], prob[p.i], ACT.Exp, scale=SCORE_SCALE).then_inc(f_exp, 1)

            def f_transposed(p):
                act.wait_ge(f_t_done, p.n + 1)
                if p.after(2):
                    act.wait_ge(f_y_done, p.n - 1)
                nc.scalar.copy(ptl[p.i % 2], bank[2 + p.i % 2][:]).then_inc(f_pt, 1)

            def f_scale(p):
                act.wait_ge(f_rate, p.n + 1)
                if p.after(2):
                    act.wait_ge(f_res, p.n - 1)
                for j in range(2):
                    ins = nc.scalar.activation(y[p.i % 2][:, j * D:(j + 1) * D], bank[4 + p.i][:, j * D:(j + 1) * D],
                                               ACT.Identity, bias=r5[:, p.i % 2, 1, j:j + 1], scale=r5[:, p.i % 2, 0, j:j + 1])
                ins.then_inc(f_norm2, 1)

            def f_turn(b):
                for i in range(PAIRS):
                    scored, turned, rated = Pair(b, i), Pair(b, i, 2), Pair(b, i, 5)
                    if turned.there:
                        f_transposed(turned)
                    if scored.there:
                        f_exponent(scored)
                    if rated.there:
                        f_scale(rated)

            f_turn(0)
            f_turn(1)
            with act.Fori(2, B) as b:
                f_turn(b)
            f_turn(B)
            f_turn(B + 1)

        @block.vector
        def _(dve):
            own = Count(dve_own)

            def link(ins):
                own.step += 1
                ins.then_inc(dve_own, 1)
                dve.wait_ge(dve_own, own.now())

            def combine(st, both, apart, spread, mv, eps, done):
                nc.vector.tensor_tensor(both, st[:, :, 1:3], st[:, :, 4:6], ALU.add)
                link(nc.vector.tensor_tensor(apart, st[:, :, 1], st[:, :, 4], ALU.subtract))
                nc.vector.tensor_tensor(apart, apart, apart, ALU.mult)
                nc.vector.tensor_scalar(mv[:, :, 0], both[:, :, 0], -0.5, None, ALU.mult)
                link(nc.vector.tensor_scalar(spread, both[:, :, 1], 1.0 / D, eps, ALU.mult, ALU.add))
                nc.vector.scalar_tensor_tensor(out=mv[:, :, 1], in0=apart, scalar=0.25, in1=spread,
                                               op0=ALU.mult, op1=ALU.add).then_inc(done, 1)

            def moments(src, mv, eps, done):
                for j in range(TJ - 1):
                    nc.vector.bn_stats(stats[:, j], src(j))
                link(nc.vector.bn_stats(stats[:, TJ - 1], src(TJ - 1)))
                combine(stats[:], both[:], apart[:], spread_var[:], mv, eps, done)

            def ln1(u):
                dve.wait_ge(x_in, 16 * (u.n + 1))
                if not (isinstance(u.n, int) and u.n == 0):
                    dve.wait_ge(ln1_rate, u.n)
                moments(lambda j: x[:, j], mv1, EPS, ln1_stats)

            def x_low(u):
                for k in range(KC):
                    dve.wait_ge(x_hi_made, KC * u.n + k + 1)
                    nc.vector.tensor_tensor(x_lo[:, k], bank[3 + k][:], x_hi[:, k], ALU.subtract).then_inc(x_lo_made, 1)

            def q_times_k(u, c):
                dve.wait_ge(q_made, CH * u.n + c + 1)
                dve.wait_ge(k_done, CH * u.n + c + 1)
                if not (isinstance(u.n, int) and u.n == 0 and c < 2):
                    dve.wait_ge(sum_done, CH * u.n + c - 1)
                nc.vector.scalar_tensor_tensor(out=qk[:, c % 2], in0=bank[1][:], scalar=bk_c[:, c:c + 1],
                                               in1=q[:, u.h, c], op0=ALU.add, op1=ALU.mult).then_inc(qk_made, 1)

            def softmax(u):
                heads = bank[5][:, 0:TJ * HEADS].rearrange("p (j h) -> p j h", h=HEADS)
                dve.wait_ge(sum_done, CH * (u.n + 1))
                link(nc.vector.tensor_reduce(smx[:], heads, X, ALU.max))
                nc.vector.tensor_tensor(att[:], heads, smx[:].unsqueeze(2).to_broadcast([P, TJ, HEADS]), ALU.subtract) \
                    .then_inc(cen_made, 1)
                dve.wait_ge(exp_made, u.n + 1)
                link(nc.vector.tensor_reduce(sums[:], att[:], X, ALU.add))
                link(nc.vector.reciprocal(rsum[:], sums[:]))
                nc.vector.tensor_tensor(att[:], att[:], rsum[:].unsqueeze(2).to_broadcast([P, TJ, HEADS]), ALU.mult) \
                    .then_inc(att_made, 1)

            def att_low(u):
                dve.wait_ge(att_hi_made, u.n + 1)
                nc.vector.tensor_tensor(att_parts[32:32 + HEADS, :], bank[5][0:HEADS, :], att_parts[0:HEADS, :],
                                        ALU.subtract).then_inc(att_lo_made, 1)

            def recur(u, c):
                dve.wait_ge(spread_done, CH * u.n + c + 1)
                dve.wait_ge(v_made, CH * u.n + c + 1)
                nc.vector.tensor_tensor(v[:, u.h, c], bank[6 + c % 2][:], v[:, u.h, c], ALU.mult).then_inc(val_made, 1)
                dve.wait_ge(val_made, CH * u.n + c + 1)
                if not (isinstance(u.n, int) and u.n == 0 and c < 2):
                    dve.wait_ge(qst_made, CH * u.n + c - 1)
                initial = 0.0 if u.h == 0 else carry[:, c:c + 1]
                nc.vector.tensor_tensor_scan(st[:, c % 2], decay[:, c:c + 1].to_broadcast([P, T]), v[:, u.h, c],
                                             initial, ALU.mult, ALU.add).then_inc(scan_made, 1)
                if u.h == 0:
                    dve.wait_ge(scan_made, CH * u.n + c + 1)
                    link(nc.vector.tensor_copy(carry[:, c:c + 1], st[:, c % 2, T - 1:T]))

            def inner(u, c):
                dve.wait_ge(qst_made, CH * u.n + c + 1)
                dve.wait_ge(th_made, CH * u.n + c + 1)
                nc.vector.scalar_tensor_tensor(out=v[:, u.h, c], in0=th[:, c % 2], scalar=1.0, in1=v[:, u.h, c],
                                               op0=ALU.add, op1=ALU.add).then_inc(inner_made, 1)

            def ln2(u):
                dve.wait_ge(wo_done, 2 * u.n + 2)
                moments(lambda j: bank[6 + j // 2][:, (j % 2) * D:(j % 2 + 1) * D], mv2, 4 * EPS_OUT, ln2_stats)

            def ln2_gain(u):
                if not (isinstance(u.n, int) and u.n == 0):
                    dve.wait_ge(x1_made, u.n)
                for j in range(TJ):
                    ins = nc.vector.scalar_tensor_tensor(out=o[:, j], in0=bank[6 + j // 2][:, (j % 2) * D:(j % 2 + 1) * D],
                                                         scalar=mv2[:, j, 0:1], in1=lns_r[:], op0=ALU.add, op1=ALU.mult)
                ins.then_inc(ln2_made, 1)

            def ln2_shift(u):
                dve.wait_ge(ln2_made, u.n + 1)
                dve.wait_ge(ln2_rate, u.n + 1)
                for j in range(TJ):
                    ins = nc.vector.scalar_tensor_tensor(out=o[:, j], in0=o[:, j], scalar=r2[:, 0, j:j + 1], in1=lnb_r[:],
                                                         op0=ALU.mult, op1=ALU.add)
                ins.then_inc(gain_made, 1)

            def ln3(u):
                dve.wait_ge(gain_made, u.n + 1)
                moments(lambda j: o[:, j], mv3, EPS, ln3_stats)

            def ln4(u):
                dve.wait_ge(ln3_made, u.n + 1)
                dve.wait_ge(xr_in, 16 * (u.n + 1))
                if not (isinstance(u.n, int) and u.n == 0):
                    dve.wait_ge(x1_out, 16 * u.n)
                    dve.wait_ge(xn2_made, u.n)
                nc.vector.tensor_tensor(x1[:], o[:], x_res, ALU.add).then_inc(x1_made, 1)
                dve.wait_ge(x1_made, u.n + 1)
                moments(lambda j: x1[:, j], mv4, EPS, ln4_stats)

            def x2_low(u):
                for k in range(KC):
                    dve.wait_ge(x2_hi_made, KC * u.n + k + 1)
                    nc.vector.tensor_tensor(x2_lo[:, k], bank[3 + k][:], x2_hi[:, k], ALU.subtract).then_inc(x2_lo_made, 1)

            def slot_max(b):
                dve.wait_ge(s_made, HM * HALVES * (b + 1))
                link(nc.vector.tensor_reduce(cmx[:], sc[:], X, ALU.max))
                nc.vector.tensor_scalar(cneg[:], cmx[:], -SCORE_SCALE, None, ALU.mult).then_inc(smax_made, 1)

            def slot_norm(b):
                dve.wait_ge(p_made, HM * (b + 1))
                link(nc.vector.reciprocal(crec[:], csum[:]))
                for m in range(HM):
                    nc.vector.tensor_scalar(sc[:, m], sc[:, m], crec[:, m:m + 1], None, ALU.mult).then_inc(pn_made, 1)

            def stage(b, first, last):
                for h in range(HALVES):
                    u = Unit(b, h)
                    ahead = not (last and h == 1)
                    p = u.prev()
                    with_slots = h == 1 and not first
                    softmax(u)
                    if u.before():
                        x2_low(u.before())
                    if p:
                        ln2(p)
                    att_low(u)
                    if p:
                        dve.wait_ge(ln2_stats, p.n + 1)
                        ln2_gain(p)
                    if ahead:
                        q_times_k(u.next(), 0)
                    if p:
                        ln2_shift(p)
                        ln3(p)
                    if ahead:
                        q_times_k(u.next(), 1)
                    recur(u, 0)
                    if not last:
                        ln1(Unit(b + 1, h))
                    recur(u, 1)
                    if with_slots:
                        slot_max(b - 1)
                    inner(u, 0)
                    if ahead:
                        q_times_k(u.next(), 2)
                    recur(u, 2)
                    recur(u, 3)
                    inner(u, 1)
                    if with_slots:
                        slot_norm(b - 1)
                    inner(u, 2)
                    if ahead:
                        q_times_k(u.next(), 3)
                    inner(u, 3)
                    if p:
                        ln4(p)
                    if not last:
                        x_low(Unit(b + 1, h))

            nc.vector.memset(att_parts[:].bitcast(F32), 0.0)
            for t in (ones_parts, bo_parts, cbo_parts):
                ins = nc.vector.memset(t[:].bitcast(F32), 0.0)
            link(ins)
            nc.vector.memset(ones_parts[0:1, :].bitcast(F32), 1.0)
            nc.vector.memset(ones_parts[32:33, :].bitcast(F32), 1.0).then_inc(rows_zero, 1)
            def w_low(w):
                dve.wait_ge(w_hi_made, w + 1)
                nc.vector.tensor_tensor(w_lo[:, :, w], w_raw[:, :, w], w_hi[:, :, w], ALU.subtract).then_inc(w_lo_made, 1)

            ln1(Unit(0, 0))
            for w in range(NW):
                w_low(w)
            x_low(Unit(0, 0))
            dve.wait_ge(vec_turned, 1)
            nc.vector.tensor_copy(vec[:], bank[7][:, 0:VROWS]).then_inc(vec_made, 1)
            dve.wait_ge(tanh_alpha, 1)
            nc.vector.tensor_scalar(decay[:], alpha_c, 0.5, 0.5, ALU.mult, ALU.add)
            link(nc.vector.tensor_scalar(keep2[:], alpha_c, -1.0, 1.0, ALU.mult, ALU.add))
            nc.vector.tensor_tensor(bv2[:], bv_c, keep2[:], ALU.mult)
            nc.vector.tensor_scalar(aug_half[:], aug_c, 0.5, None, ALU.mult).then_inc(rates_made, 1)
            q_times_k(Unit(0, 0), 0)
            ln1(Unit(0, 1))
            dve.wait_ge(fold_pe, 1)
            nc.vector.tensor_copy(sqt, bank[7][:, 0:KC * NS].rearrange("p (k n) -> p k n", k=KC))
            nc.vector.tensor_copy(wkt, bank[6][:].rearrange("p (m n) -> p m n", m=HM)).then_inc(fold_dve, 1)
            dve.wait_ge(small_in, 16 * SMALL_LOADS)
            nc.vector.tensor_scalar(bias_rows[:, 0], bias_rows[:, 0], 2.0, None, ALU.mult).then_inc(rows_twice, 1)
            q_times_k(Unit(0, 0), 1)
            dve.wait_ge(fold_pe, 2)
            for m in range(HM):
                link(nc.vector.tensor_scalar(qht[:, m], bank[7][:, m * NS:(m + 1) * NS], dbq_c[:, m:m + 1], None, ALU.add))
                ins = nc.vector.tensor_tensor(qbd[:, m].rearrange("p (h s) -> p h s", s=NS),
                                              qht[:, m].unsqueeze(1).to_broadcast([P, 8, NS]),
                                              mask8[:].unsqueeze(2).to_broadcast([P, 8, NS]), ALU.mult)
            ins.then_inc(fold_dve, 1)
            dve.wait_ge(rows_hi, 1)
            nc.vector.tensor_tensor(bo_parts[32:33, :], bias_rows[:, 0], bo_parts[0:1, :], ALU.subtract).then_inc(rows_lo, 1)
            nc.vector.tensor_tensor(cbo_parts[32:33, :], bias_rows[:, 1], cbo_parts[0:1, :], ALU.subtract).then_inc(rows_lo, 1)
            dve.wait_ge(w_hi_made, NW + 1)
            nc.vector.tensor_tensor(cq_lo[:], cwq, cq_hi[:], ALU.subtract).then_inc(w_lo_made, 1)
            q_times_k(Unit(0, 0), 2)
            dve.wait_ge(m_hi_made, 1)
            nc.vector.tensor_copy(m_bias[:], bank[7][:, 0:HM])
            nc.vector.tensor_tensor(m_lo[:], bank[6][:].rearrange("p (k n) -> p k n", k=KC), m_hi[:], ALU.subtract) \
                .then_inc(m_lo_made, 1)
            q_times_k(Unit(0, 0), 3)
            x_low(Unit(0, 1))

            stage(0, True, False)
            with dve.Fori(1, B - 1) as b:
                own.enter(b - 1, DVE_OWN)
                stage(b, False, False)
                own.leave(B - 2)
            stage(B - 1, False, True)
            u = Unit(B - 1, 1)
            x2_low(u.prev())
            ln2(u)
            dve.wait_ge(ln2_stats, u.n + 1)
            ln2_gain(u)
            ln2_shift(u)
            ln3(u)
            ln4(u)
            x2_low(u)
            slot_max(B - 1)
            slot_norm(B - 1)

            dve.wait_ge(late_in, 16 * LATE_LOADS)
            dve.wait_ge(c_pe, 1)
            nc.vector.tensor_tensor(vo, bank[0][0:64, 0:D], dbv_r, ALU.add).then_inc(c_dve, 1)
            dve.wait_ge(c_pe, 2)
            nc.vector.tensor_copy(vot.rearrange("p k n -> p (k n)"), bank[1][:, 0:128]).then_inc(c_dve, 1)
            dve.wait_ge(c_pe, 3)
            link(nc.vector.tensor_tensor(os_, bank[2][0:64, 0:D], dbo_r, ALU.add))
            link(nc.vector.tensor_tensor(os_, os_, slot_r, ALU.add))
            link(nc.vector.bn_stats(st5[0:64, 0, 0], os_))
            nc.vector.bn_aggr(mv5[0:64, 0, 0], st5[0:64, 0, 0]).then_inc(c_dve, 1)
            dve.wait_ge(c_pool, 1)
            link(nc.vector.tensor_scalar(hs, os_, mv5[0:64, 0, 0, 0:1], r5[0:64, 0, 0, 0:1], ALU.subtract, ALU.mult))
            link(nc.vector.tensor_tensor(hs, hs, eg_r, ALU.mult))
            nc.vector.tensor_tensor(hs, hs, eb_r, ALU.add).then_inc(c_dve, 1)
            dve.wait_ge(c_pe, 4)
            nc.vector.tensor_copy(ht.rearrange("p k b e -> p (k b e)"), bank[3][:, 128:256])
            nc.vector.tensor_tensor(o2t, bank[3][:, 0:128].rearrange("p (k b e) -> p k b e", k=KC, b=B),
                                    b2t.unsqueeze(2).to_broadcast([P, KC, B, NS]), ALU.add).then_inc(c_dve, 1)

            with dve.Fori(0, NS // GROUP) as g:
                own.enter(g, 3)
                dve.wait_ge(piece_used, PIECES * g + 4)
                nc.vector.tensor_copy(g_sb[:, 0:512], bank[2][:])
                nc.vector.tensor_copy(g_sb[:, 512:1024], bank[3][:]).then_inc(g_out, 1)
                for w in range(2):
                    dve.wait_ge(ut_done, 2 * g + w + 1)
                    for i in range(2):
                        bias = b1t[:, w, bass.ds(g * GROUP, GROUP), 4 * i:4 * i + 4].rearrange("p j c -> p c j") \
                            .unsqueeze(3).to_broadcast([P, 4, GROUP, B])
                        ins = nc.vector.tensor_tensor(
                            ug[:, w, 4 * i:4 * i + 4],
                            bank[4 + 2 * w + i][:].rearrange("p (c j n) -> p c j n", c=4, j=GROUP)[:, :, :, 0:B],
                            bias, ALU.add)
                ins.then_inc(ug_made, 1)
                dve.wait_ge(eug_made, g + 1)
                flat = "p w c j b -> p (w c j b)"
                link(nc.vector.tensor_scalar(eug.rearrange(flat), eug.rearrange(flat), 1.0, None, ALU.add))
                link(nc.vector.reciprocal(eug.rearrange(flat), eug.rearrange(flat)))
                link(nc.vector.tensor_tensor(ug.rearrange(flat), ug.rearrange(flat), eug.rearrange(flat), ALU.mult))
                nc.vector.tensor_tensor(at[:, :, :, 0:B], ug[:, 0], ug[:, 1], ALU.mult).then_inc(at_made, 1)
                dve.wait_ge(yt_done, g + 1)
                for k in range(KC):
                    part = o2t[:, k, :, bass.ds(g * GROUP, GROUP)].rearrange("p b j -> p j b")
                    ins = nc.vector.tensor_tensor(
                        part, part, bank[6][:, k * P:(k + 1) * P].rearrange("p (j n) -> p j n", j=GROUP)[:, :, 0:B], ALU.add)
                ins.then_inc(slots_made, 1)
                own.leave(NS // GROUP)

            dve.wait_ge(kv_done, 1)
            for w, bias in ((0, cbk_c), (1, cbv_c)):
                for m in range(HM):
                    link(nc.vector.tensor_scalar(kv_t[:, w, m].rearrange("p b s -> p (b s)"),
                                                 bank[2 + w][:, m * 64:(m + 1) * 64], bias[:, m:m + 1], None, ALU.add))
                    dst = (kb, vb)[w]
                    for b in range(B):
                        ins = nc.vector.tensor_tensor(
                            dst[:, m, b].rearrange("p (h s) -> p h s", s=NS),
                            kv_t[:, w, m, b].unsqueeze(1).to_broadcast([P, 8, NS]),
                            mask8[:].unsqueeze(2).to_broadcast([P, 8, NS]), ALU.mult)
            ins.then_inc(kv_made, 1)

            def f_centre(p):
                scores = bank[p.i % 2][:].rearrange("p (th s) -> p th s", s=NS)
                dve.wait_ge(f_s_done, p.n + 1)
                if p.after(4):
                    dve.wait_ge(f_t_done, p.n - 3)
                link(nc.vector.tensor_reduce(tmx[:, p.i % 2], scores, X, ALU.max))
                nc.vector.tensor_tensor(prob[p.i].rearrange("p (th s) -> p th s", s=NS), scores,
                                        tmx[:, p.i % 2].unsqueeze(2).to_broadcast([P, 32, NS]), ALU.subtract).then_inc(f_cen, 1)

            def f_sums(p):
                dve.wait_ge(f_exp, p.n + 1)
                if p.after(2):
                    dve.wait_ge(f_norm, p.n - 1)
                link(nc.vector.tensor_reduce(tsum[:, p.i % 2], prob[p.i].rearrange("p (th s) -> p th s", s=NS), X, ALU.add))
                nc.vector.reciprocal(trec[:, p.i % 2], tsum[:, p.i % 2]).then_inc(f_rec, 1)

            def f_moments(p):
                dve.wait_ge(f_y_done, p.n + 1)
                nc.vector.bn_stats(st5[:, p.i % 2, 0], bank[4 + p.i][:, 0:D])
                link(nc.vector.bn_stats(st5[:, p.i % 2, 1], bank[4 + p.i][:, D:2 * D]))
                if p.after(2):
                    dve.wait_ge(f_rate, p.n - 1)
                combine(st5[:, p.i % 2], both[:, 0:2], apart[:, 0:2], spread_var[:, 0:2], mv5[:, p.i % 2], EPS, f_stats)

            def f_turn(b):
                for i in range(PAIRS):
                    scored, exponent, valued = Pair(b, i), Pair(b, i, 1), Pair(b, i, 4)
                    if scored.there:
                        f_centre(scored)
                    if exponent.there:
                        f_sums(exponent)
                    if valued.there:
                        f_moments(valued)

            f_turn(0)
            f_turn(1)
            with dve.Fori(2, B) as b:
                own.enter(b - 2, 5 * PAIRS)
                f_turn(b)
                own.leave(B - 2)
            f_turn(B)

        @block.tensor
        def _(pe):
            def t1(u, prev):
                pe.wait_ge(xn_made, u.n + 1)
                for k in range(KC):
                    prev(k)
                    for j in range(TJ):
                        ins = nc.tensor.transpose(bank[3 + k][:, j * P:(j + 1) * P], xn[:, j, k * P:(k + 1) * P], ident[:])
                    ins.then_inc(t1_done, 1)

            def project(dst, w_h, w_l, x_h, x_l, cols, done):
                n = 0
                for k in range(KC):
                    for w, r in ((w_h, x_h), (w_h, x_l), (w_l, x_h)):
                        ins = nc.tensor.matmul(dst, w[:, k, cols], r[:, k], start=n == 0, stop=n == 3 * KC - 1)
                        n += 1
                ins.then_inc(done, 1)

            def qkv(u, c, free):
                if c == 0:
                    pe.wait_ge(x_hi_made, KC * (u.n + 1))
                    pe.wait_ge(x_lo_made, KC * (u.n + 1))
                cols = slice(c * P, (c + 1) * P)
                for w, done in ((0, q_done), (1, k_done), (2, v_done)):
                    if c:
                        pe.wait_ge((q_made, qk_made, v_made)[w], CH * u.n + c)
                    else:
                        free(w)
                    project(bank[w][:], w_hi[:, :, w], w_lo[:, :, w], x_hi, x_lo, cols, done)

            def head_sums(u, c):
                pe.wait_ge(qk_made, CH * u.n + c + 1)
                if c == 0 and not (isinstance(u.n, int) and u.n == 0):
                    pe.wait_ge(att_lo_made, u.n)
                for j in range(TJ):
                    at_ = j * HEADS + 2 * c
                    ins = nc.tensor.matmul(bank[5][:, at_:at_ + 2], qk[:, c % 2, j * P:(j + 1) * P], pair[:],
                                           start=True, stop=True)
                ins.then_inc(sum_done, 1)

            def att_transpose(u):
                pe.wait_ge(att_made, u.n + 1)
                for j in range(TJ):
                    ins = nc.tensor.transpose(bank[5][0:HEADS, j * P:(j + 1) * P], att[:, j], ident[:])
                ins.then_inc(att_t_done, 1)

            def spread(u, c):
                if c == 0:
                    pe.wait_ge(att_lo_made, u.n + 1)
                if c >= 2:
                    pe.wait_ge(val_made, CH * u.n + c - 1)
                elif not (isinstance(u.n, int) and u.n == 0):
                    pe.wait_ge(ln2_made, u.n)
                nc.tensor.matmul(bank[6 + c % 2][:], sel[:, c], att_parts[:], start=True, stop=True) \
                    .then_inc(spread_done, 1)

            def out_project(u):
                pe.wait_ge(inner_made, CH * (u.n + 1))
                for p in range(2):
                    for j in (2 * p, 2 * p + 1):
                        for c in range(CH):
                            ins = nc.tensor.matmul(bank[6 + p][:, (j % 2) * D:(j % 2 + 1) * D],
                                                   v[:, u.h, c, j * P:(j + 1) * P], wo[:, c], start=c == 0, stop=False)
                        ins = nc.tensor.matmul(bank[6 + p][:, (j % 2) * D:(j % 2 + 1) * D], ones_parts[:], bo_parts[:],
                                               start=False, stop=True)
                    ins.then_inc(wo_done, 1)

            def t2(u, prev):
                pe.wait_ge(xn2_made, u.n + 1)
                for k in range(KC):
                    prev(k)
                    for j in range(TJ):
                        ins = nc.tensor.transpose(bank[3 + k][:, j * P:(j + 1) * P],
                                                  xn2[:, u.h * TJ + j, k * P:(k + 1) * P], ident[:])
                    ins.then_inc(t2_done, 1)

            def slot_scores(u, m):
                if m == 0:
                    pe.wait_ge(x2_hi_made, KC * (u.n + 1))
                    pe.wait_ge(x2_lo_made, KC * (u.n + 1))
                project(bank[3 + m][:], m_hi, m_lo, x2_hi, x2_lo, slice(m * P, (m + 1) * P), s_done)

            def queries(u, m):
                pe.wait_ge(s_made, HM * u.n + m + 1)
                project(bank[3 + m][:], cq_hi, cq_lo, x2_hi, x2_lo, slice(m * P, (m + 1) * P), qp_done)

            def slots(b, ahead):
                pe.wait_ge(pn_made, HM * (b + 1))

                def turn(t):
                    if t < 2:
                        pe.wait_ge(qh_made, HM * (HALVES * b + 1) + t + 1)
                    else:
                        pe.wait_ge(pt_made, 4 * b + t - 1)
                    for i in range(2):
                        for m in range(HM):
                            ins = nc.tensor.transpose(bank[3 + t % 2][:, i * HQ + m * P:i * HQ + (m + 1) * P],
                                                      sc[:, m, (2 * t + i) * P:(2 * t + i + 1) * P], ident[:])
                    ins.then_inc(pt_done, 1)

                def add(t):
                    pe.wait_ge(pt_made, 4 * b + t + 1)
                    if t == 0:
                        if ahead:
                            pe.wait_ge(qk_made, CH * (HALVES * b + 5))
                            pe.wait_ge(v_made, CH * (HALVES * b + 5))
                        elif b == B - 1:
                            pe.wait_ge(zt_made, KC * b)
                        else:
                            pe.wait_ge(qk_made, CH * HALVES * B)
                            pe.wait_ge(v_made, CH * HALVES * B)
                    for i in range(2):
                        for k in range(KC):
                            ins = nc.tensor.matmul(bank[1 + k][:, 0:HQ], xn2[:, 2 * t + i, k * P:(k + 1) * P], pt[:, t % 2, i],
                                                   start=t + i == 0, stop=t == 3 and i == 1)
                    ins.then_inc(z_pair, 1)

                turn(0)
                for t in range(4):
                    if t < 3:
                        turn(t + 1)
                    add(t)

            def stage(b, first, last):
                for h in range(HALVES):
                    u = Unit(b, h)
                    ahead = not (last and h == 1)
                    w = u.next()
                    head_sums(u, 3)

                    def banks012(i):
                        pe.wait_ge((q_made, qk_made, v_made)[i], CH * w.n)

                    p2, with_slots = u.before(), h == 1 and not first

                    def before_t1(k):
                        if with_slots:
                            pe.wait_ge(pt_made, 4 * b - 1 + k)
                        elif p2:
                            pe.wait_ge(qh_made, HM * p2.n + k + 1)
                        else:
                            pe.wait_ge(x_lo_made, KC * (u.n + 1) + k + 1)

                    def before_t2(k):
                        if not last:
                            pe.wait_ge(x_lo_made, KC * (u.n + 2) + k + 1)
                        elif with_slots:
                            pe.wait_ge(pt_made, 4 * b - 1 + k)
                        else:
                            pe.wait_ge(qh_made, HM * p2.n + k + 1)

                    if ahead:
                        qkv(w, 0, banks012)
                    att_transpose(u)
                    if p2:
                        slot_scores(p2, 0)
                        slot_scores(p2, 1)
                        queries(p2, 0)
                    spread(u, 0)
                    spread(u, 1)
                    if ahead:
                        qkv(w, 1, banks012)
                        head_sums(w, 0)
                    if ahead:
                        qkv(w, 2, banks012)
                        head_sums(w, 1)
                    spread(u, 2)
                    spread(u, 3)
                    if p2:
                        queries(p2, 1)
                    if ahead:
                        qkv(w, 3, banks012)
                        head_sums(w, 2)
                    if with_slots:
                        slots(b - 1, ahead)
                    if not last:
                        t1(Unit(b + 1, h), before_t1)
                    out_project(u)
                    if u.prev():
                        t2(u.prev(), before_t2)

            def fold_transposes():
                pe.wait_ge(fold_in, 16 * FOLD_LOADS)
                pe.wait_ge(vec_made, 1)
                for k in range(KC):
                    nc.tensor.transpose(bank[7][:, k * NS:(k + 1) * NS], slot_in[:, k * P:(k + 1) * P], ident[0:NS, 0:NS])
                for m in range(HM):
                    for k in range(KC):
                        ins = nc.tensor.transpose(bank[6][:, m * D + k * P:m * D + (k + 1) * P],
                                                  dwk[:, k, m * P:(m + 1) * P], ident[:])
                ins.then_inc(fold_pe, 1)

            def fold_queries():
                pe.wait_ge(fold_dve, 1)
                for m in range(HM):
                    for k in range(KC):
                        ins = nc.tensor.matmul(bank[7][:, m * NS:(m + 1) * NS], dwq[:, k, m * P:(m + 1) * P], sqt[:, k],
                                               start=k == 0, stop=k == KC - 1)
                ins.then_inc(fold_pe, 1)

            def fold_weights():
                pe.wait_ge(fold_dve, 2)
                for k in range(KC):
                    for m in range(HM):
                        nc.tensor.matmul(bank[6][:, k * HQ + m * P:k * HQ + (m + 1) * P], wkt[:, m, k * P:(k + 1) * P],
                                         qbd[:, m], start=True, stop=True)
                for m in range(HM):
                    ins = nc.tensor.matmul(bank[7][:, m:m + 1], qbd[:, m], dbk_c[:, m:m + 1], start=True, stop=True)
                ins.then_inc(fold_pe, 1)

            pe.wait_ge(consts_made, 1)
            t1(Unit(0, 0), lambda k: None)
            pe.wait_ge(vec_in, 16 * len(VECTORS))
            nc.tensor.transpose(bank[7][:, 0:VROWS], vec_rows, ident[0:VROWS, 0:VROWS]).then_inc(vec_turned, 1)
            pe.wait_ge(w_lo_made, NW)
            for c in range(CH):
                qkv(Unit(0, 0), c, lambda i: None)
                if c:
                    head_sums(Unit(0, 0), c - 1)
                    (fold_transposes, fold_queries, fold_weights)[c - 1]()
            t1(Unit(0, 1), lambda k: pe.wait_ge(x_lo_made, k + 1))
            pe.wait_ge(m_lo_made, 1)
            pe.wait_ge(rows_lo, 2)
            pe.wait_ge(w_lo_made, NW + 1)
            pe.wait_ge(sel_split, 1)
            pe.wait_ge(wo_in, 16)

            stage(0, True, False)
            with pe.Fori(1, B - 1) as b:
                stage(b, False, False)
            stage(B - 1, False, True)
            for u in (Unit(B - 1, 0), Unit(B - 1, 1)):
                if u.h == 1:
                    t2(u, lambda k: pe.wait_ge(qh_made, HM * u.prev().n + k + 1))
                for m in range(HM):
                    slot_scores(u, m)
                for m in range(HM):
                    queries(u, m)
            slots(B - 1, False)

            pe.wait_ge(late_in, 16 * LATE_LOADS)
            pe.wait_ge(zt_made, KC * B)
            pe.wait_ge(qh_made, HM * HALVES * B)
            for h in range(MH):
                for k in range(KC):
                    ins = nc.tensor.matmul(bank[0][0:64, h * 16:(h + 1) * 16], zt[:, k, h].rearrange("p b q -> p (b q)"),
                                           d_wv[:, k, h * 16:(h + 1) * 16], start=k == 0, stop=k == KC - 1)
            ins.then_inc(c_pe, 1)
            pe.wait_ge(c_dve, 1)
            for k in range(KC):
                ins = nc.tensor.transpose(bank[1][:, k * 64:(k + 1) * 64], vo[:, k * P:(k + 1) * P], ident[0:64, 0:64])
            ins.then_inc(c_pe, 1)
            pe.wait_ge(c_dve, 2)
            for k in range(KC):
                ins = nc.tensor.matmul(bank[2][0:64, 0:D], vot[:, k], d_wo[:, k], start=k == 0, stop=k == KC - 1)
            ins.then_inc(c_pe, 1)
            pe.wait_ge(c_dve, 4)
            for k in range(KC):
                nc.tensor.transpose(bank[3][:, k * 64:(k + 1) * 64], os_[:, k * P:(k + 1) * P], ident[0:64, 0:64])
            hs_v = hs.rearrange("p (n k) -> p k n", k=KC)
            for k in range(KC):
                ins = nc.tensor.transpose(bank[3][:, 128 + k * 64:128 + (k + 1) * 64], hs_v[:, k], ident[0:64, 0:64])
            ins.then_inc(c_pe, 1)

            with pe.Fori(0, NS // GROUP) as g:
                pe.wait_ge(hcur_made, g + 1)
                for k in range(PIECES):
                    if k == 4:
                        for w, out_s, src in ((0, u_out, u_sb), (1, g_out, g_sb)):
                            pe.wait_ge(out_s, g + 1)
                            view = src.rearrange("p (n c) -> p c n", c=FC)
                            for c in range(FC):
                                ins = nc.tensor.transpose(bank[4 + 2 * w + c // 4][:, (c % 4) * P:(c % 4 + 1) * P], view[:, c], ident[:])
                            ins.then_inc(ut_done, 1)
                        pe.wait_ge(at_made, g + 1)
                    pe.wait_ge(piece_in[k], (g + 1) * 16)
                    if k < 4:
                        for n in range(2):
                            for j in range(GROUP):
                                ins = nc.tensor.matmul(bank[2 * (k // 2) + n][32 * j:32 * j + 32, :], hcur[:, part(k), j],
                                                       place[k][:, j, n * 512:(n + 1) * 512],
                                                       start=k % 2 == 0, stop=k % 2 == 1, tile_position=(0, 32 * j))
                    else:
                        for c in range(4):
                            for j in range(GROUP):
                                cc = part(k) * 4 + c
                                ins = nc.tensor.matmul(bank[0][32 * j:32 * j + 32, 0:D], at[:, cc, j],
                                                       place[k][:, j, c * D:(c + 1) * D],
                                                       start=k == 4 and c == 0, stop=k == 5 and c == 3, tile_position=(0, 32 * j))
                    ins.then_inc(piece_used, 1)
                pe.wait_ge(y_out, g + 1)
                for k in range(KC):
                    ins = nc.tensor.transpose(bank[6][:, k * P:(k + 1) * P], ysb[:, k * P:(k + 1) * P], ident[:])
                ins.then_inc(yt_done, 1)

            pe.wait_ge(slots_made, NS // GROUP)
            for w, weight in ((0, c_wk), (1, c_wv)):
                for m in range(HM):
                    for k in range(KC):
                        ins = nc.tensor.matmul(bank[2 + w][:, m * 64:(m + 1) * 64], weight[:, k, m * P:(m + 1) * P],
                                               o2t[:, k].rearrange("p b e -> p (b e)"), start=k == 0, stop=k == KC - 1)
            ins.then_inc(kv_done, 1)
            pe.wait_ge(kv_made, 1)
            for m in range(HM):
                for b in range(B):
                    i = m * B + b
                    ins = nc.tensor.matmul(bank[4 + i // 2][:, (i % 2) * D:(i % 2 + 1) * D], vb[:, m, b], c_wo[:, m],
                                           start=True, stop=True)
            ins.then_inc(vp_done, 1)

            def f_scores(p):
                if p.i % 2 == 0:
                    pe.wait_ge(qh_back[p.half], (p.b + 1) * 16)
                if p.after(2):
                    pe.wait_ge(f_cen, p.n - 1)
                for j in range(2):
                    tile = 2 * (p.i % 2) + j
                    for m in range(HM):
                        ins = nc.tensor.matmul(bank[p.i % 2][:, j * HQ + m * P:j * HQ + (m + 1) * P],
                                               qh_in[:, p.half, m, tile * P:(tile + 1) * P],
                                               kb[:, m, p.b], start=True, stop=True)
                ins.then_inc(f_s_done, 1)

            def f_transpose(p):
                pe.wait_ge(f_norm, p.n + 1)
                if p.after(2):
                    pe.wait_ge(f_pt, p.n - 1)
                for j in range(4):
                    ins = nc.tensor.transpose(bank[2 + p.i % 2][:, j * P:(j + 1) * P], prob[p.i][:, j * P:(j + 1) * P], ident[:])
                ins.then_inc(f_t_done, 1)

            def f_values(p):
                pe.wait_ge(f_pt, p.n + 1)
                if p.after(4):
                    pe.wait_ge(f_norm2, p.n - 3)
                for j in range(2):
                    for m in range(HM):
                        nc.tensor.matmul(bank[4 + p.i][:, j * D:(j + 1) * D],
                                         ptl[p.i % 2][:, (2 * j + m) * P:(2 * j + m + 1) * P],
                                         vp[:, m, p.b], start=m == 0, stop=False)
                    ins = nc.tensor.matmul(bank[4 + p.i][:, j * D:(j + 1) * D], ones_parts[:], cbo_parts[:],
                                           start=False, stop=True)
                ins.then_inc(f_y_done, 1)

            def f_turn(b):
                for i in range(PAIRS):
                    here, turned, valued = Pair(b, i), Pair(b, i, 2), Pair(b, i, 3)
                    if here.there:
                        f_scores(here)
                    if turned.there:
                        f_transpose(turned)
                    if valued.there:
                        f_values(valued)

            pe.wait_ge(vp_made, 1)
            f_turn(0)
            f_turn(1)
            with pe.Fori(2, B) as b:
                f_turn(b)
            f_turn(B)


def kernel(**inputs):
    import numpy as np
    import concourse.bacc as bacc
    from concourse.bass_utils import run_bass_kernel_spmd

    nc = bacc.Bacc("TRN2", target_bir_lowering=False, num_devices=1)
    arrays, aps = {}, {}
    for name, value in inputs.items():
        value = np.ascontiguousarray(value)
        arrays[name] = value
        aps[name] = nc.dram_tensor(name, value.shape, mybir.dt.from_np(value.dtype), kind="ExternalInput").ap()
    result = nc.dram_tensor("result", (B, S, D), F32, kind="ExternalOutput").ap()
    build(nc, aps, result)
    r = run_bass_kernel_spmd(nc, [arrays], core_ids=[0])
    return r.results[0]["result"]
```

```python
import concourse.bass as bass
from concourse import mybir
from contextlib import ExitStack

F32 = mybir.dt.float32
F32R = mybir.dt.float32r
ALU = mybir.AluOpType
ACT = mybir.ActivationFunctionType
X = mybir.AxisListType.X

P = 128
B, S, D = 4, 1024, 256
KC = D // P
INNER, HEADS = 512, 8
CH = INNER // P
T = 512
TJ = T // P
HALVES = S // T
PAIRS = S // (2 * P)
NS, MH = 16, 16
HQ = MH * NS
HM = HQ // P
F = 1024
FC = F // P
GROUP = 4
PIECES = 6
STAGED = 3
NW = 3
DVE_OWN = 38
POOL_OWN = 8
EPS, EPS_OUT = 1e-5, 1e-6
RECUR_SCALE = (INNER // HEADS) ** -0.5
SCORE_SCALE = (D // MH) ** -0.5


def part(k):
    return (0, 1, 1, 0, 0, 1)[k]


class Count:

    def __init__(self, sem):
        self.sem, self.base, self.step, self.turn, self.per = sem, 0, 0, None, 0

    def enter(self, turn, per):
        self.base, self.step, self.turn, self.per = self.base + self.step, 0, turn, per

    def leave(self, turns):
        assert self.step == self.per, (self.sem, self.step, self.per)
        self.base, self.step, self.turn = self.base + self.per * turns, 0, None

    def now(self):
        return self.base + self.step + (0 if self.turn is None else self.turn * self.per)


class Pair:

    def __init__(self, b, i, lag=0):
        self.b, self.i = b + (i - lag) // PAIRS, (i - lag) % PAIRS
        self.n = self.b * PAIRS + self.i
        self.half = self.i // 2
        self.nh = self.b * 2 + self.half
        self.there = not isinstance(self.n, int) or 0 <= self.n < B * PAIRS

    def after(self, n):
        return not isinstance(self.n, int) or self.n >= n


class Unit:

    def __init__(self, b, h):
        self.b, self.h, self.n = b, h, b * HALVES + h

    def next(self):
        return Unit(self.b, 1) if self.h == 0 else Unit(self.b + 1, 0)

    def prev(self):
        if self.h == 0 and isinstance(self.b, int) and self.b == 0:
            return None
        return Unit(self.b, 0) if self.h == 1 else Unit(self.b - 1, 1)

    def before(self):
        return None if isinstance(self.b, int) and self.b == 0 else Unit(self.b - 1, self.h)


def build(nc, a, out):
    ctx = ExitStack()
    with ctx:
        def sb(name, shape, dt=F32):
            return ctx.enter_context(nc.sbuf_tensor(name, shape, dt))

        def sem(name):
            return ctx.enter_context(nc.semaphore(name))

        x1_dram = nc.dram_tensor("x1_scratch", (B, HALVES, P, TJ, D), F32).ap()
        qh_dram = nc.dram_tensor("qh_scratch", (B, P, HM, S), F32).ap()

        ident = sb("ident", [P, P])
        mask8 = sb("mask8", [P, 8])
        pair = sb("pair", [P, 2])
        sel = sb("sel", [40, CH, P], F32R)
        minus_half = sb("minus_half", [P, 8])
        VECTORS = (("bq_c", "L0_attn_bq", CH), ("bk_c", "L0_attn_bk", CH), ("bv_c", "L0_attn_bv", CH),
                   ("alpha_c", "L0_attn_alpha", CH), ("aug_c", "L0_attn_aug_param", CH),
                   ("dbq_c", "L0_ffn_d_bq", HM), ("dbk_c", "L0_ffn_d_bk", HM), ("cbq_c", "L0_ffn_c_bq", HM),
                   ("cbk_c", "L0_ffn_c_bk", HM), ("cbv_c", "L0_ffn_c_bv", HM), ("b2_c", "L0_ffn_e_b2", NS * KC))
        VROWS = sum(n for _, _, n in VECTORS)
        vec = sb("vec", [P, VROWS])
        col, at_row = {}, {}
        for short, name, n in VECTORS:
            at_row[name] = sum(at_row[m][1] for m in at_row), n
            col[short] = vec[:, at_row[name][0]:at_row[name][0] + n]
        bq_c, bk_c, bv_c, alpha_c, aug_c = (col[n] for n in ("bq_c", "bk_c", "bv_c", "alpha_c", "aug_c"))
        dbq_c, dbk_c, cbq_c, cbk_c, cbv_c = (col[n] for n in ("dbq_c", "dbk_c", "cbq_c", "cbk_c", "cbv_c"))
        b2t = col["b2_c"].rearrange("p (e k) -> p k e", k=KC)
        decay = sb("decay", [P, CH])
        keep2 = sb("keep2", [P, CH])
        bv2 = sb("bv2", [P, CH])
        aug_half = sb("aug_half", [P, CH])
        lns_r = sb("lns_r", [P, D])
        lnb_r = sb("lnb_r", [P, D])
        ones_parts = sb("ones_parts", [33, P], F32R)
        bo_parts = sb("bo_parts", [33, D], F32R)
        cbo_parts = sb("cbo_parts", [33, D], F32R)
        W_WORDS = KC * NW * INNER
        wx_at = -(-nc.sbuf_base // 32) * 32
        wx = sb("wx", [P, 2 * W_WORDS + 2 * KC * T], F32R)
        w_hi, w_lo = (wx[:, i * W_WORDS:(i + 1) * W_WORDS].rearrange("p (k w n) -> p k w n", k=KC, w=NW) for i in range(2))
        x_hi, x_lo = (wx[:, 2 * W_WORDS + i * KC * T:2 * W_WORDS + (i + 1) * KC * T].rearrange("p (k t) -> p k t", k=KC)
                      for i in range(2))
        wo = sb("wo", [P, CH, D])
        pj_at = -(-nc.sbuf_base // 32) * 32
        pj = sb("pj", [P, 4 * KC * D + 2 * KC * T], F32R)
        m_hi, m_lo, cq_hi, cq_lo = (pj[:, i * KC * D:(i + 1) * KC * D].rearrange("p (k n) -> p k n", k=KC)
                                    for i in range(4))
        x2_hi, x2_lo = (pj[:, 4 * KC * D + i * KC * T:4 * KC * D + (i + 1) * KC * T].rearrange("p (k t) -> p k t", k=KC)
                        for i in range(2))
        m_bias = sb("m_bias", [P, HM])
        stream4 = sb("stream4", [P, 4, TJ, D])
        x, x_res, o, x1 = (stream4[:, i] for i in range(4))
        work = sb("work", [P, 4, 1024])
        xn = work[:, 0].rearrange("p (j d) -> p j d", j=TJ)
        qk, th, st = (work[:, 1 + i].rearrange("p (a t) -> p a t", a=2) for i in range(3))
        q = sb("q", [P, 2, CH, T])
        v = sb("v", [P, 2, CH, T])
        carry = sb("carry", [P, CH])
        xn2 = sb("xn2", [P, HALVES * TJ, D])
        slot_work = sb("slot_work", [P, HM * S + 4 * HQ + HM * T])
        sc = slot_work[:, 0:HM * S].rearrange("p (m s) -> p m s", m=HM)
        pt = slot_work[:, HM * S:HM * S + 4 * HQ].rearrange("p (a t n) -> p a t n", a=2, t=2)
        qh = slot_work[:, HM * S + 4 * HQ:].rearrange("p (m t) -> p m t", m=HM)
        zt = sb("zt", [P, KC, MH, B, NS])
        stats = sb("stats", [P, TJ, 6])
        spread_var = sb("spread_var", [P, TJ])
        both = sb("both", [P, TJ, 2])
        apart = sb("apart", [P, TJ])
        mv1 = sb("mv1", [P, TJ, 2])
        mv2 = sb("mv2", [P, TJ, 2])
        mv3 = sb("mv3", [P, TJ, 2])
        mv4 = sb("mv4", [P, TJ, 2])
        r1 = sb("r1", [P, 2, TJ])
        r2 = sb("r2", [P, 2, TJ])
        r3 = sb("r3", [P, 2, TJ])
        r4 = sb("r4", [P, 2, TJ])
        smx = sb("smx", [P, TJ])
        sums = sb("sums", [P, TJ])
        rsum = sb("rsum", [P, TJ])
        att = sb("att", [P, TJ, HEADS])
        att_parts = sb("att_parts", [40, T], F32R)
        cmx = sb("cmx", [P, HM])
        cneg = sb("cneg", [P, HM])
        csum = sb("csum", [P, HM])
        crec = sb("crec", [P, HM])
        ring = sb("ring", [P, STAGED, GROUP, 1024])
        place = [ring[:, k] for k in range(STAGED)]
        over_wx = nc.alloc_sbuf_tensor_at("over_wx", [P, 2, GROUP, 1024], F32, offset=wx_at)
        place += [over_wx[:, i] for i in range(2)]
        place += [work[:]]
        over_pj = nc.alloc_sbuf_tensor_at("over_pj", [P, GROUP, 1024], F32, offset=pj_at)
        place += [stream4[:].rearrange("p a j d -> p a (j d)"), over_pj[:],
                  slot_work[:].rearrange("p (j n) -> p j n", j=GROUP)]
        w_raw = ring[:, 0, :, :].rearrange("p j n -> p (j n)")[:, 0:W_WORDS].rearrange("p (k w n) -> p k w n", k=KC, w=NW)
        bias_rows = ring[0:1, 0, 3, 0:2 * D].rearrange("p (a n) -> p a n", a=2)
        stage1 = ring[:, 1, :, :].rearrange("p j n -> p (j n)")
        dwq = stage1[:, 0:512].rearrange("p (k n) -> p k n", k=KC)
        dwk = stage1[:, 512:1024].rearrange("p (k n) -> p k n", k=KC)
        cwq = stage1[:, 1024:1536].rearrange("p (k n) -> p k n", k=KC)
        wkt = stage1[:, 1536:2048].rearrange("p (m n) -> p m n", m=HM)
        qbd = stage1[:, 2048:2304].rearrange("p (m n) -> p m n", m=HM)
        slot_in = stage1[0:NS, 2304:2560]
        vec_rows = stage1[0:VROWS, 3584:3584 + P]
        sel_raw = stage1[0:40, 3072:3584].rearrange("r (c a n) -> r c a n", c=CH, a=2)
        sqt = stage1[:, 2560:2592].rearrange("p (k n) -> p k n", k=KC)
        qht = stage1[:, 2592:2624].rearrange("p (m n) -> p m n", m=HM)

        late = q[:].rearrange("p a c t -> p (a c t)")
        xn3 = late[:, 0:2048].rearrange("p (j d) -> p j d", d=D)
        d_wv, d_wo, c_wk, c_wv = (late[:, 2048 + i * 512:2048 + (i + 1) * 512].rearrange("p (k n) -> p k n", k=KC)
                                  for i in range(4))
        xn2_flat = xn2[:].rearrange("p j d -> p (j d)")
        c_wo = xn2_flat[:, 0:512].rearrange("p (k n) -> p k n", k=KC)
        dbv_r, dbo_r, slot_r, eg_r, eb_r = (xn2_flat[0:64, 512 + i * D:512 + (i + 1) * D] for i in range(5))
        late2 = v[:].rearrange("p a c t -> p (a c t)")
        b1t = late2[:, 0:256].rearrange("p (w e c) -> p w e c", w=2, e=NS)
        vo = late2[0:64, 256:512]
        vot = late2[:, 512:640].rearrange("p (k n) -> p k n", k=KC)
        os_ = late2[0:64, 640:896]
        hs = late2[0:64, 896:1152]
        ht = late2[:, 1152:1280].rearrange("p (k b e) -> p k b e", k=KC, b=B)
        o2t = late2[:, 1280:1408].rearrange("p (k b e) -> p k b e", k=KC, b=B)
        hcur = late2[:, 1408:1664].rearrange("p (k j n) -> p k j n", k=KC, j=GROUP)
        at = late2[:, 1664:2688].rearrange("p (c j n) -> p c j n", c=FC, j=GROUP)
        ug = late2[:, 2688:2944].rearrange("p (w c j b) -> p w c j b", w=2, c=FC, j=GROUP)
        eug = late2[:, 2944:3200].rearrange("p (w c j b) -> p w c j b", w=2, c=FC, j=GROUP)
        ysb = late2[:, 3200:3456]
        kv_t = late2[:, 3456:3712].rearrange("p (w m b s) -> p w m b s", w=2, m=HM, b=B)
        u_sb, g_sb = late[:, 0:F], late[:, F:2 * F]
        kb = late[:, 0:1024].rearrange("p (m b n) -> p m b n", m=HM, b=B)
        vb = late[:, 1024:2048].rearrange("p (m b n) -> p m b n", m=HM, b=B)
        vp = stream4[:, 0:2].rearrange("p a j d -> p (a j d)").rearrange("p (m b n) -> p m b n", m=HM, b=B)
        tail_in = over_pj[:].rearrange("p j n -> p (j n)")
        qh_in = tail_in[:, 0:2048].rearrange("p (h m s) -> p h m s", h=HALVES, m=HM)
        x1_in = tail_in[:, 2048:4096].rearrange("p (h j d) -> p h j d", h=HALVES, d=D)
        prob = [sc.rearrange("p m s -> p (m s)")[:, i * 512:(i + 1) * 512] for i in range(4)]
        ptl = [pt.rearrange("p a t n -> p (a t n)")[:, i * 512:(i + 1) * 512] for i in range(2)]
        y = [o.rearrange("p j d -> p (j d)")[:, i * 512:(i + 1) * 512] for i in range(2)]
        res = [x1.rearrange("p j d -> p (j d)")[:, i * 512:(i + 1) * 512] for i in range(2)]
        tmx = sb("tmx", [P, 2, 32])
        tsum = sb("tsum", [P, 2, 32])
        trec = sb("trec", [P, 2, 32])
        mv5 = sb("mv5", [P, 2, 4, 2])
        st5 = sb("st5", [P, 2, 4, 6])
        r5 = sb("r5", [P, 2, 2, 4])

        bank = [ctx.enter_context(nc.psum_tensor(f"bank{i}", [P, 512], F32)) for i in range(8)]

        x_in, xr_in = sem("x_in"), sem("xr_in")
        vec_in, vec_turned, vec_made = sem("vec_in"), sem("vec_turned"), sem("vec_made")
        w_in = [sem("wq_in"), sem("wk_in"), sem("wv_in")]
        small_in, fold_in, cq_in, wo_in, late_in = sem("small_in"), sem("fold_in"), sem("cq_in"), sem("wo_in"), sem("late_in")
        x1_out, qh_out, res_out = sem("x1_out"), sem("qh_out"), [sem("res_out0"), sem("res_out1")]
        piece_in = [sem(f"piece_in{i}") for i in range(len(place))]
        qh_back = [sem("qh_back0"), sem("qh_back1")]
        x1_back = [sem("x1_back0"), sem("x1_back1")]
        consts_made, sel_split, tanh_alpha, rates_made = sem("consts_made"), sem("sel_split"), sem("tanh_alpha"), sem("rates_made")
        w_hi_made, w_lo_made, rows_hi, rows_lo, rows_zero, rows_twice = (
            sem("w_hi_made"), sem("w_lo_made"), sem("rows_hi"), sem("rows_lo"), sem("rows_zero"), sem("rows_twice"))
        fold_pe, fold_dve, m_hi_made, m_lo_made = sem("fold_pe"), sem("fold_dve"), sem("m_hi_made"), sem("m_lo_made")
        ln1_stats, ln1_rate, xn_made = sem("ln1_stats"), sem("ln1_rate"), sem("xn_made")
        t1_done, x_hi_made, x_lo_made = sem("t1_done"), sem("x_hi_made"), sem("x_lo_made")
        q_done, k_done, v_done = sem("q_done"), sem("k_done"), sem("v_done")
        q_made, qk_made, v_made = sem("q_made"), sem("qk_made"), sem("v_made")
        sum_done, cen_made, exp_made, att_made = sem("sum_done"), sem("cen_made"), sem("exp_made"), sem("att_made")
        att_t_done, att_hi_made, att_lo_made, spread_done = sem("att_t_done"), sem("att_hi_made"), sem("att_lo_made"), sem("spread_done")
        th_made, scan_made, qst_made, inner_made = sem("th_made"), sem("scan_made"), sem("qst_made"), sem("inner_made")
        wo_done, ln2_stats, ln2_rate, ln2_made = sem("wo_done"), sem("ln2_stats"), sem("ln2_rate"), sem("ln2_made")
        gain_made, ln3_stats, ln3_rate, ln3_made = sem("gain_made"), sem("ln3_stats"), sem("ln3_rate"), sem("ln3_made")
        x1_made, ln4_stats, ln4_rate, xn2_made = sem("x1_made"), sem("ln4_stats"), sem("ln4_rate"), sem("xn2_made")
        t2_done, x2_hi_made, x2_lo_made = sem("t2_done"), sem("x2_hi_made"), sem("x2_lo_made")
        s_done, qp_done, s_made, qh_made = sem("s_done"), sem("qp_done"), sem("s_made"), sem("qh_made")
        smax_made, p_made, pn_made = sem("smax_made"), sem("p_made"), sem("pn_made")
        pt_done, pt_made, z_pair, zt_made = sem("pt_done"), sem("pt_made"), sem("z_pair"), sem("zt_made")
        val_made = sem("val_made")
        c_pe, c_dve, c_pool = sem("c_pe"), sem("c_dve"), sem("c_pool")
        pads_made, hcur_made, piece_used = sem("pads_made"), sem("hcur_made"), sem("piece_used")
        u_out, g_out = sem("u_out"), sem("g_out")
        ut_done, ug_made, eug_made, at_made = sem("ut_done"), sem("ug_made"), sem("eug_made"), sem("at_made")
        y_out, yt_done, slots_made = sem("y_out"), sem("yt_done"), sem("slots_made")
        kv_done, kv_made, vp_done, vp_made = sem("kv_done"), sem("kv_made"), sem("vp_done"), sem("vp_made")
        f_s_done, f_cen, f_exp, f_rec, f_norm = sem("f_s_done"), sem("f_cen"), sem("f_exp"), sem("f_rec"), sem("f_norm")
        f_t_done, f_pt, f_y_done, f_norm2, f_stats, f_rate, f_res = (
            sem("f_t_done"), sem("f_pt"), sem("f_y_done"), sem("f_norm2"), sem("f_stats"), sem("f_rate"), sem("f_res"))
        dve_own, pool_own = sem("dve_own"), sem("pool_own")

        x_dram = a["L0_attn_x"].rearrange("b (h j p) d -> b h p j d", h=HALVES, j=TJ)
        out_dram = out.rearrange("b (n j p) d -> b n p j d", j=2, p=P)

        def normed(b):
            return xn3 if isinstance(b, int) and b == B - 1 else xn2

        def is_last(u):
            return isinstance(u.n, int) and u.n == HALVES * B - 1

        def layer_out(u):
            return x if is_last(u) else o

        def out_banks(u):
            return (bank[5], bank[2]) if is_last(u) else (bank[6], bank[7])

        def spread_banks(u):
            return (bank[1], bank[2]) if is_last(u) else (bank[6], bank[7])

        def chunks(w):
            return w.rearrange("(k p) n -> p k n", p=P)

        def row(vec, n=P):
            return vec.rearrange("(o n) -> o n", o=1).to_broadcast([n, D])

        SMALL_LOADS = 4
        FOLD_LOADS = 3
        LATE_LOADS = 5 + 2 + B * 3 + 2

        block = ctx.enter_context(nc.Block())

        @block.sync
        def _(sp):
            sp.dma_start(x, x_dram[0, 0]).then_inc(x_in, 16)
            sp.dma_start(w_raw[:, :, 0, :], chunks(a["L0_attn_Wq"])).then_inc(w_in[0], 16)
            sp.dma_start(w_raw[:, :, 1, :], chunks(a["L0_attn_Wk"])).then_inc(w_in[1], 16)
            sp.dma_start(w_raw[:, :, 2, :], chunks(a["L0_attn_Wv"])).then_inc(w_in[2], 16)
            for _, name, n in VECTORS:
                vector = a[name]
                if len(vector.shape) == 2:
                    vector = vector.rearrange("h d -> (h d)")
                elif len(vector.shape) == 3:
                    vector = vector.rearrange("o h d -> (o h d)")
                first = at_row[name][0]
                sp.dma_start(vec_rows[first:first + n, :], vector.rearrange("(c p) -> c p", p=P)).then_inc(vec_in, 16)
            sp.wait_ge(xn_made, 1)
            sp.dma_start(x, x_dram[0, 1]).then_inc(x_in, 16)
            sp.dma_start(dwq, chunks(a["L0_ffn_d_Wq"])).then_inc(fold_in, 16)
            sp.dma_start(dwk, chunks(a["L0_ffn_d_Wk"])).then_inc(fold_in, 16)
            sp.dma_start(slot_in, a["L0_ffn_slot_query"].rearrange("o s d -> (o s) d")).then_inc(fold_in, 16)
            sp.dma_start(cwq, chunks(a["L0_ffn_c_Wq"])).then_inc(cq_in, 16)
            for i, name in enumerate(("L0_attn_bo", "L0_ffn_c_bo")):
                sp.dma_start(bias_rows[:, i], row(a[name], 1)).then_inc(small_in, 16)
            sp.dma_start(lns_r[:], row(a["L0_attn_ln_scale"])).then_inc(small_in, 16)
            sp.dma_start(lnb_r[:], row(a["L0_attn_ln_bias"])).then_inc(small_in, 16)
            sp.dma_start(wo[:], chunks(a["L0_attn_Wo"])).then_inc(wo_in, 16)
            sp.dma_start(x_res, x_dram[0, 0]).then_inc(xr_in, 16)

            def piece(g, k):
                w = a[("L0_ffn_e_W1", "L0_ffn_e_Wg", "L0_ffn_e_W2")[k // 2]]
                src = w.rearrange("(g j) (p r) n -> g p j (r n)", j=GROUP, p=P)[g]
                n = PIECES * g + k
                sp.dma_start(place[n % len(place)], src[:, :, part(k) * 1024:(part(k) + 1) * 1024]) \
                    .then_inc(piece_in[n % len(place)], 16)

            def stored(u):
                sp.wait_ge(x1_made, u.n + 1)
                sp.dma_start(x1_dram[u.b, u.h], x1).then_inc(x1_out, 16)
                if not (isinstance(u.n, int) and u.n == HALVES * B - 1):
                    w = u.next()
                    sp.dma_start(x_res, x_dram[w.b, w.h]).then_inc(xr_in, 16)

            def queries_stored(u):
                sp.wait_ge(qh_made, HM * (u.n + 1))
                sp.dma_start(qh_dram[u.b, :, :, u.h * T:(u.h + 1) * T], qh).then_inc(qh_out, 16)

            def stage(b, first, last):
                for h in range(HALVES - last):
                    u = Unit(b, h)
                    if not last:
                        sp.wait_ge(xn_made, u.n + 2)
                        sp.dma_start(x, x_dram[b + 1, h]).then_inc(x_in, 16)
                    if first and h == 0:
                        sp.wait_ge(w_lo_made, NW + 1)
                        sp.wait_ge(m_lo_made, 1)
                        sp.wait_ge(sel_split, 1)
                        sp.wait_ge(rows_lo, 2)
                        piece(0, 0)
                    else:
                        if u.before():
                            queries_stored(u.before())
                        stored(u.prev())
                        if first:
                            piece(0, 1)

            stage(0, True, False)
            with sp.Fori(1, B - 1) as b:
                stage(b, False, False)
            piece(0, 2)
            stage(B - 1, False, True)
            u = Unit(B - 1, 1)
            queries_stored(u.before())
            sp.wait_ge(v_done, CH * HALVES * B)
            piece(0, 3)
            piece(0, 4)
            sp.wait_ge(inner_made, CH * HALVES * B)
            for dst, name in ((d_wv, "d_Wv"), (d_wo, "d_Wo"), (c_wk, "c_Wk"), (c_wv, "c_Wv")):
                sp.dma_start(dst, chunks(a["L0_ffn_" + name])).then_inc(late_in, 16)
            sp.wait_ge(wo_done, 2 * HALVES * B)
            sp.dma_start(b1t[:, 0], a["L0_ffn_e_b1"].rearrange("e (p c) -> p e c", p=P)).then_inc(late_in, 16)
            sp.dma_start(b1t[:, 1], a["L0_ffn_e_bg"].rearrange("e (p c) -> p e c", p=P)).then_inc(late_in, 16)
            stored(u.prev())
            piece(0, 5)
            sp.wait_ge(z_pair, 4 * (B - 1))
            sp.dma_start(c_wo, chunks(a["L0_ffn_c_Wo"])).then_inc(late_in, 16)
            sp.dma_start(dbv_r, row(a["L0_ffn_d_bv"], 64)).then_inc(late_in, 16)
            sp.dma_start(dbo_r, row(a["L0_ffn_d_bo"], 64)).then_inc(late_in, 16)
            for b in range(B):
                rows = slice(b * NS, (b + 1) * NS)
                sp.dma_start(slot_r[rows, :], a["L0_ffn_slot_query"].rearrange("o s d -> (o s) d")).then_inc(late_in, 16)
                sp.dma_start(eg_r[rows, :], a["L0_ffn_e_ln_g"]).then_inc(late_in, 16)
                sp.dma_start(eb_r[rows, :], a["L0_ffn_e_ln_b"]).then_inc(late_in, 16)
            queries_stored(u.prev())
            stored(u)
            sp.wait_ge(x1_out, 16 * HALVES * B)
            sp.wait_ge(xn2_made, HALVES * B)
            piece(1, 0)
            queries_stored(u)
            sp.wait_ge(qp_done, HM * HALVES * B)
            piece(1, 1)
            sp.wait_ge(z_pair, 4 * B)
            sp.wait_ge(qh_out, 16 * HALVES * B)
            piece(1, 2)
            for n in range(len(place), PIECES * NS // GROUP):
                sp.wait_ge(piece_used, n - len(place) + 1)
                piece(n // PIECES, n % PIECES)

            sp.wait_ge(qh_out, 16 * HALVES * B)
            sp.wait_ge(x1_out, 16 * HALVES * B)
            sp.wait_ge(piece_used, 2 * len(place) - 1)

            def queries(b, h):
                sp.dma_start(qh_in[:, h], qh_dram[b, :, :, h * T:(h + 1) * T]).then_inc(qh_back[h], 16)

            def stream(b, h):
                sp.dma_start(x1_in[:, h], x1_dram[b, h]).then_inc(x1_back[h], 16)

            def f_turn(b):
                for i in range(PAIRS):
                    if i % 2 == 1 and not (isinstance(b, int) and b >= B - 1):
                        sp.wait_ge(f_s_done, PAIRS * b + i + 1)
                        queries(b + 1, i // 2)
                    p = Pair(b, i, 6)
                    if p.there:
                        sp.wait_ge(f_res, p.n + 1)
                        sp.dma_start(out_dram[p.b, p.i], res[p.i % 2].rearrange("p (j d) -> p j d", j=2)) \
                            .then_inc(res_out[p.i % 2], 16)
                        if i % 2 == 1 and not (isinstance(p.b, int) and p.b == B - 1):
                            stream(p.b + 1, p.half)

            for h in range(HALVES):
                queries(0, h)
                stream(0, h)
            f_turn(0)
            f_turn(1)
            with sp.Fori(2, B - 1) as b:
                f_turn(b)
            f_turn(B - 1)
            f_turn(B)
            f_turn(B + 1)
            for s in range(2):
                sp.wait_ge(res_out[s], 16 * B * PAIRS // 2)

        @block.gpsimd
        def _(pool):
            own = Count(pool_own)

            def link(ins):
                own.step += 1
                ins.then_inc(pool_own, 1)
                pool.wait_ge(pool_own, own.now())

            nc.gpsimd.memset(minus_half[:], -0.5)
            nc.gpsimd.memset(mask8[:], 1.0)
            nc.gpsimd.memset(pair[:], 1.0)
            nc.gpsimd.memset(sel_raw, 0.0)
            link(nc.gpsimd.memset(ident[:], 0.0))
            nc.gpsimd.affine_select(out=ident[:], in_=ident[:], compare_op=ALU.not_equal, fill=1.0, base=0,
                                    pattern=[[-1, P]], channel_multiplier=1)
            for t, width, n in ((mask8, NS, 8), (pair, 64, 2)):
                link(nc.gpsimd.affine_select(out=t[:], in_=t[:], compare_op=ALU.is_ge, fill=0.0, base=0,
                                             pattern=[[-width, n]], channel_multiplier=1))
                link(nc.gpsimd.affine_select(out=t[:], in_=t[:], compare_op=ALU.is_ge, fill=0.0, base=width - 1,
                                             pattern=[[width, n]], channel_multiplier=-1))
            link(nc.gpsimd.affine_select(out=sel_raw, in_=sel_raw, compare_op=ALU.not_equal, fill=1.0, base=0,
                                         pattern=[[-2, CH], [-1, 2], [0, 64]], channel_multiplier=1))
            nc.gpsimd.affine_select(out=sel_raw, in_=sel_raw, compare_op=ALU.not_equal, fill=1.0, base=-32,
                                    pattern=[[-2, CH], [-1, 2], [0, 64]], channel_multiplier=1).then_inc(consts_made, 1)

            def rate(mv, r, n, ready, at, done):
                pool.wait_ge(ready, at)
                link(nc.gpsimd.tensor_tensor(r[:, 0, 0:n], mv[:, :, 1], minus_half[:, 0:n], ALU.pow))
                nc.gpsimd.tensor_tensor(r[:, 1, 0:n], mv[:, :, 0], r[:, 0, 0:n], ALU.mult).then_inc(done, 1)

            def q_state(u, c):
                pool.wait_ge(scan_made, CH * u.n + c + 1)
                nc.gpsimd.tensor_tensor(v[:, u.h, c], q[:, u.h, c], st[:, c % 2], ALU.mult).then_inc(qst_made, 1)

            def stage(b, first, last):
                for h in range(HALVES - last):
                    u = Unit(b, h)
                    p = u.prev()
                    if p:
                        rate(mv2, r2, TJ, ln2_stats, p.n + 1, ln2_rate)
                    q_state(u, 0)
                    q_state(u, 1)
                    if p:
                        rate(mv3, r3, TJ, ln3_stats, p.n + 1, ln3_rate)
                    with_slots = h == 1 and not first
                    if with_slots:
                        q_state(u, 2)
                        q_state(u, 3)
                    if not last:
                        w = Unit(b + 1, h)
                        pool.wait_ge(xn_made, w.n)
                        rate(mv1, r1, TJ, ln1_stats, w.n + 1, ln1_rate)
                    if not with_slots:
                        q_state(u, 2)
                        q_state(u, 3)
                    if p:
                        rate(mv4, r4, TJ, ln4_stats, p.n + 1, ln4_rate)

            rate(mv1, r1, TJ, ln1_stats, 1, ln1_rate)
            pool.wait_ge(xn_made, 1)
            rate(mv1, r1, TJ, ln1_stats, 2, ln1_rate)
            pool.wait_ge(small_in, 16 * SMALL_LOADS)
            stage(0, True, False)
            with pool.Fori(1, B - 1) as b:
                own.enter(b - 1, POOL_OWN)
                stage(b, False, False)
                own.leave(B - 2)
            stage(B - 1, False, True)
            u, p = Unit(B - 1, 1), Unit(B - 1, 0)
            for c in range(CH):
                q_state(u, c)
            rate(mv2, r2, TJ, ln2_stats, p.n + 1, ln2_rate)
            rate(mv3, r3, TJ, ln3_stats, p.n + 1, ln3_rate)
            rate(mv2, r2, TJ, ln2_stats, u.n + 1, ln2_rate)
            rate(mv4, r4, TJ, ln4_stats, p.n + 1, ln4_rate)
            rate(mv3, r3, TJ, ln3_stats, u.n + 1, ln3_rate)
            rate(mv4, r4, TJ, ln4_stats, u.n + 1, ln4_rate)

            pool.wait_ge(wo_done, 2 * HALVES * B)
            nc.gpsimd.memset(hcur, 0.0)
            nc.gpsimd.memset(at, 0.0).then_inc(pads_made, 1)
            pool.wait_ge(c_dve, 3)
            link(nc.gpsimd.tensor_scalar(r5[0:64, 0, 1, 0:1], mv5[0:64, 0, 0, 1:2], EPS, None, ALU.add))
            nc.gpsimd.tensor_tensor(r5[0:64, 0, 0, 0:1], r5[0:64, 0, 1, 0:1], minus_half[0:64, 0:1], ALU.pow).then_inc(c_pool, 1)

            def f_normalise(p):
                pool.wait_ge(f_rec, p.n + 1)
                pv = prob[p.i].rearrange("p (th s) -> p th s", s=NS)
                nc.gpsimd.tensor_tensor(pv, pv, trec[:, p.i % 2].unsqueeze(2).to_broadcast([P, 32, NS]), ALU.mult) \
                    .then_inc(f_norm, 1)

            def f_result(p):
                pool.wait_ge(f_norm2, p.n + 1)
                if p.i % 2 == 0:
                    pool.wait_ge(x1_back[p.half], (p.b + 1) * 16)
                if p.after(2):
                    pool.wait_ge(res_out[p.i % 2], (p.b * 2 + p.i // 2) * 16)
                nc.gpsimd.tensor_tensor(res[p.i % 2], y[p.i % 2],
                                        x1_in[:, p.half, 2 * (p.i % 2):2 * (p.i % 2) + 2].rearrange("p j d -> p (j d)"),
                                        ALU.add).then_inc(f_res, 1)

            def f_turn(b):
                for i in range(PAIRS):
                    made, rated, ended = Pair(b, i, 1), Pair(b, i, 4), Pair(b, i, 6)
                    if made.there:
                        f_normalise(made)
                    if rated.there and rated.i % 2 == 1:
                        if rated.after(4):
                            pool.wait_ge(f_norm2, 2 * (rated.nh - 1))
                        rate(mv5[:, rated.half], r5[:, rated.half], 4, f_stats, rated.nh + 1, f_rate)
                    if ended.there:
                        f_result(ended)

            f_turn(0)
            f_turn(1)
            with pool.Fori(2, B) as b:
                own.enter(b - 2, PAIRS // 2)
                f_turn(b)
                own.leave(B - 2)
            f_turn(B)
            f_turn(B + 1)

        @block.scalar
        def _(act):
            def ln1(u):
                act.wait_ge(ln1_rate, u.n + 1)
                if not (isinstance(u.n, int) and u.n == 0):
                    act.wait_ge(t1_done, KC * u.n)
                for j in range(TJ):
                    ins = nc.scalar.activation(xn[:, j], x[:, j], ACT.Identity,
                                               bias=r1[:, 1, j:j + 1], scale=r1[:, 0, j:j + 1])
                ins.then_inc(xn_made, 1)

            def ln3(u):
                act.wait_ge(ln3_rate, u.n + 1)
                y = layer_out(u)
                for j in range(TJ):
                    ins = nc.scalar.activation(y[:, j], y[:, j], ACT.Identity,
                                               bias=r3[:, 1, j:j + 1], scale=r3[:, 0, j:j + 1])
                ins.then_inc(ln3_made, 1)

            def x_high(u):
                for k in range(KC):
                    act.wait_ge(t1_done, KC * u.n + k + 1)
                    if k == 0 and not (isinstance(u.n, int) and u.n == 0):
                        act.wait_ge(v_done, CH * u.n)
                    nc.scalar.copy(x_hi[:, k], bank[3 + k][:]).then_inc(x_hi_made, 1)

            def q_out(u, c):
                act.wait_ge(q_done, CH * u.n + c + 1)
                if not (isinstance(u.b, int) and u.b == 0):
                    act.wait_ge(qst_made, CH * (u.n - 2) + c + 1)
                    act.wait_ge(inner_made, CH * (u.n - 2) + c + 1)
                nc.scalar.activation(q[:, u.h, c], bank[0][:], ACT.Identity, bias=bq_c[:, c:c + 1]).then_inc(q_made, 1)

            def v_out(u, c):
                act.wait_ge(v_done, CH * u.n + c + 1)
                if not (isinstance(u.b, int) and u.b == 0):
                    act.wait_ge(wo_done, 2 * (u.n - 1))
                nc.scalar.activation(v[:, u.h, c], bank[2][:], ACT.Identity, bias=bv2[:, c:c + 1],
                                     scale=keep2[:, c:c + 1]).then_inc(v_made, 1)

            def qv(u, c):
                q_out(u, c)
                v_out(u, c)

            def tanh_q(u, c):
                act.wait_ge(q_made, CH * u.n + c + 1)
                if not (isinstance(u.n, int) and u.n == 0 and c < 2):
                    act.wait_ge(inner_made, CH * u.n + c - 1)
                nc.scalar.activation(th[:, c % 2], q[:, u.h, c], ACT.Tanh, scale=aug_half[:, c:c + 1]).then_inc(th_made, 1)

            def softmax_exp(u):
                act.wait_ge(cen_made, u.n + 1)
                nc.scalar.activation(att[:], att[:], ACT.Exp, scale=RECUR_SCALE).then_inc(exp_made, 1)

            def att_high(u):
                act.wait_ge(att_t_done, u.n + 1)
                if not (isinstance(u.n, int) and u.n == 0):
                    act.wait_ge(spread_done, CH * u.n)
                nc.scalar.copy(att_parts[0:HEADS, :], bank[5][0:HEADS, :]).then_inc(att_hi_made, 1)

            def x2_high(u):
                for k in range(KC):
                    act.wait_ge(t2_done, KC * u.n + k + 1)
                    if k == 0 and not (isinstance(u.n, int) and u.n == 0):
                        act.wait_ge(qp_done, HM * u.n)
                    nc.scalar.copy(x2_hi[:, k], bank[3 + k][:]).then_inc(x2_hi_made, 1)

            def scored(u, m):
                act.wait_ge(s_done, HM * u.n + m + 1)
                if m == 0 and u.h == 0 and not (isinstance(u.b, int) and u.b == 0):
                    act.wait_ge(pt_done, 4 * u.b)
                nc.scalar.activation(sc[:, m, u.h * T:(u.h + 1) * T], bank[3 + m][:], ACT.Identity,
                                     bias=m_bias[:, m:m + 1]).then_inc(s_made, 1)

            def queried(u, m):
                act.wait_ge(qp_done, HM * u.n + m + 1)
                if m == 0 and not (isinstance(u.n, int) and u.n == 0):
                    act.wait_ge(qh_out, 16 * u.n)
                nc.scalar.activation(qh[:, m], bank[3 + m][:], ACT.Identity, bias=cbq_c[:, m:m + 1]).then_inc(qh_made, 1)

            def slot_exp(b):
                for m in range(HM):
                    act.wait_ge(smax_made, HM * b + m + 1)
                    nc.scalar.activation(sc[:, m], sc[:, m], ACT.Exp, bias=cneg[:, m:m + 1], scale=SCORE_SCALE,
                                         accum_out=csum[:, m:m + 1]).then_inc(p_made, 1)

            def slot_weights(b, steps):
                for t in steps:
                    act.wait_ge(pt_done, 4 * b + t + 1)
                    if t >= 2:
                        act.wait_ge(z_pair, 4 * b + t - 1)
                    nc.scalar.copy(pt[:, t % 2], bank[3 + t % 2][:].rearrange("p (t n) -> p t n", t=2)) \
                        .then_inc(pt_made, 1)

            def slot_sums(b):
                act.wait_ge(z_pair, 4 * b + 4)
                for k in range(KC):
                    nc.scalar.copy(zt[:, k, :, b, :], bank[0][:, k * HQ:(k + 1) * HQ].rearrange("p (h q) -> p h q", q=NS)) \
                        .then_inc(zt_made, 1)

            def ln4(u):
                act.wait_ge(ln4_rate, u.n + 1)
                if u.h == 0 and isinstance(u.b, int) and u.b == B - 1:
                    act.wait_ge(inner_made, CH * (u.n + 1))
                elif u.h == 0 and not (isinstance(u.b, int) and u.b == 0):
                    act.wait_ge(z_pair, 4 * u.b)
                for j in range(TJ):
                    ins = nc.scalar.activation(normed(u.b)[:, u.h * TJ + j], x1[:, j], ACT.Identity,
                                               bias=r4[:, 1, j:j + 1], scale=r4[:, 0, j:j + 1])
                ins.then_inc(xn2_made, 1)

            def stage(b, first, last):
                for h in range(HALVES - last):
                    u = Unit(b, h)
                    p = u.prev()
                    with_slots = h == 1 and not first
                    p2 = u.before()
                    w = u.next()
                    if p2:
                        x2_high(p2)
                    q_out(w, 0)
                    v_out(w, 0)
                    tanh_q(u, 0)
                    tanh_q(u, 1)
                    if p2:
                        scored(p2, 0)
                        scored(p2, 1)
                        queried(p2, 0)
                    q_out(w, 1)
                    v_out(w, 1)
                    q_out(w, 2)
                    if p:
                        ln3(p)
                    if with_slots:
                        slot_exp(b - 1)
                    elif not last:
                        ln1(Unit(b + 1, h))
                    tanh_q(u, 2)
                    v_out(w, 2)
                    if p2:
                        queried(p2, 1)
                    q_out(w, 3)
                    tanh_q(u, 3)
                    v_out(w, 3)
                    if with_slots:
                        slot_weights(b - 1, (0, 1))
                        ln1(Unit(b + 1, h))
                        slot_weights(b - 1, (2, 3))
                        slot_sums(b - 1)
                    if not last:
                        x_high(Unit(b + 1, h))
                    if p:
                        ln4(p)
                    softmax_exp(w)
                    att_high(w)

            def w_high(w):
                act.wait_ge(w_in[w], 16)
                nc.scalar.copy(w_hi[:, :, w], w_raw[:, :, w]).then_inc(w_hi_made, 1)

            w_high(0)
            ln1(Unit(0, 0))
            w_high(1)
            w_high(2)
            x_high(Unit(0, 0))
            act.wait_ge(vec_made, 1)
            nc.scalar.activation(alpha_c, alpha_c, ACT.Tanh, scale=0.5).then_inc(tanh_alpha, 1)
            act.wait_ge(consts_made, 1)
            nc.scalar.copy(sel[:], sel_raw.rearrange("r c a n -> r c (a n)")).then_inc(sel_split, 1)
            act.wait_ge(rates_made, 1)
            qv(Unit(0, 0), 0)
            ln1(Unit(0, 1))
            qv(Unit(0, 0), 1)
            act.wait_ge(rows_zero, 1)
            act.wait_ge(rows_twice, 1)
            nc.scalar.copy(bo_parts[0:1, :], bias_rows[:, 0])
            nc.scalar.copy(cbo_parts[0:1, :], bias_rows[:, 1]).then_inc(rows_hi, 1)
            act.wait_ge(cq_in, 16)
            nc.scalar.copy(cq_hi[:], cwq).then_inc(w_hi_made, 1)
            qv(Unit(0, 0), 2)
            act.wait_ge(fold_pe, 3)
            nc.scalar.copy(m_hi[:], bank[6][:].rearrange("p (k n) -> p k n", k=KC)).then_inc(m_hi_made, 1)
            qv(Unit(0, 0), 3)
            x_high(Unit(0, 1))
            softmax_exp(Unit(0, 0))
            att_high(Unit(0, 0))
            stage(0, True, False)
            with act.Fori(1, B - 1) as b:
                stage(b, False, False)
            stage(B - 1, False, True)
            u, p, p2 = Unit(B - 1, 1), Unit(B - 1, 0), Unit(B - 2, 1)
            x2_high(p2)
            tanh_q(u, 0)
            tanh_q(u, 1)
            scored(p2, 0)
            tanh_q(u, 2)
            scored(p2, 1)
            tanh_q(u, 3)
            queried(p2, 0)
            queried(p2, 1)
            slot_exp(B - 2)
            ln3(p)
            slot_weights(B - 2, range(4))
            ln4(p)
            slot_sums(B - 2)
            x2_high(p)
            ln3(u)
            for m in range(HM):
                scored(p, m)
            ln4(u)
            for m in range(HM):
                queried(p, m)
            x2_high(u)
            for m in range(HM):
                scored(u, m)
            for m in range(HM):
                queried(u, m)
            slot_exp(B - 1)
            slot_weights(B - 1, range(4))
            slot_sums(B - 1)

            act.wait_ge(pads_made, 1)
            act.wait_ge(c_dve, 5)
            with act.Fori(0, NS // GROUP) as g:
                for k in range(KC):
                    ins = nc.scalar.copy(hcur[:, k, :, 0:B],
                                         ht[:, k, :, bass.ds(g * GROUP, GROUP)].rearrange("p b j -> p j b"))
                ins.then_inc(hcur_made, 1)
                act.wait_ge(piece_used, PIECES * g + 2)
                nc.scalar.copy(u_sb[:, 0:512], bank[0][:])
                nc.scalar.copy(u_sb[:, 512:1024], bank[1][:]).then_inc(u_out, 1)
                act.wait_ge(ug_made, g + 1)
                nc.scalar.activation(eug.rearrange("p w c j b -> p (w c j b)"),
                                     ug.rearrange("p w c j b -> p (w c j b)"), ACT.Exp, scale=-1.0).then_inc(eug_made, 1)
                act.wait_ge(piece_used, PIECES * g + 6)
                nc.scalar.copy(ysb, bank[0][:, 0:D]).then_inc(y_out, 1)

            def values_out():
                for i in range(4):
                    act.wait_ge(vp_done, i // 2 + 1)
                    ins = nc.scalar.copy(vp[:, i // 2, (i % 2) * 2:(i % 2) * 2 + 2, :],
                                         bank[4 + i][:].rearrange("p (b n) -> p b n", b=2))
                ins.then_inc(vp_made, 1)

            def f_exponent(p):
                act.wait_ge(f_cen, p.n + 1)
                nc.scalar.activation(prob[p.i], prob[p.i], ACT.Exp, scale=SCORE_SCALE).then_inc(f_exp, 1)

            def f_transposed(p):
                act.wait_ge(f_t_done, p.n + 1)
                if p.after(2):
                    act.wait_ge(f_y_done, p.n - 1)
                nc.scalar.copy(ptl[p.i % 2], bank[2 + p.i % 2][:]).then_inc(f_pt, 1)

            def f_scale(p):
                act.wait_ge(f_rate, p.nh + 1)
                if p.after(2):
                    act.wait_ge(f_res, p.n - 1)
                k = 2 * (p.i % 2)
                for j in range(2):
                    ins = nc.scalar.activation(y[p.i % 2][:, j * D:(j + 1) * D], bank[4 + p.i][:, j * D:(j + 1) * D],
                                               ACT.Identity, bias=r5[:, p.half, 1, k + j:k + j + 1],
                                               scale=r5[:, p.half, 0, k + j:k + j + 1])
                ins.then_inc(f_norm2, 1)

            def f_turn(b):
                for i in range(PAIRS):
                    scored, turned, rated = Pair(b, i), Pair(b, i, 2), Pair(b, i, 6)
                    if isinstance(b, int) and b == 0 and i == 2:
                        values_out()
                    if turned.there:
                        f_transposed(turned)
                    if scored.there:
                        f_exponent(scored)
                    if rated.there:
                        f_scale(rated)

            f_turn(0)
            f_turn(1)
            with act.Fori(2, B) as b:
                f_turn(b)
            f_turn(B)
            f_turn(B + 1)

        @block.vector
        def _(dve):
            own = Count(dve_own)

            def link(ins):
                own.step += 1
                ins.then_inc(dve_own, 1)
                dve.wait_ge(dve_own, own.now())

            def combine(st, both, apart, spread, mv, eps, done):
                nc.vector.tensor_tensor(both, st[:, :, 1:3], st[:, :, 4:6], ALU.add)
                link(nc.vector.tensor_tensor(apart, st[:, :, 1], st[:, :, 4], ALU.subtract))
                nc.vector.tensor_tensor(apart, apart, apart, ALU.mult)
                nc.vector.tensor_scalar(mv[:, :, 0], both[:, :, 0], -0.5, None, ALU.mult)
                link(nc.vector.tensor_scalar(spread, both[:, :, 1], 1.0 / D, eps, ALU.mult, ALU.add))
                nc.vector.scalar_tensor_tensor(out=mv[:, :, 1], in0=apart, scalar=0.25, in1=spread,
                                               op0=ALU.mult, op1=ALU.add).then_inc(done, 1)

            def moments(src, mv, eps, done):
                for j in range(TJ - 1):
                    nc.vector.bn_stats(stats[:, j], src(j))
                link(nc.vector.bn_stats(stats[:, TJ - 1], src(TJ - 1)))
                combine(stats[:], both[:], apart[:], spread_var[:], mv, eps, done)

            def ln1(u):
                dve.wait_ge(x_in, 16 * (u.n + 1))
                if not (isinstance(u.n, int) and u.n == 0):
                    dve.wait_ge(ln1_rate, u.n)
                moments(lambda j: x[:, j], mv1, EPS, ln1_stats)

            def x_low(u):
                for k in range(KC):
                    dve.wait_ge(x_hi_made, KC * u.n + k + 1)
                    nc.vector.tensor_tensor(x_lo[:, k], bank[3 + k][:], x_hi[:, k], ALU.subtract).then_inc(x_lo_made, 1)

            def q_times_k(u, c):
                dve.wait_ge(q_made, CH * u.n + c + 1)
                dve.wait_ge(k_done, CH * u.n + c + 1)
                if not (isinstance(u.n, int) and u.n == 0 and c < 2):
                    dve.wait_ge(sum_done, CH * u.n + c - 1)
                nc.vector.scalar_tensor_tensor(out=qk[:, c % 2], in0=bank[1][:], scalar=bk_c[:, c:c + 1],
                                               in1=q[:, u.h, c], op0=ALU.add, op1=ALU.mult).then_inc(qk_made, 1)

            def softmax(u):
                heads = bank[5][:, 0:TJ * HEADS].rearrange("p (j h) -> p j h", h=HEADS)
                dve.wait_ge(sum_done, CH * (u.n + 1))
                link(nc.vector.tensor_reduce(smx[:], heads, X, ALU.max))
                nc.vector.tensor_tensor(att[:], heads, smx[:].unsqueeze(2).to_broadcast([P, TJ, HEADS]), ALU.subtract) \
                    .then_inc(cen_made, 1)
                dve.wait_ge(exp_made, u.n + 1)
                link(nc.vector.tensor_reduce(sums[:], att[:], X, ALU.add))
                link(nc.vector.reciprocal(rsum[:], sums[:]))
                nc.vector.tensor_tensor(att[:], att[:], rsum[:].unsqueeze(2).to_broadcast([P, TJ, HEADS]), ALU.mult) \
                    .then_inc(att_made, 1)

            def att_low(u):
                dve.wait_ge(att_hi_made, u.n + 1)
                nc.vector.tensor_tensor(att_parts[32:32 + HEADS, :], bank[5][0:HEADS, :], att_parts[0:HEADS, :],
                                        ALU.subtract).then_inc(att_lo_made, 1)

            def recur(u, c):
                dve.wait_ge(spread_done, CH * u.n + c + 1)
                dve.wait_ge(v_made, CH * u.n + c + 1)
                nc.vector.tensor_tensor(v[:, u.h, c], spread_banks(u)[c % 2][:], v[:, u.h, c], ALU.mult).then_inc(val_made, 1)
                dve.wait_ge(val_made, CH * u.n + c + 1)
                if not (isinstance(u.n, int) and u.n == 0 and c < 2):
                    dve.wait_ge(qst_made, CH * u.n + c - 1)
                initial = 0.0 if u.h == 0 else carry[:, c:c + 1]
                nc.vector.tensor_tensor_scan(st[:, c % 2], decay[:, c:c + 1].to_broadcast([P, T]), v[:, u.h, c],
                                             initial, ALU.mult, ALU.add).then_inc(scan_made, 1)
                if u.h == 0:
                    dve.wait_ge(scan_made, CH * u.n + c + 1)
                    link(nc.vector.tensor_copy(carry[:, c:c + 1], st[:, c % 2, T - 1:T]))

            def inner(u, c):
                dve.wait_ge(qst_made, CH * u.n + c + 1)
                dve.wait_ge(th_made, CH * u.n + c + 1)
                nc.vector.scalar_tensor_tensor(out=v[:, u.h, c], in0=th[:, c % 2], scalar=1.0, in1=v[:, u.h, c],
                                               op0=ALU.add, op1=ALU.add).then_inc(inner_made, 1)

            def ln2(u):
                dve.wait_ge(wo_done, 2 * u.n + 2)
                moments(lambda j: out_banks(u)[j // 2][:, (j % 2) * D:(j % 2 + 1) * D], mv2, 4 * EPS_OUT, ln2_stats)

            def ln2_gain(u):
                if is_last(u):
                    dve.wait_ge(xn_made, u.n + 1)
                elif not (isinstance(u.n, int) and u.n == 0):
                    dve.wait_ge(x1_made, u.n)
                y = layer_out(u)
                for j in range(TJ):
                    ins = nc.vector.scalar_tensor_tensor(out=y[:, j], in0=out_banks(u)[j // 2][:, (j % 2) * D:(j % 2 + 1) * D],
                                                         scalar=mv2[:, j, 0:1], in1=lns_r[:], op0=ALU.add, op1=ALU.mult)
                ins.then_inc(ln2_made, 1)

            def ln2_shift(u):
                dve.wait_ge(ln2_made, u.n + 1)
                dve.wait_ge(ln2_rate, u.n + 1)
                y = layer_out(u)
                for j in range(TJ):
                    ins = nc.vector.scalar_tensor_tensor(out=y[:, j], in0=y[:, j], scalar=r2[:, 0, j:j + 1], in1=lnb_r[:],
                                                         op0=ALU.mult, op1=ALU.add)
                ins.then_inc(gain_made, 1)

            def ln3(u):
                dve.wait_ge(gain_made, u.n + 1)
                moments(lambda j: layer_out(u)[:, j], mv3, EPS, ln3_stats)

            def ln4(u):
                dve.wait_ge(ln3_made, u.n + 1)
                dve.wait_ge(xr_in, 16 * (u.n + 1))
                if not (isinstance(u.n, int) and u.n == 0):
                    dve.wait_ge(x1_out, 16 * u.n)
                    dve.wait_ge(xn2_made, u.n)
                nc.vector.tensor_tensor(x1, layer_out(u), x_res, ALU.add).then_inc(x1_made, 1)
                dve.wait_ge(x1_made, u.n + 1)
                moments(lambda j: x1[:, j], mv4, EPS, ln4_stats)

            def x2_low(u):
                for k in range(KC):
                    dve.wait_ge(x2_hi_made, KC * u.n + k + 1)
                    nc.vector.tensor_tensor(x2_lo[:, k], bank[3 + k][:], x2_hi[:, k], ALU.subtract).then_inc(x2_lo_made, 1)

            def slot_max(b):
                for m in range(HM):
                    dve.wait_ge(s_made, HM * (HALVES * b + 1) + m + 1)
                    link(nc.vector.tensor_reduce(cmx[:, m:m + 1], sc[:, m], X, ALU.max))
                    nc.vector.tensor_scalar(cneg[:, m:m + 1], cmx[:, m:m + 1], -SCORE_SCALE, None, ALU.mult) \
                        .then_inc(smax_made, 1)

            def slot_norm(b):
                for m in range(HM):
                    dve.wait_ge(p_made, HM * b + m + 1)
                    link(nc.vector.reciprocal(crec[:, m:m + 1], csum[:, m:m + 1]))
                    nc.vector.tensor_scalar(sc[:, m], sc[:, m], crec[:, m:m + 1], None, ALU.mult).then_inc(pn_made, 1)

            def stage(b, first, last):
                for h in range(HALVES - last):
                    u = Unit(b, h)
                    p = u.prev()
                    with_slots = h == 1 and not first
                    w = u.next()
                    if p:
                        dve.wait_ge(ln2_stats, p.n + 1)
                        ln2_gain(p)
                    if u.before():
                        x2_low(u.before())
                    q_times_k(w, 0)
                    recur(u, 0)
                    recur(u, 1)
                    if p:
                        ln2_shift(p)
                        ln3(p)
                    inner(u, 0)
                    q_times_k(w, 1)
                    if with_slots:
                        slot_max(b - 1)
                    elif not last:
                        ln1(Unit(b + 1, h))
                    recur(u, 2)
                    inner(u, 1)
                    q_times_k(w, 2)
                    recur(u, 3)
                    if with_slots:
                        slot_norm(b - 1)
                    inner(u, 2)
                    inner(u, 3)
                    q_times_k(w, 3)
                    if with_slots:
                        ln1(Unit(b + 1, h))
                    if p:
                        ln4(p)
                    if not last:
                        x_low(Unit(b + 1, h))
                    softmax(w)
                    ln2(u)
                    att_low(w)

            nc.vector.memset(att_parts[:].bitcast(F32), 0.0)
            for t in (ones_parts, bo_parts, cbo_parts):
                ins = nc.vector.memset(t[:].bitcast(F32), 0.0)
            link(ins)
            nc.vector.memset(ones_parts[0:1, :].bitcast(F32), 1.0)
            nc.vector.memset(ones_parts[32:33, :].bitcast(F32), 1.0).then_inc(rows_zero, 1)
            def w_low(w):
                dve.wait_ge(w_hi_made, w + 1)
                nc.vector.tensor_tensor(w_lo[:, :, w], w_raw[:, :, w], w_hi[:, :, w], ALU.subtract).then_inc(w_lo_made, 1)

            ln1(Unit(0, 0))
            for w in range(NW):
                w_low(w)
            x_low(Unit(0, 0))
            dve.wait_ge(vec_turned, 1)
            nc.vector.tensor_copy(vec[:], bank[7][:, 0:VROWS]).then_inc(vec_made, 1)
            dve.wait_ge(tanh_alpha, 1)
            nc.vector.tensor_scalar(decay[:], alpha_c, 0.5, 0.5, ALU.mult, ALU.add)
            link(nc.vector.tensor_scalar(keep2[:], alpha_c, -1.0, 1.0, ALU.mult, ALU.add))
            nc.vector.tensor_tensor(bv2[:], bv_c, keep2[:], ALU.mult)
            nc.vector.tensor_scalar(aug_half[:], aug_c, 0.5, None, ALU.mult).then_inc(rates_made, 1)
            q_times_k(Unit(0, 0), 0)
            ln1(Unit(0, 1))
            dve.wait_ge(fold_pe, 1)
            nc.vector.tensor_copy(sqt, bank[7][:, 0:KC * NS].rearrange("p (k n) -> p k n", k=KC))
            nc.vector.tensor_copy(wkt, bank[6][:].rearrange("p (m n) -> p m n", m=HM)).then_inc(fold_dve, 1)
            dve.wait_ge(small_in, 16 * SMALL_LOADS)
            nc.vector.tensor_scalar(bias_rows[:, 0], bias_rows[:, 0], 2.0, None, ALU.mult).then_inc(rows_twice, 1)
            q_times_k(Unit(0, 0), 1)
            dve.wait_ge(fold_pe, 2)
            for m in range(HM):
                link(nc.vector.tensor_scalar(qht[:, m], bank[7][:, m * NS:(m + 1) * NS], dbq_c[:, m:m + 1], None, ALU.add))
                ins = nc.vector.tensor_tensor(qbd[:, m].rearrange("p (h s) -> p h s", s=NS),
                                              qht[:, m].unsqueeze(1).to_broadcast([P, 8, NS]),
                                              mask8[:].unsqueeze(2).to_broadcast([P, 8, NS]), ALU.mult)
            ins.then_inc(fold_dve, 1)
            dve.wait_ge(rows_hi, 1)
            nc.vector.tensor_tensor(bo_parts[32:33, :], bias_rows[:, 0], bo_parts[0:1, :], ALU.subtract).then_inc(rows_lo, 1)
            nc.vector.tensor_tensor(cbo_parts[32:33, :], bias_rows[:, 1], cbo_parts[0:1, :], ALU.subtract).then_inc(rows_lo, 1)
            dve.wait_ge(w_hi_made, NW + 1)
            nc.vector.tensor_tensor(cq_lo[:], cwq, cq_hi[:], ALU.subtract).then_inc(w_lo_made, 1)
            q_times_k(Unit(0, 0), 2)
            dve.wait_ge(m_hi_made, 1)
            nc.vector.tensor_copy(m_bias[:], bank[7][:, 0:HM])
            nc.vector.tensor_tensor(m_lo[:], bank[6][:].rearrange("p (k n) -> p k n", k=KC), m_hi[:], ALU.subtract) \
                .then_inc(m_lo_made, 1)
            q_times_k(Unit(0, 0), 3)
            x_low(Unit(0, 1))
            softmax(Unit(0, 0))
            att_low(Unit(0, 0))

            stage(0, True, False)
            with dve.Fori(1, B - 1) as b:
                own.enter(b - 1, DVE_OWN)
                stage(b, False, False)
                own.leave(B - 2)
            stage(B - 1, False, True)
            u, p, p2 = Unit(B - 1, 1), Unit(B - 1, 0), Unit(B - 2, 1)
            x2_low(p2)
            recur(u, 0)
            recur(u, 1)
            inner(u, 0)
            dve.wait_ge(ln2_stats, p.n + 1)
            ln2_gain(p)
            recur(u, 2)
            inner(u, 1)
            recur(u, 3)
            inner(u, 2)
            inner(u, 3)
            slot_max(B - 2)
            ln2_shift(p)
            slot_norm(B - 2)
            ln3(p)
            ln2(u)
            dve.wait_ge(ln2_stats, u.n + 1)
            ln2_gain(u)
            ln4(p)
            ln2_shift(u)
            ln3(u)
            x2_low(p)
            ln4(u)
            x2_low(u)
            slot_max(B - 1)
            slot_norm(B - 1)

            dve.wait_ge(late_in, 16 * LATE_LOADS)
            dve.wait_ge(c_pe, 1)
            nc.vector.tensor_tensor(vo, bank[0][0:64, 0:D], dbv_r, ALU.add).then_inc(c_dve, 1)
            dve.wait_ge(c_pe, 2)
            nc.vector.tensor_copy(vot.rearrange("p k n -> p (k n)"), bank[1][:, 0:128]).then_inc(c_dve, 1)
            dve.wait_ge(c_pe, 3)
            link(nc.vector.tensor_tensor(os_, bank[2][0:64, 0:D], dbo_r, ALU.add))
            link(nc.vector.tensor_tensor(os_, os_, slot_r, ALU.add))
            link(nc.vector.bn_stats(st5[0:64, 0, 0], os_))
            nc.vector.bn_aggr(mv5[0:64, 0, 0], st5[0:64, 0, 0]).then_inc(c_dve, 1)
            dve.wait_ge(c_pool, 1)
            link(nc.vector.tensor_scalar(hs, os_, mv5[0:64, 0, 0, 0:1], r5[0:64, 0, 0, 0:1], ALU.subtract, ALU.mult))
            link(nc.vector.tensor_tensor(hs, hs, eg_r, ALU.mult))
            nc.vector.tensor_tensor(hs, hs, eb_r, ALU.add).then_inc(c_dve, 1)
            dve.wait_ge(c_pe, 4)
            nc.vector.tensor_copy(ht.rearrange("p k b e -> p (k b e)"), bank[3][:, 128:256])
            nc.vector.tensor_tensor(o2t, bank[3][:, 0:128].rearrange("p (k b e) -> p k b e", k=KC, b=B),
                                    b2t.unsqueeze(2).to_broadcast([P, KC, B, NS]), ALU.add).then_inc(c_dve, 1)

            with dve.Fori(0, NS // GROUP) as g:
                own.enter(g, 3)
                dve.wait_ge(piece_used, PIECES * g + 4)
                nc.vector.tensor_copy(g_sb[:, 0:512], bank[2][:])
                nc.vector.tensor_copy(g_sb[:, 512:1024], bank[3][:]).then_inc(g_out, 1)
                for w in range(2):
                    dve.wait_ge(ut_done, 2 * g + w + 1)
                    for i in range(2):
                        bias = b1t[:, w, bass.ds(g * GROUP, GROUP), 4 * i:4 * i + 4].rearrange("p j c -> p c j") \
                            .unsqueeze(3).to_broadcast([P, 4, GROUP, B])
                        ins = nc.vector.tensor_tensor(
                            ug[:, w, 4 * i:4 * i + 4],
                            bank[4 + 2 * w + i][:].rearrange("p (c j n) -> p c j n", c=4, j=GROUP)[:, :, :, 0:B],
                            bias, ALU.add)
                ins.then_inc(ug_made, 1)
                dve.wait_ge(eug_made, g + 1)
                flat = "p w c j b -> p (w c j b)"
                link(nc.vector.tensor_scalar(eug.rearrange(flat), eug.rearrange(flat), 1.0, None, ALU.add))
                link(nc.vector.reciprocal(eug.rearrange(flat), eug.rearrange(flat)))
                link(nc.vector.tensor_tensor(ug.rearrange(flat), ug.rearrange(flat), eug.rearrange(flat), ALU.mult))
                nc.vector.tensor_tensor(at[:, :, :, 0:B], ug[:, 0], ug[:, 1], ALU.mult).then_inc(at_made, 1)
                dve.wait_ge(yt_done, g + 1)
                for k in range(KC):
                    part = o2t[:, k, :, bass.ds(g * GROUP, GROUP)].rearrange("p b j -> p j b")
                    ins = nc.vector.tensor_tensor(
                        part, part, bank[6][:, k * P:(k + 1) * P].rearrange("p (j n) -> p j n", j=GROUP)[:, :, 0:B], ALU.add)
                ins.then_inc(slots_made, 1)
                own.leave(NS // GROUP)

            dve.wait_ge(kv_done, 1)
            for w, bias in ((0, cbk_c), (1, cbv_c)):
                for m in range(HM):
                    ins = nc.vector.tensor_scalar(kv_t[:, w, m].rearrange("p b s -> p (b s)"),
                                                  bank[2 + w][:, m * 64:(m + 1) * 64], bias[:, m:m + 1], None, ALU.add)
                link(ins)
                for m in range(HM):
                    nc.vector.tensor_tensor(
                        (kb, vb)[w][:, m].rearrange("p b (h s) -> p b h s", s=NS),
                        kv_t[:, w, m].unsqueeze(2).to_broadcast([P, B, 8, NS]),
                        mask8[:].unsqueeze(1).unsqueeze(3).to_broadcast([P, B, 8, NS]), ALU.mult).then_inc(kv_made, 1)

            def f_centre(p):
                scores = bank[p.i % 2][:].rearrange("p (th s) -> p th s", s=NS)
                dve.wait_ge(f_s_done, p.n + 1)
                if p.after(4):
                    dve.wait_ge(f_t_done, p.n - 3)
                link(nc.vector.tensor_reduce(tmx[:, p.i % 2], scores, X, ALU.max))
                nc.vector.tensor_tensor(prob[p.i].rearrange("p (th s) -> p th s", s=NS), scores,
                                        tmx[:, p.i % 2].unsqueeze(2).to_broadcast([P, 32, NS]), ALU.subtract).then_inc(f_cen, 1)

            def f_sums(p):
                dve.wait_ge(f_exp, p.n + 1)
                if p.after(2):
                    dve.wait_ge(f_norm, p.n - 1)
                link(nc.vector.tensor_reduce(tsum[:, p.i % 2], prob[p.i].rearrange("p (th s) -> p th s", s=NS), X, ALU.add))
                nc.vector.reciprocal(trec[:, p.i % 2], tsum[:, p.i % 2]).then_inc(f_rec, 1)

            def f_moments(p):
                dve.wait_ge(f_y_done, p.n + 1)
                k = 2 * (p.i % 2)
                nc.vector.bn_stats(st5[:, p.half, k], bank[4 + p.i][:, 0:D])
                ins = nc.vector.bn_stats(st5[:, p.half, k + 1], bank[4 + p.i][:, D:2 * D])
                if p.i % 2 == 1:
                    link(ins)
                    if p.after(4):
                        dve.wait_ge(f_rate, p.nh - 1)
                    combine(st5[:, p.half], both[:], apart[:], spread_var[:], mv5[:, p.half], EPS, f_stats)

            def f_turn(b):
                for i in range(PAIRS):
                    scored, exponent, valued = Pair(b, i), Pair(b, i, 1), Pair(b, i, 4)
                    if scored.there:
                        f_centre(scored)
                    if exponent.there:
                        f_sums(exponent)
                    if valued.there:
                        f_moments(valued)

            f_turn(0)
            f_turn(1)
            with dve.Fori(2, B) as b:
                own.enter(b - 2, 2 * PAIRS + 3 * PAIRS // 2)
                f_turn(b)
                own.leave(B - 2)
            f_turn(B)

        @block.tensor
        def _(pe):
            def t1(u, prev):
                pe.wait_ge(xn_made, u.n + 1)
                for k in range(KC):
                    prev(k)
                    for j in range(TJ):
                        ins = nc.tensor.transpose(bank[3 + k][:, j * P:(j + 1) * P], xn[:, j, k * P:(k + 1) * P], ident[:])
                    ins.then_inc(t1_done, 1)

            def project(dst, w_h, w_l, x_h, x_l, cols, done):
                n = 0
                for k in range(KC):
                    for w, r in ((w_h, x_h), (w_h, x_l), (w_l, x_h)):
                        ins = nc.tensor.matmul(dst, w[:, k, cols], r[:, k], start=n == 0, stop=n == 3 * KC - 1)
                        n += 1
                ins.then_inc(done, 1)

            def qkv(u, c, free):
                if c == 0:
                    pe.wait_ge(x_hi_made, KC * (u.n + 1))
                    pe.wait_ge(x_lo_made, KC * (u.n + 1))
                cols = slice(c * P, (c + 1) * P)
                for w, done in ((0, q_done), (1, k_done), (2, v_done)):
                    if c:
                        pe.wait_ge((q_made, qk_made, v_made)[w], CH * u.n + c)
                    else:
                        free(w)
                    project(bank[w][:], w_hi[:, :, w], w_lo[:, :, w], x_hi, x_lo, cols, done)

            def head_sums(u, c):
                pe.wait_ge(qk_made, CH * u.n + c + 1)
                if c == 0 and not (isinstance(u.n, int) and u.n == 0):
                    pe.wait_ge(att_lo_made, u.n)
                for j in range(TJ):
                    at_ = j * HEADS + 2 * c
                    ins = nc.tensor.matmul(bank[5][:, at_:at_ + 2], qk[:, c % 2, j * P:(j + 1) * P], pair[:],
                                           start=True, stop=True)
                ins.then_inc(sum_done, 1)

            def att_transpose(u):
                pe.wait_ge(att_made, u.n + 1)
                for j in range(TJ):
                    ins = nc.tensor.transpose(bank[5][0:HEADS, j * P:(j + 1) * P], att[:, j], ident[:])
                ins.then_inc(att_t_done, 1)

            def spread(u, c):
                if c == 0:
                    pe.wait_ge(att_lo_made, u.n + 1)
                if c >= 2:
                    pe.wait_ge(val_made, CH * u.n + c - 1)
                elif is_last(u):
                    pe.wait_ge((qk_made, v_made)[c], CH * HALVES * B)
                elif not (isinstance(u.n, int) and u.n == 0):
                    pe.wait_ge(ln2_made, u.n)
                nc.tensor.matmul(spread_banks(u)[c % 2][:], sel[:, c], att_parts[:], start=True, stop=True) \
                    .then_inc(spread_done, 1)

            def out_project(u):
                pe.wait_ge(inner_made, CH * (u.n + 1))
                for p in range(2):
                    to = out_banks(u)[p]
                    if is_last(u) and p == 1:
                        pe.wait_ge(q_made, CH * HALVES * B)
                    for j in (2 * p, 2 * p + 1):
                        for c in range(CH):
                            ins = nc.tensor.matmul(to[:, (j % 2) * D:(j % 2 + 1) * D],
                                                   v[:, u.h, c, j * P:(j + 1) * P], wo[:, c], start=c == 0, stop=False)
                        ins = nc.tensor.matmul(to[:, (j % 2) * D:(j % 2 + 1) * D], ones_parts[:], bo_parts[:],
                                               start=False, stop=True)
                    ins.then_inc(wo_done, 1)

            def t2(u, prev):
                pe.wait_ge(xn2_made, u.n + 1)
                for k in range(KC):
                    prev(k)
                    for j in range(TJ):
                        ins = nc.tensor.transpose(bank[3 + k][:, j * P:(j + 1) * P],
                                                  normed(u.b)[:, u.h * TJ + j, k * P:(k + 1) * P], ident[:])
                    ins.then_inc(t2_done, 1)

            def slot_scores(u, m):
                if m == 0:
                    pe.wait_ge(x2_hi_made, KC * (u.n + 1))
                    pe.wait_ge(x2_lo_made, KC * (u.n + 1))
                project(bank[3 + m][:], m_hi, m_lo, x2_hi, x2_lo, slice(m * P, (m + 1) * P), s_done)

            def queries(u, m):
                pe.wait_ge(s_made, HM * u.n + m + 1)
                project(bank[3 + m][:], cq_hi, cq_lo, x2_hi, x2_lo, slice(m * P, (m + 1) * P), qp_done)

            def slots(b, ahead):
                pe.wait_ge(pn_made, HM * (b + 1))

                def turn(t):
                    if t < 2:
                        pe.wait_ge(qh_made, HM * (HALVES * b + 1) + t + 1)
                    else:
                        pe.wait_ge(pt_made, 4 * b + t - 1)
                    for i in range(2):
                        for m in range(HM):
                            ins = nc.tensor.transpose(bank[3 + t % 2][:, i * HQ + m * P:i * HQ + (m + 1) * P],
                                                      sc[:, m, (2 * t + i) * P:(2 * t + i + 1) * P], ident[:])
                    ins.then_inc(pt_done, 1)

                def add(t):
                    pe.wait_ge(pt_made, 4 * b + t + 1)
                    if t == 0:
                        if ahead:
                            pe.wait_ge(q_made, CH * (HALVES * b + 5))
                        elif b == B - 1:
                            pe.wait_ge(zt_made, KC * b)
                        else:
                            pe.wait_ge(q_made, CH * HALVES * B)
                    for i in range(2):
                        for k in range(KC):
                            ins = nc.tensor.matmul(bank[0][:, k * HQ:(k + 1) * HQ], normed(b)[:, 2 * t + i, k * P:(k + 1) * P], pt[:, t % 2, i],
                                                   start=t + i + k == 0, stop=t == 3 and i == 1 and k == KC - 1)
                    ins.then_inc(z_pair, 1)

                turn(0)
                for t in range(4):
                    if t < 3:
                        turn(t + 1)
                    add(t)

            def stage(b, first, last):
                for h in range(HALVES - last):
                    u = Unit(b, h)
                    w = u.next()
                    def banks012(i):
                        pe.wait_ge((q_made, qk_made, v_made)[i], CH * w.n)

                    p2, with_slots = u.before(), h == 1 and not first

                    def before_t1(k):
                        if with_slots:
                            pe.wait_ge(pt_made, 4 * b - 1 + k)
                        elif p2:
                            pe.wait_ge(qh_made, HM * p2.n + k + 1)
                        else:
                            pe.wait_ge(x_lo_made, KC * (u.n + 1) + k + 1)

                    def before_t2(k):
                        if not last:
                            pe.wait_ge(x_lo_made, KC * (u.n + 2) + k + 1)
                        elif with_slots:
                            pe.wait_ge(pt_made, 4 * b - 1 + k)
                        else:
                            pe.wait_ge(qh_made, HM * p2.n + k + 1)

                    qkv(w, 0, banks012)
                    spread(u, 0)
                    spread(u, 1)
                    if p2:
                        slot_scores(p2, 0)
                        slot_scores(p2, 1)
                        queries(p2, 0)
                    qkv(w, 1, banks012)
                    head_sums(w, 0)
                    spread(u, 2)
                    spread(u, 3)
                    qkv(w, 2, banks012)
                    head_sums(w, 1)
                    if p2:
                        queries(p2, 1)
                    qkv(w, 3, banks012)
                    head_sums(w, 2)
                    if with_slots:
                        slots(b - 1, True)
                    if not last:
                        t1(Unit(b + 1, h), before_t1)
                    head_sums(w, 3)
                    out_project(u)
                    att_transpose(w)
                    if u.prev():
                        t2(u.prev(), before_t2)

            def fold_transposes():
                pe.wait_ge(fold_in, 16 * FOLD_LOADS)
                pe.wait_ge(vec_made, 1)
                for k in range(KC):
                    nc.tensor.transpose(bank[7][:, k * NS:(k + 1) * NS], slot_in[:, k * P:(k + 1) * P], ident[0:NS, 0:NS])
                for m in range(HM):
                    for k in range(KC):
                        ins = nc.tensor.transpose(bank[6][:, m * D + k * P:m * D + (k + 1) * P],
                                                  dwk[:, k, m * P:(m + 1) * P], ident[:])
                ins.then_inc(fold_pe, 1)

            def fold_queries():
                pe.wait_ge(fold_dve, 1)
                for m in range(HM):
                    for k in range(KC):
                        ins = nc.tensor.matmul(bank[7][:, m * NS:(m + 1) * NS], dwq[:, k, m * P:(m + 1) * P], sqt[:, k],
                                               start=k == 0, stop=k == KC - 1)
                ins.then_inc(fold_pe, 1)

            def fold_weights():
                pe.wait_ge(fold_dve, 2)
                for k in range(KC):
                    for m in range(HM):
                        nc.tensor.matmul(bank[6][:, k * HQ + m * P:k * HQ + (m + 1) * P], wkt[:, m, k * P:(k + 1) * P],
                                         qbd[:, m], start=True, stop=True)
                for m in range(HM):
                    ins = nc.tensor.matmul(bank[7][:, m:m + 1], qbd[:, m], dbk_c[:, m:m + 1], start=True, stop=True)
                ins.then_inc(fold_pe, 1)

            pe.wait_ge(consts_made, 1)
            t1(Unit(0, 0), lambda k: None)
            pe.wait_ge(vec_in, 16 * len(VECTORS))
            nc.tensor.transpose(bank[7][:, 0:VROWS], vec_rows, ident[0:VROWS, 0:VROWS]).then_inc(vec_turned, 1)
            pe.wait_ge(w_lo_made, NW)
            for c in range(CH):
                qkv(Unit(0, 0), c, lambda i: None)
                if c:
                    head_sums(Unit(0, 0), c - 1)
                    (fold_transposes, fold_queries, fold_weights)[c - 1]()
            head_sums(Unit(0, 0), 3)
            t1(Unit(0, 1), lambda k: pe.wait_ge(x_lo_made, k + 1))
            att_transpose(Unit(0, 0))
            pe.wait_ge(m_lo_made, 1)
            pe.wait_ge(rows_lo, 2)
            pe.wait_ge(w_lo_made, NW + 1)
            pe.wait_ge(sel_split, 1)
            pe.wait_ge(wo_in, 16)

            stage(0, True, False)
            with pe.Fori(1, B - 1) as b:
                stage(b, False, False)
            stage(B - 1, False, True)
            u, p, p2 = Unit(B - 1, 1), Unit(B - 1, 0), Unit(B - 2, 1)
            spread(u, 0)
            spread(u, 1)
            slot_scores(p2, 0)
            spread(u, 2)
            slot_scores(p2, 1)
            spread(u, 3)
            queries(p2, 0)
            queries(p2, 1)
            out_project(u)
            slots(B - 2, False)
            t2(p, lambda k: pe.wait_ge(pt_made, 4 * (B - 2) + 3 + k))
            for m in range(HM):
                slot_scores(p, m)
            for m in range(HM):
                queries(p, m)
            t2(u, lambda k: pe.wait_ge(qh_made, HM * p.n + k + 1))
            for m in range(HM):
                slot_scores(u, m)
            for m in range(HM):
                queries(u, m)
            slots(B - 1, False)

            pe.wait_ge(late_in, 16 * LATE_LOADS)
            pe.wait_ge(zt_made, KC * B)
            pe.wait_ge(qh_made, HM * HALVES * B)
            for h in range(MH):
                for k in range(KC):
                    ins = nc.tensor.matmul(bank[0][0:64, h * 16:(h + 1) * 16], zt[:, k, h].rearrange("p b q -> p (b q)"),
                                           d_wv[:, k, h * 16:(h + 1) * 16], start=k == 0, stop=k == KC - 1)
            ins.then_inc(c_pe, 1)
            pe.wait_ge(c_dve, 1)
            for k in range(KC):
                ins = nc.tensor.transpose(bank[1][:, k * 64:(k + 1) * 64], vo[:, k * P:(k + 1) * P], ident[0:64, 0:64])
            ins.then_inc(c_pe, 1)
            pe.wait_ge(c_dve, 2)
            for k in range(KC):
                ins = nc.tensor.matmul(bank[2][0:64, 0:D], vot[:, k], d_wo[:, k], start=k == 0, stop=k == KC - 1)
            ins.then_inc(c_pe, 1)
            pe.wait_ge(c_dve, 4)
            for k in range(KC):
                nc.tensor.transpose(bank[3][:, k * 64:(k + 1) * 64], os_[:, k * P:(k + 1) * P], ident[0:64, 0:64])
            hs_v = hs.rearrange("p (n k) -> p k n", k=KC)
            for k in range(KC):
                ins = nc.tensor.transpose(bank[3][:, 128 + k * 64:128 + (k + 1) * 64], hs_v[:, k], ident[0:64, 0:64])
            ins.then_inc(c_pe, 1)

            def experts(g):
                pe.wait_ge(hcur_made, g + 1)
                for k in range(PIECES):
                    if k == 4:
                        for w, out_s, src in ((0, u_out, u_sb), (1, g_out, g_sb)):
                            pe.wait_ge(out_s, g + 1)
                            view = src.rearrange("p (n c) -> p c n", c=FC)
                            for c in range(FC):
                                ins = nc.tensor.transpose(bank[4 + 2 * w + c // 4][:, (c % 4) * P:(c % 4 + 1) * P], view[:, c], ident[:])
                            ins.then_inc(ut_done, 1)
                        pe.wait_ge(at_made, g + 1)
                    n = PIECES * g + k
                    weights = place[n % len(place)]
                    pe.wait_ge(piece_in[n % len(place)], 16 * (n // len(place) + 1))
                    if k < 4:
                        for half in range(2):
                            for j in range(GROUP):
                                ins = nc.tensor.matmul(bank[2 * (k // 2) + half][32 * j:32 * j + 32, :], hcur[:, part(k), j],
                                                       weights[:, j, half * 512:(half + 1) * 512],
                                                       start=k % 2 == 0, stop=k % 2 == 1, tile_position=(0, 32 * j))
                    else:
                        for c in range(4):
                            for j in range(GROUP):
                                cc = part(k) * 4 + c
                                ins = nc.tensor.matmul(bank[0][32 * j:32 * j + 32, 0:D], at[:, cc, j],
                                                       weights[:, j, c * D:(c + 1) * D],
                                                       start=k == 4 and c == 0, stop=k == 5 and c == 3, tile_position=(0, 32 * j))
                    ins.then_inc(piece_used, 1)
                pe.wait_ge(y_out, g + 1)
                for k in range(KC):
                    ins = nc.tensor.transpose(bank[6][:, k * P:(k + 1) * P], ysb[:, k * P:(k + 1) * P], ident[:])
                ins.then_inc(yt_done, 1)

            for g in range(NS // GROUP):
                experts(g)

            pe.wait_ge(slots_made, NS // GROUP)
            for w, weight in ((0, c_wk), (1, c_wv)):
                for m in range(HM):
                    for k in range(KC):
                        ins = nc.tensor.matmul(bank[2 + w][:, m * 64:(m + 1) * 64], weight[:, k, m * P:(m + 1) * P],
                                               o2t[:, k].rearrange("p b e -> p (b e)"), start=k == 0, stop=k == KC - 1)
            ins.then_inc(kv_done, 1)
            def values_out(m):
                pe.wait_ge(kv_made, 2 * HM)
                for b in range(B):
                    i = m * B + b
                    ins = nc.tensor.matmul(bank[4 + i // 2][:, (i % 2) * D:(i % 2 + 1) * D], vb[:, m, b], c_wo[:, m],
                                           start=True, stop=True)
                ins.then_inc(vp_done, 1)

            def f_scores(p):
                if p.i % 2 == 0:
                    pe.wait_ge(qh_back[p.half], (p.b + 1) * 16)
                if p.after(2):
                    pe.wait_ge(f_cen, p.n - 1)
                for j in range(2):
                    tile = 2 * (p.i % 2) + j
                    for m in range(HM):
                        ins = nc.tensor.matmul(bank[p.i % 2][:, j * HQ + m * P:j * HQ + (m + 1) * P],
                                               qh_in[:, p.half, m, tile * P:(tile + 1) * P],
                                               kb[:, m, p.b], start=True, stop=True)
                ins.then_inc(f_s_done, 1)

            def f_transpose(p):
                pe.wait_ge(f_norm, p.n + 1)
                if p.after(2):
                    pe.wait_ge(f_pt, p.n - 1)
                for j in range(4):
                    ins = nc.tensor.transpose(bank[2 + p.i % 2][:, j * P:(j + 1) * P], prob[p.i][:, j * P:(j + 1) * P], ident[:])
                ins.then_inc(f_t_done, 1)

            def f_values(p):
                pe.wait_ge(f_pt, p.n + 1)
                if p.after(4):
                    pe.wait_ge(f_norm2, p.n - 3)
                elif p.n == 0:
                    pe.wait_ge(vp_made, 1)
                for j in range(2):
                    for m in range(HM):
                        nc.tensor.matmul(bank[4 + p.i][:, j * D:(j + 1) * D],
                                         ptl[p.i % 2][:, (2 * j + m) * P:(2 * j + m + 1) * P],
                                         vp[:, m, p.b], start=m == 0, stop=False)
                    ins = nc.tensor.matmul(bank[4 + p.i][:, j * D:(j + 1) * D], ones_parts[:], cbo_parts[:],
                                           start=False, stop=True)
                ins.then_inc(f_y_done, 1)

            def f_turn(b):
                for i in range(PAIRS):
                    here, turned, valued = Pair(b, i), Pair(b, i, 2), Pair(b, i, 3)
                    if here.there:
                        f_scores(here)
                    if isinstance(b, int) and b == 0 and i in (1, 2):
                        values_out(i - 1)
                    if turned.there:
                        f_transpose(turned)
                    if valued.there:
                        f_values(valued)

            pe.wait_ge(kv_made, HM)
            f_turn(0)
            f_turn(1)
            with pe.Fori(2, B) as b:
                f_turn(b)
            f_turn(B)


def kernel(**inputs):
    import numpy as np
    import concourse.bacc as bacc
    from concourse.bass_utils import run_bass_kernel_spmd

    nc = bacc.Bacc("TRN2", target_bir_lowering=False, num_devices=1)
    arrays, aps = {}, {}
    for name, value in inputs.items():
        value = np.ascontiguousarray(value)
        arrays[name] = value
        aps[name] = nc.dram_tensor(name, value.shape, mybir.dt.from_np(value.dtype), kind="ExternalInput").ap()
    result = nc.dram_tensor("result", (B, S, D), F32, kind="ExternalOutput").ap()
    build(nc, aps, result)
    r = run_bass_kernel_spmd(nc, [arrays], core_ids=[0])
    return r.results[0]["result"]
```
